# Optimizing a Trainium2 kernel written in Bass

```python
import numpy as np
import jax
import jax.numpy as jnp

def _softmax(x, axis=-1):
    return jax.nn.softmax(x, axis=axis)

def _gelu(x):
    return jax.nn.gelu(x, approximate=True)

def _silu(x):
    return jax.nn.silu(x)

def _sigmoid(x):
    return jax.nn.sigmoid(x)

def _layernorm(x, axis=-1, eps=1e-05):
    m = jnp.mean(x, axis=axis, keepdims=True)
    v = jnp.var(x, axis=axis, keepdims=True)
    return (x - m) / jnp.sqrt(v + eps)

def _scatter_add(tgt, idx, src, axis=0):
    return tgt.at[idx].add(src)

def _segment_sum(src, seg, n):
    return jax.ops.segment_sum(src, seg, n)
kernel_name = 'mk_perceiver_d2_seqx_r4_557fef'

def setup_inputs(seed: int=0):
    np.random.seed(seed)
    _w = jnp.asarray

    def _rec_inputs():
        import jax
        import jax.numpy as jnp
        _rk = jax.random.key(seed)
        x = 7.22e-05 + 1 * jax.random.normal(jax.random.fold_in(_rk, 1), (16, 64, 256), jnp.float32)
        _lenS = 64 - jax.random.randint(jax.random.fold_in(_rk, 7), (16,), 0, max(1, 64 // 4) + 1, jnp.int32)
        _lenS2 = 1601 - jax.random.randint(jax.random.fold_in(_rk, 8), (16,), 0, max(1, 1601 // 4) + 1, jnp.int32)
        _ctx_1024P = jax.random.normal(jax.random.fold_in(_rk, 11), (16, 16, 256), jnp.float32)
        _ctx_1024c = jax.random.dirichlet(jax.random.fold_in(_rk, 511), 0.3 * jnp.ones((16,), jnp.float32), (16, 1601))
        _ctx_1024t = jnp.einsum('bsk,bkd->bsd', _ctx_1024c, _ctx_1024P)
        _ctx_1024t = _ctx_1024t * jax.lax.rsqrt(jnp.mean(jnp.square(_ctx_1024t)) + 1e-12) * 0.953939
        ctx_1024 = 2.81802e-05 + 1.00001 * (_ctx_1024t + 0.3 * jax.random.normal(jax.random.fold_in(_rk, 611), (16, 1601, 256), jnp.float32))
        return (x, ctx_1024)
    x, ctx_1024 = _rec_inputs()

    def _L0_xattn_setup():
        import jax, jax.numpy as jnp
        import numpy as np
        B, T, S, D = (4, 512, 1024, 256)
        TOP_K = 32

        def _read(query, mem_state, top_k, Wq, bq, Wk, bk, Wv, bv, Wo, bo):
            b, t, d = query.shape
            s = mem_state.shape[1]
            scale = 1.0 / np.sqrt(d)
            q = query @ Wq.T + bq
            k = mem_state @ Wk.T + bk
            v = mem_state @ Wv.T + bv
            scores = jnp.einsum('btd,bsd->bts', q, k) * scale
            if top_k < s:
                vals, idx = jax.lax.top_k(scores, top_k)
                b_ix = jnp.arange(b)[:, None, None]
                t_ix = jnp.arange(t)[None, :, None]
                masked = jnp.full_like(scores, -jnp.inf)
                scores = masked.at[b_ix, t_ix, idx].set(vals)
            attn = jax.nn.softmax(scores, axis=-1)
            ctx = jnp.einsum('bts,bsd->btd', attn, v)
            return ctx @ Wo.T + bo
        key = jax.random.key(seed)
        ks = jax.random.split(key, 12)
        std = 0.02
        inp = {'query': jax.random.normal(ks[0], (B, T, D), dtype=jnp.float32), 'mem_state': jax.random.normal(ks[1], (B, S, D), dtype=jnp.float32), 'top_k': TOP_K, 'Wq': jax.random.normal(ks[2], (D, D), dtype=jnp.float32) * std, 'bq': jnp.zeros((D,), dtype=jnp.float32), 'Wk': jax.random.normal(ks[3], (D, D), dtype=jnp.float32) * std, 'bk': jnp.zeros((D,), dtype=jnp.float32), 'Wv': jax.random.normal(ks[4], (D, D), dtype=jnp.float32) * std, 'bv': jnp.zeros((D,), dtype=jnp.float32), 'Wo': jax.random.normal(ks[5], (D, D), dtype=jnp.float32) * std, 'bo': jnp.zeros((D,), dtype=jnp.float32)}
        return inp
    _L0_xattn_all = _L0_xattn_setup()
    _L0_xattn_in = {k: v for k, v in _L0_xattn_all.items() if k in ('Wq', 'bq', 'Wk', 'bk', 'Wv', 'bv', 'Wo', 'bo')}
    del _L0_xattn_all

    def _L0_attn_setup():
        import jax, jax.numpy as jnp
        import numpy as np
        GAMMA = 0.96875
        H = 256
        B = 4
        L = 512
        key = jax.random.key(seed)
        k0, k1, k2, k3, k4 = jax.random.split(key, 5)
        x = jax.random.normal(k0, (B, L, H), dtype=jnp.float32)
        weight_q = jax.random.normal(k1, (H, H), dtype=jnp.float32) / H
        weight_k = jax.random.normal(k2, (H, H), dtype=jnp.float32) / H
        weight_v = jax.random.normal(k3, (H, H), dtype=jnp.float32) / H
        theta = jax.random.normal(k4, (H,), dtype=jnp.float32) / H
        return {'x': x, 'weight_q': weight_q, 'weight_k': weight_k, 'weight_v': weight_v, 'theta': theta}
    _L0_attn_all = _L0_attn_setup()
    _L0_attn_in = {k: v for k, v in _L0_attn_all.items() if k in ('weight_q', 'weight_k', 'weight_v', 'theta')}
    del _L0_attn_all

    def _L0_ffn_setup():
        import jax, jax.numpy as jnp
        import numpy as np
        D = 256
        H = 4
        HD = D // H
        E = 8
        FF = 1024
        CAP_FACTOR = 1.0

        def _ln(x, g, b, eps=1e-05):
            mu = jnp.mean(x, -1, keepdims=True)
            v = jnp.mean((x - mu) ** 2, -1, keepdims=True)
            return (x - mu) * jax.lax.rsqrt(v + eps) * g + b

        def _mha(x, w, b, ow, ob):
            L, N, _ = x.shape
            qkv = x @ w.T + b
            q, k, v = jnp.split(qkv, 3, axis=-1)
            rh = lambda t: t.reshape(L, N, H, HD).transpose(1, 2, 0, 3)
            q, k, v = (rh(q), rh(k), rh(v))
            scores = jnp.einsum('nhld,nhmd->nhlm', q, k) / np.float32(np.sqrt(HD))
            attn = jax.nn.softmax(scores, axis=-1)
            o = jnp.einsum('nhlm,nhmd->nhld', attn, v).transpose(2, 0, 1, 3).reshape(L, N, D)
            return o @ ow.T + ob

        def _moe(x, wg, w1, b1, w2, b2):
            L, N, _ = x.shape
            S = L * N
            cap = int(CAP_FACTOR * S) // E
            xf = x.reshape(S, D)
            gates = jax.nn.softmax(xf @ wg, axis=-1)
            idx = jnp.argmax(gates, axis=-1)
            mask1 = jax.nn.one_hot(idx, E, dtype=x.dtype)
            loc = jnp.sum((jnp.cumsum(mask1, 0) - 1.0) * mask1, -1).astype(jnp.int32)
            keep = loc < cap
            gate_val = jnp.take_along_axis(gates, idx[:, None], -1)[:, 0]
            slot = jnp.where(keep, idx.astype(jnp.int32) * cap + loc, E * cap)
            disp = jnp.zeros((E * cap, D), x.dtype).at[slot].set(xf, mode='drop')
            disp = disp.reshape(E, cap, D)
            h = jnp.einsum('ecd,edf->ecf', disp, w1) + b1[:, None, :]
            y = (jnp.einsum('ecf,efd->ecd', h, w2) + b2[:, None, :]).reshape(E * cap, D)
            out = jnp.where(keep[:, None], gate_val[:, None] * y[jnp.minimum(slot, E * cap - 1)], 0.0)
            return out.reshape(L, N, D)
        key = jax.random.key(seed)
        ks = jax.random.split(key, 8)
        L, N = (256, 16)
        s = 0.02
        return {'x': jax.random.normal(ks[0], (L, N, D), jnp.float32), 'in_proj_w': jax.random.normal(ks[1], (3 * D, D), jnp.float32) * s, 'in_proj_b': jnp.zeros((3 * D,), jnp.float32), 'out_proj_w': jax.random.normal(ks[2], (D, D), jnp.float32) * s, 'out_proj_b': jnp.zeros((D,), jnp.float32), 'ln1_g': jnp.ones((D,), jnp.float32), 'ln1_b': jnp.zeros((D,), jnp.float32), 'ln2_g': jnp.ones((D,), jnp.float32), 'ln2_b': jnp.zeros((D,), jnp.float32), 'wg': jax.random.normal(ks[3], (D, E), jnp.float32) * s, 'w1': jax.random.normal(ks[4], (E, D, FF), jnp.float32) * s, 'b1': jnp.zeros((E, FF), jnp.float32), 'w2': jax.random.normal(ks[5], (E, FF, D), jnp.float32) * s, 'b2': jnp.zeros((E, D), jnp.float32)}
    _L0_ffn_all = _L0_ffn_setup()
    _L0_ffn_in = {k: v for k, v in _L0_ffn_all.items() if k in ('in_proj_w', 'in_proj_b', 'out_proj_w', 'out_proj_b', 'ln1_g', 'ln1_b', 'ln2_g', 'ln2_b', 'wg', 'w1', 'b1', 'w2', 'b2')}
    del _L0_ffn_all

    def _L1_xattn_setup():
        import jax, jax.numpy as jnp
        import numpy as np
        B, L, D_MODEL, H = (4, 512, 256, 16)
        E = D_MODEL // H
        EPS = 1e-05

        def layernorm(x, w, b):
            mu = jnp.mean(x, axis=-1, keepdims=True)
            var = jnp.mean((x - mu) ** 2, axis=-1, keepdims=True)
            return (x - mu) * jax.lax.rsqrt(var + EPS) * w + b
        key = jax.random.key(seed)
        ks = jax.random.split(key, 12)
        s_in = 1.0 / np.sqrt(D_MODEL)
        inp = {'q': jax.random.normal(ks[0], (B, L, D_MODEL), jnp.float32), 'k': jax.random.normal(ks[1], (B, L, D_MODEL), jnp.float32), 'v': jax.random.normal(ks[2], (B, L, D_MODEL), jnp.float32), 'norm_w': jnp.ones((D_MODEL,), jnp.float32), 'norm_b': jnp.zeros((D_MODEL,), jnp.float32), 'norm1_w': jnp.ones((D_MODEL,), jnp.float32), 'norm1_b': jnp.zeros((D_MODEL,), jnp.float32), 'Wq': jax.random.uniform(ks[3], (D_MODEL, H * E), jnp.float32, -s_in, s_in), 'bq': jnp.zeros((H * E,), jnp.float32), 'Wk': jax.random.uniform(ks[4], (D_MODEL, H * E), jnp.float32, -s_in, s_in), 'bk': jnp.zeros((H * E,), jnp.float32), 'Wv': jax.random.uniform(ks[5], (D_MODEL, H * E), jnp.float32, -s_in, s_in), 'bv': jnp.zeros((H * E,), jnp.float32), 'Wo': jax.random.uniform(ks[6], (H * E, D_MODEL), jnp.float32, -s_in, s_in), 'bo': jnp.zeros((D_MODEL,), jnp.float32)}
        return inp
    _L1_xattn_all = _L1_xattn_setup()
    _L1_xattn_in = {k: v for k, v in _L1_xattn_all.items() if k in ('norm_w', 'norm_b', 'norm1_w', 'norm1_b', 'Wq', 'bq', 'Wk', 'bk', 'Wv', 'bv', 'Wo', 'bo')}
    del _L1_xattn_all

    def _L1_attn_setup():
        import jax, jax.numpy as jnp
        import numpy as np
        import math
        NUM_RFS = 256
        DIM = 256
        OUT_DIM = 256
        B, S = (4, 512)

        def _rfs(xw, ab, AB, gs):
            dot_products = jnp.einsum('...d,rd->...r', xw, ab[:, None] * gs)
            correction = (0.5 * jnp.sum(xw * xw, axis=-1))[..., None] * (ab * ab)
            return 1.0 / math.sqrt(NUM_RFS) * AB * jnp.exp(dot_products - correction)
        key = jax.random.key(seed)
        k1, k2, k3, k4 = jax.random.split(key, 4)
        x = jax.random.normal(k1, (B, S, DIM), dtype=jnp.float32) * 0.03
        input_weights = jax.random.normal(k2, (OUT_DIM, DIM), dtype=jnp.float32) * 0.03
        xis = jax.random.uniform(k3, (NUM_RFS,), dtype=jnp.float32) * 0.5
        proj_matrix = jax.random.normal(k4, (NUM_RFS, DIM), dtype=jnp.float32)
        return {'x': x, 'input_weights': input_weights, 'xis': xis, 'proj_matrix': proj_matrix}
    _L1_attn_all = _L1_attn_setup()
    _L1_attn_in = {k: v for k, v in _L1_attn_all.items() if k in ('input_weights', 'xis', 'proj_matrix')}
    del _L1_attn_all

    def _L1_ffn_setup():
        import jax, jax.numpy as jnp
        import numpy as np
        LATENT = 256
        LEAF_W = 64
        DEPTH = 4
        N_LEAVES = 2 ** DEPTH
        N_NODES = 2 ** DEPTH - 1
        B, S = (4, 512)

        def _fff_params(key, prefix):
            ks = jax.random.split(key, 4)
            d, h, l, n = (LATENT, LEAF_W, N_LEAVES, N_NODES)
            s_in = 1.0 / np.sqrt(d).astype(np.float32)
            s_h = 1.0 / np.sqrt(h).astype(np.float32)
            return {f'{prefix}_node_w': jax.random.normal(ks[0], (n, d), jnp.float32) * s_in, f'{prefix}_node_b': jax.random.normal(ks[1], (n,), jnp.float32) * s_in, f'{prefix}_w1': jax.random.normal(ks[2], (l, d, h), jnp.float32) * s_in, f'{prefix}_b1': jnp.zeros((l, h), jnp.float32), f'{prefix}_w2': jax.random.normal(ks[3], (l, h, d), jnp.float32) * s_h, f'{prefix}_b2': jnp.zeros((l, d), jnp.float32)}

        def _fff(x, node_w, node_b, w1, b1, w2, b2):
            Bx, Sx, D = x.shape
            xf = x.reshape(-1, D)
            N = xf.shape[0]
            cur = jnp.zeros((N,), jnp.int32)
            for _ in range(DEPTH):
                pw = node_w[cur]
                score = jnp.einsum('nd,nd->n', xf, pw) + node_b[cur]
                cur = 2 * cur + 1 + (score >= 0).astype(jnp.int32)
            leaf = cur - N_NODES
            sel = jax.nn.one_hot(leaf, N_LEAVES, dtype=xf.dtype)
            hidden_all = jax.nn.relu(jnp.einsum('nd,ldh->lnh', xf, w1) + b1[:, None, :])
            hidden = hidden_all * sel.T[:, :, None]
            out = jnp.einsum('lnh,lho->no', hidden, w2) + sel @ b2
            return out.reshape(Bx, Sx, D)
        key = jax.random.key(seed)
        kx, kq, kk, kv = jax.random.split(key, 4)
        inp = {'x': jax.random.normal(kx, (B, S, LATENT), jnp.float32)}
        inp.update(_fff_params(kq, 'q'))
        inp.update(_fff_params(kk, 'k'))
        inp.update(_fff_params(kv, 'v'))
        return inp
    _L1_ffn_all = _L1_ffn_setup()
    _L1_ffn_in = {k: v for k, v in _L1_ffn_all.items() if k in ('q_node_w', 'q_node_b', 'q_w1', 'q_b1', 'q_w2', 'q_b2', 'k_node_w', 'k_node_b', 'k_w1', 'k_b1', 'k_w2', 'k_b2', 'v_node_w', 'v_node_b', 'v_w1', 'v_b1', 'v_w2', 'v_b2')}
    del _L1_ffn_all
    return {'x': x, 'ctx_1024': ctx_1024, 'L0_xattn_Wq': _L0_xattn_in['Wq'], 'L0_xattn_bq': _L0_xattn_in['bq'], 'L0_xattn_Wk': _L0_xattn_in['Wk'], 'L0_xattn_bk': _L0_xattn_in['bk'], 'L0_xattn_Wv': _L0_xattn_in['Wv'], 'L0_xattn_bv': _L0_xattn_in['bv'], 'L0_xattn_Wo': _L0_xattn_in['Wo'], 'L0_xattn_bo': _L0_xattn_in['bo'], 'L0_attn_weight_q': _L0_attn_in['weight_q'], 'L0_attn_weight_k': _L0_attn_in['weight_k'], 'L0_attn_weight_v': _L0_attn_in['weight_v'], 'L0_attn_theta': _L0_attn_in['theta'], 'L0_ffn_in_proj_w': _L0_ffn_in['in_proj_w'], 'L0_ffn_in_proj_b': _L0_ffn_in['in_proj_b'], 'L0_ffn_out_proj_w': _L0_ffn_in['out_proj_w'], 'L0_ffn_out_proj_b': _L0_ffn_in['out_proj_b'], 'L0_ffn_ln1_g': _L0_ffn_in['ln1_g'], 'L0_ffn_ln1_b': _L0_ffn_in['ln1_b'], 'L0_ffn_ln2_g': _L0_ffn_in['ln2_g'], 'L0_ffn_ln2_b': _L0_ffn_in['ln2_b'], 'L0_ffn_wg': _L0_ffn_in['wg'], 'L0_ffn_w1': _L0_ffn_in['w1'], 'L0_ffn_b1': _L0_ffn_in['b1'], 'L0_ffn_w2': _L0_ffn_in['w2'], 'L0_ffn_b2': _L0_ffn_in['b2'], 'L1_xattn_norm_w': _L1_xattn_in['norm_w'], 'L1_xattn_norm_b': _L1_xattn_in['norm_b'], 'L1_xattn_norm1_w': _L1_xattn_in['norm1_w'], 'L1_xattn_norm1_b': _L1_xattn_in['norm1_b'], 'L1_xattn_Wq': _L1_xattn_in['Wq'], 'L1_xattn_bq': _L1_xattn_in['bq'], 'L1_xattn_Wk': _L1_xattn_in['Wk'], 'L1_xattn_bk': _L1_xattn_in['bk'], 'L1_xattn_Wv': _L1_xattn_in['Wv'], 'L1_xattn_bv': _L1_xattn_in['bv'], 'L1_xattn_Wo': _L1_xattn_in['Wo'], 'L1_xattn_bo': _L1_xattn_in['bo'], 'L1_attn_input_weights': _L1_attn_in['input_weights'], 'L1_attn_xis': _L1_attn_in['xis'], 'L1_attn_proj_matrix': _L1_attn_in['proj_matrix'], 'L1_ffn_q_node_w': _L1_ffn_in['q_node_w'], 'L1_ffn_q_node_b': _L1_ffn_in['q_node_b'], 'L1_ffn_q_w1': _L1_ffn_in['q_w1'], 'L1_ffn_q_b1': _L1_ffn_in['q_b1'], 'L1_ffn_q_w2': _L1_ffn_in['q_w2'], 'L1_ffn_q_b2': _L1_ffn_in['q_b2'], 'L1_ffn_k_node_w': _L1_ffn_in['k_node_w'], 'L1_ffn_k_node_b': _L1_ffn_in['k_node_b'], 'L1_ffn_k_w1': _L1_ffn_in['k_w1'], 'L1_ffn_k_b1': _L1_ffn_in['k_b1'], 'L1_ffn_k_w2': _L1_ffn_in['k_w2'], 'L1_ffn_k_b2': _L1_ffn_in['k_b2'], 'L1_ffn_v_node_w': _L1_ffn_in['v_node_w'], 'L1_ffn_v_node_b': _L1_ffn_in['v_node_b'], 'L1_ffn_v_w1': _L1_ffn_in['v_w1'], 'L1_ffn_v_b1': _L1_ffn_in['v_b1'], 'L1_ffn_v_w2': _L1_ffn_in['v_w2'], 'L1_ffn_v_b2': _L1_ffn_in['v_b2']}

def reference(x, ctx_1024, L0_xattn_Wq, L0_xattn_bq, L0_xattn_Wk, L0_xattn_bk, L0_xattn_Wv, L0_xattn_bv, L0_xattn_Wo, L0_xattn_bo, L0_attn_weight_q, L0_attn_weight_k, L0_attn_weight_v, L0_attn_theta, L0_ffn_in_proj_w, L0_ffn_in_proj_b, L0_ffn_out_proj_w, L0_ffn_out_proj_b, L0_ffn_ln1_g, L0_ffn_ln1_b, L0_ffn_ln2_g, L0_ffn_ln2_b, L0_ffn_wg, L0_ffn_w1, L0_ffn_b1, L0_ffn_w2, L0_ffn_b2, L1_xattn_norm_w, L1_xattn_norm_b, L1_xattn_norm1_w, L1_xattn_norm1_b, L1_xattn_Wq, L1_xattn_bq, L1_xattn_Wk, L1_xattn_bk, L1_xattn_Wv, L1_xattn_bv, L1_xattn_Wo, L1_xattn_bo, L1_attn_input_weights, L1_attn_xis, L1_attn_proj_matrix, L1_ffn_q_node_w, L1_ffn_q_node_b, L1_ffn_q_w1, L1_ffn_q_b1, L1_ffn_q_w2, L1_ffn_q_b2, L1_ffn_k_node_w, L1_ffn_k_node_b, L1_ffn_k_w1, L1_ffn_k_b1, L1_ffn_k_w2, L1_ffn_k_b2, L1_ffn_v_node_w, L1_ffn_v_node_b, L1_ffn_v_w1, L1_ffn_v_b1, L1_ffn_v_w2, L1_ffn_v_b2):
    import jax
    import jax.numpy as jnp

    def _L0_xattn_ref(query, mem_state, top_k, Wq, bq, Wk, bk, Wv, bv, Wo, bo):
        import jax, jax.numpy as jnp
        import numpy as np
        B, T, S, D = (4, 512, 1024, 256)
        TOP_K = 32

        def _read(query, mem_state, top_k, Wq, bq, Wk, bk, Wv, bv, Wo, bo):
            b, t, d = query.shape
            s = mem_state.shape[1]
            scale = 1.0 / np.sqrt(d)
            q = query @ Wq.T + bq
            k = mem_state @ Wk.T + bk
            v = mem_state @ Wv.T + bv
            scores = jnp.einsum('btd,bsd->bts', q, k) * scale
            if top_k < s:
                vals, idx = jax.lax.top_k(scores, top_k)
                b_ix = jnp.arange(b)[:, None, None]
                t_ix = jnp.arange(t)[None, :, None]
                masked = jnp.full_like(scores, -jnp.inf)
                scores = masked.at[b_ix, t_ix, idx].set(vals)
            attn = jax.nn.softmax(scores, axis=-1)
            ctx = jnp.einsum('bts,bsd->btd', attn, v)
            return ctx @ Wo.T + bo
        return _read(query, mem_state, top_k, Wq, bq, Wk, bk, Wv, bv, Wo, bo)

    def _L0_attn_ref(x, weight_q, weight_k, weight_v, theta):
        import jax, jax.numpy as jnp
        import numpy as np
        GAMMA = 0.96875
        H = 256
        B = 4
        L = 512
        Bb, Ll, Hh = x.shape
        dt = x.dtype
        seq = jnp.arange(1, Ll + 1, dtype=dt)
        zero = jnp.asarray(0.0, dtype=dt)
        thetas = jnp.exp(zero * seq[:, None] * theta[None, :])
        theta_conj = thetas
        q = jnp.matmul(x, weight_q) * thetas[None]
        k = jnp.matmul(x, weight_k) * theta_conj[None]
        v = jnp.matmul(x, weight_v)
        n = jnp.arange(Ll)
        diff = n[:, None] - n[None, :]
        D = jnp.where(diff >= 0, jnp.asarray(GAMMA, dt) ** diff.astype(dt), jnp.zeros((), dt))
        scores = jnp.einsum('bid,bjd->bij', q, k) * D[None]
        return jnp.einsum('bij,bjd->bid', scores, v)

    def _L0_ffn_ref(x, in_proj_w, in_proj_b, out_proj_w, out_proj_b, ln1_g, ln1_b, ln2_g, ln2_b, wg, w1, b1, w2, b2):
        import jax, jax.numpy as jnp
        import numpy as np
        D = 256
        H = 4
        HD = D // H
        E = 8
        FF = 1024
        CAP_FACTOR = 1.0

        def _ln(x, g, b, eps=1e-05):
            mu = jnp.mean(x, -1, keepdims=True)
            v = jnp.mean((x - mu) ** 2, -1, keepdims=True)
            return (x - mu) * jax.lax.rsqrt(v + eps) * g + b

        def _mha(x, w, b, ow, ob):
            L, N, _ = x.shape
            qkv = x @ w.T + b
            q, k, v = jnp.split(qkv, 3, axis=-1)
            rh = lambda t: t.reshape(L, N, H, HD).transpose(1, 2, 0, 3)
            q, k, v = (rh(q), rh(k), rh(v))
            scores = jnp.einsum('nhld,nhmd->nhlm', q, k) / np.float32(np.sqrt(HD))
            attn = jax.nn.softmax(scores, axis=-1)
            o = jnp.einsum('nhlm,nhmd->nhld', attn, v).transpose(2, 0, 1, 3).reshape(L, N, D)
            return o @ ow.T + ob

        def _moe(x, wg, w1, b1, w2, b2):
            L, N, _ = x.shape
            S = L * N
            cap = int(CAP_FACTOR * S) // E
            xf = x.reshape(S, D)
            gates = jax.nn.softmax(xf @ wg, axis=-1)
            idx = jnp.argmax(gates, axis=-1)
            mask1 = jax.nn.one_hot(idx, E, dtype=x.dtype)
            loc = jnp.sum((jnp.cumsum(mask1, 0) - 1.0) * mask1, -1).astype(jnp.int32)
            keep = loc < cap
            gate_val = jnp.take_along_axis(gates, idx[:, None], -1)[:, 0]
            slot = jnp.where(keep, idx.astype(jnp.int32) * cap + loc, E * cap)
            disp = jnp.zeros((E * cap, D), x.dtype).at[slot].set(xf, mode='drop')
            disp = disp.reshape(E, cap, D)
            h = jnp.einsum('ecd,edf->ecf', disp, w1) + b1[:, None, :]
            y = (jnp.einsum('ecf,efd->ecd', h, w2) + b2[:, None, :]).reshape(E * cap, D)
            out = jnp.where(keep[:, None], gate_val[:, None] * y[jnp.minimum(slot, E * cap - 1)], 0.0)
            return out.reshape(L, N, D)
        y1 = _ln(x + _mha(x, in_proj_w, in_proj_b, out_proj_w, out_proj_b), ln1_g, ln1_b)
        y2 = _ln(y1 + _moe(y1, wg, w1, b1, w2, b2), ln2_g, ln2_b)
        return y2

    def _L1_xattn_ref(q, k, v, norm_w, norm_b, norm1_w, norm1_b, Wq, bq, Wk, bk, Wv, bv, Wo, bo):
        import jax, jax.numpy as jnp
        import numpy as np
        B, L, D_MODEL, H = (4, 512, 256, 16)
        E = D_MODEL // H
        EPS = 1e-05

        def layernorm(x, w, b):
            mu = jnp.mean(x, axis=-1, keepdims=True)
            var = jnp.mean((x - mu) ** 2, axis=-1, keepdims=True)
            return (x - mu) * jax.lax.rsqrt(var + EPS) * w + b
        b, l, _ = q.shape
        s = k.shape[1]
        qn = layernorm(q, norm_w, norm_b)
        kn = layernorm(k, norm_w, norm_b)
        vn = layernorm(v, norm_w, norm_b)
        Q = (qn @ Wq + bq).reshape(b, l, H, E)
        K = (kn @ Wk + bk).reshape(b, s, H, E)
        V = (vn @ Wv + bv).reshape(b, s, H, E)
        scale = 1.0 / jnp.sqrt(jnp.asarray(E, Q.dtype))
        scores = jnp.einsum('blhe,bshe->bhls', Q, K)
        A = jax.nn.softmax(scale * scores, axis=-1)
        O = jnp.einsum('bhls,bshd->blhd', A, V)
        O = O + Q
        out = jnp.transpose(O, (0, 2, 1, 3)).reshape(b, l, H * E)
        return layernorm(out, norm1_w, norm1_b) @ Wo + bo + out

    def _L1_attn_ref(x, input_weights, xis, proj_matrix):
        import jax, jax.numpy as jnp
        import numpy as np
        import math
        NUM_RFS = 256
        DIM = 256
        OUT_DIM = 256
        B, S = (4, 512)

        def _rfs(xw, ab, AB, gs):
            dot_products = jnp.einsum('...d,rd->...r', xw, ab[:, None] * gs)
            correction = (0.5 * jnp.sum(xw * xw, axis=-1))[..., None] * (ab * ab)
            return 1.0 / math.sqrt(NUM_RFS) * AB * jnp.exp(dot_products - correction)
        ab = xis
        AB = jnp.exp(xis)
        weights = _rfs(input_weights, ab, AB, proj_matrix)
        feats = _rfs(x, ab, AB, proj_matrix)
        return jnp.einsum('bsr,or->bso', feats, weights)

    def _L1_ffn_ref(x, q_node_w, q_node_b, q_w1, q_b1, q_w2, q_b2, k_node_w, k_node_b, k_w1, k_b1, k_w2, k_b2, v_node_w, v_node_b, v_w1, v_b1, v_w2, v_b2):
        import jax, jax.numpy as jnp
        import numpy as np
        LATENT = 256
        LEAF_W = 64
        DEPTH = 4
        N_LEAVES = 2 ** DEPTH
        N_NODES = 2 ** DEPTH - 1
        B, S = (4, 512)

        def _fff_params(key, prefix):
            ks = jax.random.split(key, 4)
            d, h, l, n = (LATENT, LEAF_W, N_LEAVES, N_NODES)
            s_in = 1.0 / np.sqrt(d).astype(np.float32)
            s_h = 1.0 / np.sqrt(h).astype(np.float32)
            return {f'{prefix}_node_w': jax.random.normal(ks[0], (n, d), jnp.float32) * s_in, f'{prefix}_node_b': jax.random.normal(ks[1], (n,), jnp.float32) * s_in, f'{prefix}_w1': jax.random.normal(ks[2], (l, d, h), jnp.float32) * s_in, f'{prefix}_b1': jnp.zeros((l, h), jnp.float32), f'{prefix}_w2': jax.random.normal(ks[3], (l, h, d), jnp.float32) * s_h, f'{prefix}_b2': jnp.zeros((l, d), jnp.float32)}

        def _fff(x, node_w, node_b, w1, b1, w2, b2):
            Bx, Sx, D = x.shape
            xf = x.reshape(-1, D)
            N = xf.shape[0]
            cur = jnp.zeros((N,), jnp.int32)
            for _ in range(DEPTH):
                pw = node_w[cur]
                score = jnp.einsum('nd,nd->n', xf, pw) + node_b[cur]
                cur = 2 * cur + 1 + (score >= 0).astype(jnp.int32)
            leaf = cur - N_NODES
            sel = jax.nn.one_hot(leaf, N_LEAVES, dtype=xf.dtype)
            hidden_all = jax.nn.relu(jnp.einsum('nd,ldh->lnh', xf, w1) + b1[:, None, :])
            hidden = hidden_all * sel.T[:, :, None]
            out = jnp.einsum('lnh,lho->no', hidden, w2) + sel @ b2
            return out.reshape(Bx, Sx, D)
        q = _fff(x, q_node_w, q_node_b, q_w1, q_b1, q_w2, q_b2)
        k = _fff(x, k_node_w, k_node_b, k_w1, k_b1, k_w2, k_b2)
        v = _fff(x, v_node_w, v_node_b, v_w1, v_b1, v_w2, v_b2)
        scale = 1.0 / np.sqrt(LATENT).astype(np.float32)
        attn = jax.nn.softmax(jnp.einsum('bqd,bkd->bqk', q, k) * scale, axis=-1)
        return jnp.einsum('bqk,bkd->bqd', attn, v)
    x = x + _L0_xattn_ref(_layernorm(x, axis=-1), ctx_1024, 32, L0_xattn_Wq, L0_xattn_bq, L0_xattn_Wk, L0_xattn_bk, L0_xattn_Wv, L0_xattn_bv, L0_xattn_Wo, L0_xattn_bo)
    x = x + _L0_attn_ref(_layernorm(x, axis=-1), L0_attn_weight_q, L0_attn_weight_k, L0_attn_weight_v, L0_attn_theta)
    x = x + _L0_ffn_ref(_layernorm(x, axis=-1), L0_ffn_in_proj_w, L0_ffn_in_proj_b, L0_ffn_out_proj_w, L0_ffn_out_proj_b, L0_ffn_ln1_g, L0_ffn_ln1_b, L0_ffn_ln2_g, L0_ffn_ln2_b, L0_ffn_wg, L0_ffn_w1, L0_ffn_b1, L0_ffn_w2, L0_ffn_b2)
    x = x + _L1_xattn_ref(_layernorm(x, axis=-1), ctx_1024, ctx_1024, L1_xattn_norm_w, L1_xattn_norm_b, L1_xattn_norm1_w, L1_xattn_norm1_b, L1_xattn_Wq, L1_xattn_bq, L1_xattn_Wk, L1_xattn_bk, L1_xattn_Wv, L1_xattn_bv, L1_xattn_Wo, L1_xattn_bo)
    x = x + _L1_attn_ref(_layernorm(x, axis=-1), L1_attn_input_weights, L1_attn_xis, L1_attn_proj_matrix)
    x = x + _L1_ffn_ref(_layernorm(x, axis=-1), L1_ffn_q_node_w, L1_ffn_q_node_b, L1_ffn_q_w1, L1_ffn_q_b1, L1_ffn_q_w2, L1_ffn_q_b2, L1_ffn_k_node_w, L1_ffn_k_node_b, L1_ffn_k_w1, L1_ffn_k_b1, L1_ffn_k_w2, L1_ffn_k_b2, L1_ffn_v_node_w, L1_ffn_v_node_b, L1_ffn_v_w1, L1_ffn_v_b1, L1_ffn_v_w2, L1_ffn_v_b2)
    return x

_drawn_inputs = setup_inputs


def setup_inputs(seed=0):
    import zlib

    import numpy as np

    out = dict(_drawn_inputs(seed))
    spreads = {'L0_xattn_bq': (0.0, 0.1),
     'L0_xattn_bk': (0.0, 0.8),
     'L0_xattn_bv': (0.0, 0.1),
     'L0_xattn_bo': (0.0, 0.1),
     'L0_ffn_in_proj_b': (0.0, 0.1),
     'L0_ffn_out_proj_b': (0.0, 0.1),
     'L0_ffn_ln1_g': (1.0, 0.2),
     'L0_ffn_ln1_b': (0.0, 0.1),
     'L0_ffn_ln2_g': (1.0, 0.2),
     'L0_ffn_ln2_b': (0.0, 0.1),
     'L0_ffn_b1': (0.0, 0.563),
     'L0_ffn_b2': (0.0, 0.1),
     'L1_xattn_norm_w': (1.0, 0.2),
     'L1_xattn_norm_b': (0.0, 0.1),
     'L1_xattn_norm1_w': (1.0, 0.2),
     'L1_xattn_norm1_b': (0.0, 0.1),
     'L1_xattn_bq': (0.0, 0.1),
     'L1_xattn_bk': (0.0, 0.8),
     'L1_xattn_bv': (0.0, 0.1),
     'L1_xattn_bo': (0.0, 0.1),
     'L1_ffn_q_b1': (0.0, 0.8),
     'L1_ffn_q_b2': (0.0, 0.8),
     'L1_ffn_k_b1': (0.0, 0.8),
     'L1_ffn_k_b2': (0.0, 0.8),
     'L1_ffn_v_b1': (0.0, 0.8),
     'L1_ffn_v_b2': (0.0, 0.8)}
    factors = {'L1_ffn_q_node_w': 8.0,
     'L1_ffn_q_node_b': 8.0,
     'L1_ffn_q_w1': 8.0,
     'L1_ffn_q_w2': 8.0,
     'L1_ffn_k_node_w': 8.0,
     'L1_ffn_k_node_b': 8.0,
     'L1_ffn_k_w1': 8.0,
     'L1_ffn_k_w2': 8.0,
     'L1_ffn_v_node_w': 4.794,
     'L1_ffn_v_node_b': 8.0,
     'L1_ffn_v_w1': 5.748,
     'L1_ffn_v_w2': 3.285}
    for name, (base, spread) in spreads.items():
        noise = np.random.default_rng([zlib.crc32(name.encode()), seed]).standard_normal(out[name].shape)
        drawn = base * np.exp(spread * noise) if base else spread * noise
        out[name] = jnp.asarray(drawn.astype(out[name].dtype))
    for name, factor in factors.items():
        out[name] = (out[name] * factor).astype(out[name].dtype)
    return out
```

```python
from contextlib import ExitStack

import concourse.bass as bass
import numpy as np
from concourse import mybir

F32 = mybir.dt.float32
BF16 = mybir.dt.bfloat16
F32R = mybir.dt.float32r
ALU = mybir.AluOpType
ACT = mybir.ActivationFunctionType
X = mybir.AxisListType.X

B, L, D = 16, 64, 256
S = 1601
P = 128
N = B * L
NT = N // P
KD = D // P
NC = -(-S // P)
SL = S - (NC - 1) * P
SW = -(-S // 4)
QUARTERS = [(i * SW, min(SW, S - i * SW)) for i in range(4)]
TOPK = 32
LOWEST = -3.0e38
MASKED = -1.0e30
EPS = 1e-5
H0, HD0 = 4, 64
E, CAP, FF = 8, N // 8, 1024
FC = FF // P
H1, HD1 = 16, 16
NLEAF, NNODE, DEPTH, TREES = 16, 15, 4, 3
HALF = N // 2

PACKS = {
    "pk": [("ident", P)],
    "pa": [("l0_wqT", 512), ("l0_wk", 512), ("l0_wvT", 512), ("l0_woT", 512),
           ("l0_bq", 2), ("l0_bk", 2), ("l0_bv", 2), ("l0_bo", 256)],
    "pb0": [("ret_wq", 512), ("ret_wk", 512), ("ret_wv", 512), ("ret_theta", 2), ("ret_decay", P)],
    "pb1": [("mha_wqT", 512), ("mha_wkT", 512), ("mha_wvT", 512), ("mha_bq", 2), ("mha_bk", 2),
           ("mha_bv", 256), ("mha_mask", 2 * P), ("mha_woT", 512), ("mha_bo", 256),
           ("ln1_g", 256), ("ln1_b", 256)],
    "pc": [("moe_wg", 16), ("moe_prefer", 8), ("moe_base", 8), ("moe_tri", P), ("moe_ones", P),
           ("moe_iota", E * CAP), ("moe_b1", E * FC), ("moe_b2", E * D), ("ln2_g", 256), ("ln2_b", 256)],
    "pd": [("n_wrow", 256), ("n_brow", 256), ("n_wcol", 2), ("n_bcol", 2), ("n1_w", 256), ("n1_b", 256),
           ("l1_wq", 512), ("l1_wk", 512), ("l1_wv", 512), ("l1_wo", 512), ("l1_bq", 2), ("l1_bk", 2),
           ("l1_bv", 2), ("l1_bo", 256), ("head_mask", 8), ("parity", 2)],
    "pe": [("rf_gsT", 512), ("rf_iwT", 512), ("rf_ab", 256), ("rf_abcol", 2)],
    "pf": [("ff_nodes", 2 * TREES * NNODE), ("ff_nodeb", TREES * NNODE), ("ff_w1", TREES * 2048),
           ("ff_w2", TREES * 2048), ("ff_b1", TREES * 8), ("ff_b2", TREES * 256),
           ("ff_leaf", 8 * P), ("pair_mask", P)],
}
WIDTH = {k: sum(n for _, n in v) for k, v in PACKS.items()}


class Signals:

    def __init__(self, nc):
        self.nc, self.made = nc, {}

    def __call__(self, name):
        if name not in self.made:
            self.made[name] = self.nc.alloc_semaphore(name=name)
        return self.made[name]

    def close(self):
        self.nc.clear_and_free_semaphores(list(self.made.values()))
        self.nc.all_engine_barrier()


class Core:

    def __init__(self, nc, ctx):
        self.nc, self.sig = nc, None
        self.psum = ctx.enter_context(nc.psum_tensor("psum", [P, 8, 512], F32))
        self.params, self.packs = {}, {}

    def tensor(self, ctx, name, shape, dt=F32):
        return ctx.enter_context(self.nc.sbuf_tensor(name, shape, dt))

    def phase(self, build, *args):
        self.sig = Signals(self.nc)
        build(self, *args)
        self.sig.close()

    def load_pack(self, ctx, pack):
        tile = self.tensor(ctx, pack, [P, WIDTH[pack]])
        self.packs[pack] = tile
        at = 0
        for name, n in PACKS[pack]:
            self.params[name] = tile[:, at:at + n]
            at += n
        return tile

    def p(self, name):
        return self.params[name]

    def w(self, name):
        return self.params[name].rearrange("p (k n) -> p k n", k=KD)


def natural(dram):
    return dram.rearrange("(t b) l d -> (b l) t d", t=NT)


def norm_vector(dve, sig, tag, scratch, src, dst, ready=(), gain=None, shift=None):
    stats, moments, var, std, rstd = scratch
    for s, v in ready:
        dve.wait_ge(s, v)
    for t in range(NT):
        dve.bn_stats(stats[:, t, :], src[:, t, :]).then_inc(sig(f"{tag}_stats"), 1)
    for t in range(NT):
        dve.wait_ge(sig(f"{tag}_stats"), t + 1)
        dve.bn_aggr(moments[:, t, :], stats[:, t, :]).then_inc(sig(f"{tag}_moments"), 1)
    dve.wait_ge(sig(f"{tag}_moments"), NT)
    dve.tensor_scalar(var[:, :], moments[:, :, 1], EPS, None, ALU.add).then_inc(sig(f"{tag}_var"), 1)
    dve.wait_ge(sig(f"{tag}_std"), 1)
    dve.reciprocal(rstd[:, :], std[:, :]).then_inc(sig(f"{tag}_rstd"), 1)
    dve.wait_ge(sig(f"{tag}_rstd"), 1)
    for t in range(NT):
        dve.tensor_scalar(dst[:, t, :], src[:, t, :], moments[:, t, 0:1], rstd[:, t:t + 1],
                          ALU.subtract, ALU.mult).then_inc(sig(f"{tag}_out"), 1)
    if gain is not None:
        dve.wait_ge(sig(f"{tag}_out"), NT)
        for t in range(NT):
            dve.tensor_tensor(dst[:, t, :], dst[:, t, :], gain, ALU.mult).then_inc(sig(f"{tag}_gained"), 1)
        for t in range(NT):
            dve.wait_ge(sig(f"{tag}_gained"), t + 1)
            dve.tensor_tensor(dst[:, t, :], dst[:, t, :], shift, ALU.add).then_inc(sig(f"{tag}_shifted"), 1)


def norm_scalar(act, sig, tag, scratch):
    act.wait_ge(sig(f"{tag}_var"), 1)
    act.activation(scratch[3][:, :], scratch[2][:, :], ACT.Sqrt).then_inc(sig(f"{tag}_std"), 1)


def turn_tensor(pe, core, tag, src, first, ready, free=()):
    for s, v in free:
        pe.wait_ge(s, v)
    for c in range(2):
        for s, each in ready:
            pe.wait_ge(s, 4 * (c + 1) if each else 1)
        for k in range(KD):
            for j in range(4):
                last = pe.transpose(core.psum[:, first + 2 * c + k, j * P:(j + 1) * P],
                                    src[:, 4 * c + j, k * P:(k + 1) * P], core.p("ident"))
            last.then_inc(core.sig(f"{tag}_ps"), 1)


def by_group(T, k, c):
    return T[:, k, :].rearrange("p (g l j) -> p l g j", l=B, j=8)[:, 8 * c:8 * c + 8, :, :]


def grouped(psum_bank):
    return psum_bank.rearrange("p (l g j) -> p l g j", l=8, j=8)


def turn_scalar(act, core, tag, dst, first, group=False):
    for c in range(2):
        act.wait_ge(core.sig(f"{tag}_ps"), 2 * c + 1)
        out, bank = dst[:, 0, c * HALF:(c + 1) * HALF], core.psum[:, first + 2 * c, :]
        if group:
            out, bank = by_group(dst, 0, c), grouped(bank)
        act.activation(out, bank, ACT.Copy).then_inc(core.sig(f"{tag}_a"), 1)


def turn_vector(dve, core, tag, dst, first, group=False):
    for c in range(2):
        dve.wait_ge(core.sig(f"{tag}_ps"), 2 * c + 2)
        out, bank = dst[:, 1, c * HALF:(c + 1) * HALF], core.psum[:, first + 2 * c + 1, :]
        if group:
            out, bank = by_group(dst, 1, c), grouped(bank)
        dve.tensor_copy(out, bank).then_inc(core.sig(f"{tag}_d"), 1)


def project_tensor(pe, core, tag, weight, src, first, src_tag, free=(), ready=()):
    for s, v in tuple(free) + tuple(ready):
        pe.wait_ge(s, v)
    for c in range(2):
        pe.wait_ge(core.sig(f"{src_tag}_a"), c + 1)
        pe.wait_ge(core.sig(f"{src_tag}_d"), c + 1)
        for m in range(KD):
            for k in range(KD):
                last = pe.matmul(core.psum[:, first + 2 * c + m, :], weight[:, k, m * P:(m + 1) * P],
                                 src[:, k, c * HALF:(c + 1) * HALF], start=(k == 0), stop=(k == KD - 1))
            last.then_inc(core.sig(f"{tag}_ps"), 1)


def project_scalar(act, core, tag, dst, first, bias=None, scale=1.0):
    for c in range(2):
        act.wait_ge(core.sig(f"{tag}_ps"), 2 * c + 1)
        b = 0.0 if bias is None else bias[:, 0:1]
        act.activation(dst[:, 0, c * HALF:(c + 1) * HALF], core.psum[:, first + 2 * c, :],
                       ACT.Identity, bias=b, scale=scale).then_inc(core.sig(f"{tag}_a"), 1)


def project_vector(dve, core, tag, dst, first, bias, op=ALU.add):
    for c in range(2):
        dve.wait_ge(core.sig(f"{tag}_ps"), 2 * c + 2)
        dve.tensor_scalar(dst[:, 1, c * HALF:(c + 1) * HALF], core.psum[:, first + 2 * c + 1, :],
                          bias[:, 1:2], None, op).then_inc(core.sig(f"{tag}_d"), 1)


def both(sig, tag, v=2):
    return [(sig(f"{tag}_a"), v), (sig(f"{tag}_d"), v)]


def rows_tensor(pe, core, tag, src, weight, first, waits):
    for s, v in waits:
        pe.wait_ge(s, v)
    for i in range(NT // 2):
        for j in range(2):
            t = 2 * i + j
            for k in range(KD):
                last = pe.matmul(core.psum[:, first + i, j * D:(j + 1) * D], src[:, k, t * P:(t + 1) * P],
                                 weight[:, k, :], start=(k == 0), stop=(k == KD - 1))
        last.then_inc(core.sig(f"{tag}_ps"), 1)


def two(psum_bank):
    return psum_bank.rearrange("p (j n) -> p j n", j=2)


def scratch_of(core, ctx, name):
    return (core.tensor(ctx, f"{name}_stats", [P, NT, 6]), core.tensor(ctx, f"{name}_moments", [P, NT, 2]),
            core.tensor(ctx, f"{name}_var", [P, NT]), core.tensor(ctx, f"{name}_std", [P, NT]),
            core.tensor(ctx, f"{name}_rstd", [P, NT]))


def phase_topk_read(core, x, drams, cstats):
    nc, sig, ps = core.nc, core.sig, core.psum
    with ExitStack() as ctx:
        ctx_rows, ctxT = drams["ctx_rows"], drams["ctxT"]
        params = core.load_pack(ctx, "pa")
        scratch = scratch_of(core, ctx, "a_ln")
        xn = core.tensor(ctx, "a_xn", [P, NT, D])
        xnT = core.tensor(ctx, "a_xnT", [P, KD, N])
        qT = core.tensor(ctx, "a_qT", [P, KD, N])
        keyqT = core.tensor(ctx, "a_keyqT", [P, KD, N])
        qbk = core.tensor(ctx, "a_qbk", [P, NT])
        cT = core.tensor(ctx, "a_cT", [P, 2, 2, KD, S])
        cR = core.tensor(ctx, "a_cR", [P, 2, 2, NC, D])
        pair_q = core.tensor(ctx, "a_pair_q", [P, 2, KD, P])
        pair_c = core.tensor(ctx, "a_pair_c", [P, 2])
        scores = core.tensor(ctx, "a_scores", [P, 2, S])
        left = core.tensor(ctx, "a_left", [P, S])
        probs = core.tensor(ctx, "a_probs", [P, S])
        probsT = core.tensor(ctx, "a_probsT", [P, NC, P])
        best = core.tensor(ctx, "a_best", [P, TOPK // 8, 8])
        negmax = core.tensor(ctx, "a_negmax", [P, 1])
        fence = core.tensor(ctx, "a_fence", [P, 1])
        total = core.tensor(ctx, "a_total", [P, 2])
        inv = core.tensor(ctx, "a_inv", [P, 2])
        read, readT, valT = xn, xnT, qT
        block = ctx.enter_context(nc.Block())
        T_BANK, V_BANK = 4, 6

        @block.sync
        def _(sp):
            sp.dma_start(x[:, :, :], natural(drams["x"])).then_inc(sig("a_x_in"), 16)
            sp.dma_start(core.packs["pk"][:, :], drams["pk"]).then_inc(sig("ident_in"), 16)
            sp.dma_start(params[:, :], drams["pa"]).then_inc(sig("a_params_in"), 16)

            def load(i, u, turn):
                for j in range(2):
                    at = bass.ds(4 * i + 2 * u + j, 1)
                    if turn is not None:
                        sp.wait_ge(sig("a_scores_ps"), 8 * i + 4 * u - 4)
                    sp.dma_start(cT[:, u, j, :, :], ctxT[at].rearrange("b (k p) s -> p (b k) s", p=P))\
                      .then_inc(sig(f"a_cT_in{u}{j}"), 16)
                for j in range(2):
                    at = bass.ds(4 * i + 2 * u + j, 1)
                    if turn is not None:
                        sp.wait_ge(sig("a_pair_read"), 2 * i + u - 1)
                        sp.wait_ge(sig("a_pair_stats"), 2 * i + u - 1)
                    sp.dma_start(cR[:, u, j, :, :], ctx_rows[at].rearrange("b (c p) d -> p (b c) d", p=P))\
                      .then_inc(sig(f"a_cR_in{u}{j}"), 16)

            load(0, 0, None)
            load(0, 1, None)
            with sp.Fori(1, NT // 2) as i:
                load(i, 0, i)
                load(i, 1, i)

        @block.tensor
        def _(pe):
            pe.wait_ge(sig("ident_in"), 16)
            pe.wait_ge(sig("a_params_in"), 16)
            turn_tensor(pe, core, "a_xnT", xn, 0, [(sig("a_ln_out"), True)])
            project_tensor(pe, core, "a_qT", core.w("l0_wqT"), xnT, 4, "a_xnT")
            project_tensor(pe, core, "a_keyqT", core.w("l0_wk"), qT, 0, "a_qT", free=both(sig, "a_xnT"))
            for s, v in both(sig, "a_qT"):
                pe.wait_ge(s, v)
            for t in range(NT):
                for k in range(KD):
                    last = pe.matmul(ps[:, 4, t:t + 1], qT[:, k, t * P:(t + 1) * P],
                                     core.p("l0_bk")[:, k:k + 1], start=(k == 0), stop=(k == KD - 1))
            last.then_inc(sig("a_qbk_ps"), 1)
            for s, v in both(sig, "a_keyqT"):
                pe.wait_ge(s, v)
            pe.wait_ge(sig("a_qbk"), 1)

            def score(i, u, first=False):
                n = 2 * i + u
                pe.wait_ge(sig("a_pair_q"), n + 1)
                if not first:
                    pe.wait_ge(sig("a_scores"), 4 * n)
                for j in range(2):
                    pe.wait_ge(sig(f"a_cT_in{u}{j}"), 16 * i + 16)
                for c, (s0, w) in enumerate(QUARTERS):
                    for k in range(KD):
                        for j in range(2):
                            last = pe.matmul(ps[64 * j:64 * j + 64, c, 0:w],
                                             pair_q[:, u, k, 64 * j:64 * j + 64],
                                             cT[:, u, j, k, s0:s0 + w], start=(k == 0), stop=(k == KD - 1),
                                             tile_position=(0, 64 * j))
                    last.then_inc(sig("a_scores_ps"), 1)

            def value(i, u, first=False):
                n = 2 * i + u
                pe.wait_ge(sig("a_probs"), n + 1)
                for g in range(4):
                    if not (first and g < 2):
                        pe.wait_ge(sig("a_probsT"), 4 * n + g - 1)
                    for c in range(4 * g, min(4 * g + 4, NC)):
                        w = P if c < NC - 1 else SL
                        last = pe.transpose(ps[0:w, T_BANK + g % 2, (c % 4) * P:(c % 4 + 1) * P],
                                            probs[:, c * P:c * P + w], core.p("ident"))
                    last.then_inc(sig("a_probsT_ps"), 1)
                pe.wait_ge(sig("a_probsT"), 4 * n + 4)
                for j in range(2):
                    pe.wait_ge(sig(f"a_cR_in{u}{j}"), 16 * i + 16)
                if not first:
                    pe.wait_ge(sig("a_read"), n)
                for c in range(NC):
                    w = P if c < NC - 1 else SL
                    for j in range(2):
                        last = pe.matmul(ps[64 * j:64 * j + 64, V_BANK, 0:D], probsT[0:w, c, 64 * j:64 * j + 64],
                                         cR[0:w, u, j, c, :], start=(c == 0), stop=(c == NC - 1),
                                         tile_position=(0, 64 * j))
                last.then_inc(sig("a_pair_read"), 1)

            score(0, 0, first=True)
            score(0, 1)
            value(0, 0, first=True)
            with pe.Fori(1, NT // 2) as i:
                score(i, 0)
                value(i - 1, 1)
                score(i, 1)
                value(i, 0)
            value(NT // 2 - 1, 1)
            turn_tensor(pe, core, "a_readT", read, 0, [(sig("a_read"), True)])
            project_tensor(pe, core, "a_valT", core.w("l0_wvT"), readT, 4, "a_readT",
                           free=[(sig("a_read"), NT), (sig("a_probsT"), 4 * NT)])
            rows_tensor(pe, core, "a_out", valT, core.w("l0_woT"), 0, both(sig, "a_valT") + both(sig, "a_readT"))

        @block.scalar
        def _(act):
            norm_scalar(act, sig, "a_ln", scratch)
            turn_scalar(act, core, "a_xnT", xnT, 0)
            project_scalar(act, core, "a_qT", qT, 4, core.p("l0_bq"))
            project_scalar(act, core, "a_keyqT", keyqT, 0)
            act.wait_ge(sig("a_qbk_ps"), 1)
            act.mul(qbk[:, :], ps[:, 4, 0:NT], D ** -0.5).then_inc(sig("a_qbk"), 1)

            def gather(i, u, first=False):
                n = 2 * i + u
                act.wait_ge(sig("a_pair_q"), n + 1)
                if not first:
                    act.wait_ge(sig("a_probs"), n - 1)
                for c, (s0, w) in enumerate(QUARTERS):
                    act.wait_ge(sig("a_scores_ps"), 4 * n + c + 1)
                    act.activation(scores[:, u, s0:s0 + w], ps[:, c, 0:w], ACT.Identity,
                                   bias=pair_c[:, u:u + 1], scale=D ** -0.5).then_inc(sig("a_scores"), 1)

            def exps(i, u, first=False):
                n = 2 * i + u
                act.wait_ge(sig("a_negmax"), n + 1)
                act.wait_ge(sig("a_scores"), 4 * n + 4)
                if not first:
                    act.wait_ge(sig("a_probsT_ps"), 4 * n)
                act.activation(probs[:, :], scores[:, u, :], ACT.Exp, bias=negmax[:, 0:1])\
                   .then_inc(sig("a_exp"), 1)

            def take(i, u, first=False):
                n = 2 * i + u
                for g in range(4):
                    act.wait_ge(sig("a_probsT_ps"), 4 * n + g + 1)
                    if g == 0 and not first:
                        act.wait_ge(sig("a_pair_read"), n)
                    if g < 3:
                        act.activation(probsT[:, 4 * g:4 * g + 4, :], ps[:, T_BANK + g % 2, :], ACT.Copy)\
                           .then_inc(sig("a_probsT"), 1)
                    else:
                        act.activation(probsT[0:SL, 12, :], ps[0:SL, T_BANK + 1, 0:P], ACT.Copy)\
                           .then_inc(sig("a_probsT"), 1)
                act.wait_ge(sig("a_pair_read"), n + 1)
                act.wait_ge(sig("a_inv"), n + 1)
                act.activation(read[:, bass.ds(2 * i + u, 1), :].rearrange("p a d -> p (a d)"),
                               ps[:, V_BANK, 0:D], ACT.Copy, scale=inv[:, u:u + 1]).then_inc(sig("a_read"), 1)

            gather(0, 0, first=True)
            gather(0, 1, first=True)
            exps(0, 0, first=True)
            take(0, 0, first=True)
            with act.Fori(1, NT // 2) as i:
                gather(i, 0)
                exps(i - 1, 1)
                take(i - 1, 1)
                gather(i, 1)
                exps(i, 0)
                take(i, 0)
            exps(NT // 2 - 1, 1)
            take(NT // 2 - 1, 1)
            turn_scalar(act, core, "a_readT", readT, 0)
            project_scalar(act, core, "a_valT", valT, 4, core.p("l0_bv"))

        @block.vector
        def _(dve):
            norm_vector(dve, sig, "a_ln", scratch, x, xn, ready=[(sig("a_x_in"), 16)])
            dve.wait_ge(sig("a_params_in"), 16)
            turn_vector(dve, core, "a_xnT", xnT, 0)
            project_vector(dve, core, "a_qT", qT, 4, core.p("l0_bq"))
            for c in range(2):
                dve.wait_ge(sig("a_keyqT_ps"), 2 * c + 2)
                dve.tensor_copy(keyqT[:, 1, c * HALF:(c + 1) * HALF], ps[:, 2 * c + 1, :])\
                   .then_inc(sig("a_keyqT_d"), 1)
            dve.wait_ge(sig("a_qbk"), 1)
            for s, v in both(sig, "a_keyqT"):
                dve.wait_ge(s, v)

            def pair_inputs(i, u):
                t = 2 * i + u
                dve.tensor_copy(pair_c[:, u:u + 1], qbk[:, bass.ds(t, 1)]).then_inc(sig("a_pair_c"), 1)
                dve.wait_ge(sig("a_pair_c"), t + 1)
                dve.tensor_copy(pair_q[:, u, :, :], keyqT[:, :, bass.ds(t * P, P)]).then_inc(sig("a_pair_q"), 1)

            def choose(i, u, first=False):
                n = 2 * i + u
                dve.wait_ge(sig("a_scores"), 4 * n + 4)
                for r in range(TOPK // 8):
                    src = scores[:, u, :] if r == 0 else left[:, :]
                    if r:
                        dve.wait_ge(sig("a_left"), 4 * n + r)
                    dve.memset(fence[:, :], 0.0)
                    dve.max(best[:, r, :], src).then_inc(sig("a_best"), 1)
                    dve.wait_ge(sig("a_best"), 4 * n + r + 1)
                    if r == 0:
                        dve.tensor_scalar(negmax[:, :], best[:, 0, 0:1], -1.0, None, ALU.mult)\
                           .then_inc(sig("a_negmax"), 1)
                    dve.memset(fence[:, :], 0.0)
                    dve.match_replace(left[:, :], best[:, r, :], src, LOWEST).then_inc(sig("a_left"), 1)
                dve.wait_ge(sig("a_left"), 4 * n + 4)
                dve.wait_ge(sig("a_exp"), n + 1)
                dve.scalar_tensor_tensor(probs[:, :], left[:, :], LOWEST, probs[:, :], ALU.is_le, ALU.mult,
                                         accum_out=total[:, u:u + 1]).then_inc(sig("a_probs"), 1)
                dve.wait_ge(sig("a_probs"), n + 1)
                if not first:
                    dve.wait_ge(sig("a_read"), n)
                dve.reciprocal(inv[:, u:u + 1], total[:, u:u + 1]).then_inc(sig("a_inv"), 1)

            def row_stats(i, u):
                for j in range(2):
                    dve.wait_ge(sig(f"a_cR_in{u}{j}"), 16 * i + 16)
                    for c in range(NC):
                        col = (4 * i + 2 * u + j) * NC + c
                        last = dve.bn_stats(cstats[:, bass.ds(col, 1), :].rearrange("p a n -> p (a n)"),
                                            cR[:, u, j, c, :])
                last.then_inc(sig("a_pair_stats"), 1)

            pair_inputs(0, 0)
            pair_inputs(0, 1)
            choose(0, 0, first=True)
            row_stats(0, 0)
            with dve.Fori(1, NT // 2) as i:
                for u, (ci, cu) in enumerate(((i - 1, 1), (i, 0))):
                    dve.wait_ge(sig("a_scores_ps"), 8 * i + 4 * u - 4)
                    dve.wait_ge(sig("a_scores"), 8 * i + 4 * u - 4)
                    pair_inputs(i, u)
                    choose(ci, cu)
                    row_stats(ci, cu)
            choose(NT // 2 - 1, 1)
            row_stats(NT // 2 - 1, 1)
            turn_vector(dve, core, "a_readT", readT, 0)
            project_vector(dve, core, "a_valT", valT, 4, core.p("l0_bv"))
            for i in range(NT // 2):
                dve.wait_ge(sig("a_out_ps"), i + 1)
                dve.tensor_tensor(x[:, 2 * i:2 * i + 2, :], x[:, 2 * i:2 * i + 2, :], two(ps[:, i, :]), ALU.add)\
                   .then_inc(sig("a_x_sum"), 1)
            for t in range(NT):
                dve.wait_ge(sig("a_x_sum"), t // 2 + 1)
                dve.tensor_tensor(x[:, t, :], x[:, t, :], core.p("l0_bo"), ALU.add).then_inc(sig("a_x"), 1)


def phase_retention(core, x, drams):
    nc, sig, ps = core.nc, core.sig, core.psum
    with ExitStack() as ctx:
        params = core.load_pack(ctx, "pb0")
        scratch = scratch_of(core, ctx, "b_ln")
        xn = core.tensor(ctx, "b_xn", [P, NT, D])
        xnT = core.tensor(ctx, "b_xnT", [P, KD, N])
        theta = core.tensor(ctx, "b_theta", [P, KD])
        qT = core.tensor(ctx, "b_qT", [P, KD, N])
        kT = core.tensor(ctx, "b_kT", [P, KD, N])
        v = core.tensor(ctx, "b_v", [P, NT, D])
        sT = core.tensor(ctx, "b_sT", [P, NT, P])
        block = ctx.enter_context(nc.Block())

        @block.sync
        def _(sp):
            sp.dma_start(params[:, :], drams["pb0"]).then_inc(sig("b_params_in"), 16)

        @block.tensor
        def _(pe):
            pe.wait_ge(sig("b_params_in"), 16)
            turn_tensor(pe, core, "b_xnT", xn, 0, [(sig("b_ln_out"), True)])
            project_tensor(pe, core, "b_qT", core.w("ret_wq"), xnT, 4, "b_xnT")
            project_tensor(pe, core, "b_kT", core.w("ret_wk"), xnT, 0, "b_xnT", free=both(sig, "b_xnT"))
            rows_tensor(pe, core, "b_v", xnT, core.w("ret_wv"), 4, both(sig, "b_qT"))
            for s, n in both(sig, "b_kT"):
                pe.wait_ge(s, n)
            for t in range(NT):
                for k in range(KD):
                    last = pe.matmul(ps[:, t // 4, (t % 4) * P:(t % 4 + 1) * P], kT[:, k, t * P:(t + 1) * P],
                                     qT[:, k, t * P:(t + 1) * P], start=(k == 0), stop=(k == KD - 1))
                if t % 4 == 3:
                    last.then_inc(sig("b_sT_ps"), 1)
            pe.wait_ge(sig("b_v"), NT // 2)
            for t in range(NT):
                pe.wait_ge(sig("b_sT"), t // 4 + 1)
                last = pe.matmul(ps[:, 4 + t // 2, (t % 2) * D:(t % 2 + 1) * D], sT[:, t, :], v[:, t, :],
                                 start=True, stop=True)
                if t % 2:
                    last.then_inc(sig("b_out_ps"), 1)

        @block.scalar
        def _(act):
            act.wait_ge(sig("b_params_in"), 16)
            act.activation(theta[:, :], core.p("ret_theta"), ACT.Exp, scale=0.0).then_inc(sig("b_theta"), 1)
            norm_scalar(act, sig, "b_ln", scratch)
            turn_scalar(act, core, "b_xnT", xnT, 0)
            act.wait_ge(sig("b_theta"), 1)
            project_scalar(act, core, "b_qT", qT, 4, scale=theta[:, 0:1])
            project_scalar(act, core, "b_kT", kT, 0, scale=theta[:, 0:1])
            for i in range(NT // 2):
                act.wait_ge(sig("b_v_ps"), i + 1)
                act.activation(v[:, 2 * i:2 * i + 2, :], two(ps[:, 4 + i, :]), ACT.Copy).then_inc(sig("b_v"), 1)

        @block.vector
        def _(dve):
            norm_vector(dve, sig, "b_ln", scratch, x, xn)
            turn_vector(dve, core, "b_xnT", xnT, 0)
            dve.wait_ge(sig("b_theta"), 1)
            project_vector(dve, core, "b_qT", qT, 4, theta, ALU.mult)
            project_vector(dve, core, "b_kT", kT, 0, theta, ALU.mult)
            decay = core.p("ret_decay").unsqueeze(1).broadcast_to([P, 4, P])
            for i in range(2):
                dve.wait_ge(sig("b_sT_ps"), i + 1)
                dve.tensor_tensor(sT[:, 4 * i:4 * i + 4, :], ps[:, i, :].rearrange("p (t n) -> p t n", t=4), decay,
                                  ALU.mult).then_inc(sig("b_sT"), 1)
            for i in range(NT // 2):
                dve.wait_ge(sig("b_out_ps"), i + 1)
                dve.tensor_tensor(x[:, 2 * i:2 * i + 2, :], x[:, 2 * i:2 * i + 2, :], two(ps[:, 4 + i, :]), ALU.add)\
                   .then_inc(sig("b_x"), 1)


def phase_moe(core, x, drams):
    with ExitStack() as ctx:
        w1 = core.tensor(ctx, "moe_w1", [P, 2, KD, FF])
        w2 = core.tensor(ctx, "moe_w2", [P, 2, FC, D])
        y1 = core.tensor(ctx, "moe_in", [P, NT, D])
        phase_mha(core, x, y1, w1, w2, drams)
        phase_experts(core, x, y1, w1, w2, drams)


def load_expert(sp, sig, w1, w2, drams, e, u):
    sp.dma_start(w1[:, u, :, :], drams["moe_w1"][e].rearrange("e (k p) f -> p (e k) f", p=P))\
      .then_inc(sig(f"c_w1_in{u}"), 16)
    sp.dma_start(w2[:, u, :, :], drams["moe_w2"][e].rearrange("e (c p) d -> p (e c) d", p=P))\
      .then_inc(sig(f"c_w2_in{u}"), 16)


def phase_mha(core, x, y1, w1, w2, drams):
    nc, sig, ps = core.nc, core.sig, core.psum
    G, J = 8, 8
    with ExitStack() as ctx:
        params = core.load_pack(ctx, "pb1")
        scratch = scratch_of(core, ctx, "m_ln")
        scratch2 = scratch_of(core, ctx, "m_ln2")
        xf = core.tensor(ctx, "m_xf", [P, NT, D])
        xfT = core.tensor(ctx, "m_xfT", [P, KD, N])
        qT = core.tensor(ctx, "m_qT", [P, KD, N])
        kT = core.tensor(ctx, "m_kT", [P, KD, N])
        vG = core.tensor(ctx, "m_vG", [P, G, D])
        oT = core.tensor(ctx, "m_oT", [P, KD, N])
        s = core.tensor(ctx, "m_s", [P, 2, H0, P])
        s1 = core.tensor(ctx, "m_s1", [P, 2, H0, P])
        prob = core.tensor(ctx, "m_prob", [P, 2, H0, P])
        probn = core.tensor(ctx, "m_probn", [P, 2, H0, P])
        probT = core.tensor(ctx, "m_probT", [P, 2, H0, P])
        negmax = core.tensor(ctx, "m_negmax", [P, 2, H0])
        total = core.tensor(ctx, "m_total", [P, 2, H0])
        inv = core.tensor(ctx, "m_inv", [P, 2, H0])
        block = ctx.enter_context(nc.Block())

        def group(T, g):
            return T[:, :, :].rearrange("p k (l n) -> p k l n", l=B)[:, :, :, J * g:J * g + J]

        @block.sync
        def _(sp):
            sp.dma_start(params[:, :], drams["pb1"]).then_inc(sig("m_params_in"), 16)
            for u in range(2):
                load_expert(sp, sig, w1, w2, drams, bass.ds(u, 1), u)

        @block.tensor
        def _(pe):
            pe.wait_ge(sig("m_params_in"), 16)
            turn_tensor(pe, core, "m_xfT", xf, 0, [(sig("m_ln_out"), True)])
            project_tensor(pe, core, "m_qT", core.w("mha_wqT"), xfT, 4, "m_xfT", ready=both(sig, "m_xfT"))
            project_tensor(pe, core, "m_kT", core.w("mha_wkT"), xfT, 0, "m_xfT", free=both(sig, "m_xfT"))
            for sm, n in both(sig, "m_qT"):
                pe.wait_ge(sm, n)
            for g in range(G):
                for k in range(KD):
                    last = pe.matmul(ps[:, 4 + g // 2, (g % 2) * D:(g % 2 + 1) * D], xfT[:, k, g * P:(g + 1) * P],
                                     core.w("mha_wvT")[:, k, :], start=(k == 0), stop=(k == KD - 1))
                if g % 2:
                    last.then_inc(sig("m_vG_ps"), 1)

            def scores(g):
                if g >= 2:
                    pe.wait_ge(sig("m_s"), g - 1)
                for h in range(H0):
                    r = 64 * (h % 2)
                    last = pe.matmul(ps[:, 2 * (g % 2) + h % 2, (h // 2) * P:(h // 2 + 1) * P], qT[r:r + 64, h // 2, g * P:(g + 1) * P],
                                     kT[r:r + 64, h // 2, g * P:(g + 1) * P], start=True, stop=True,
                                     tile_position=(r, 0))
                last.then_inc(sig("m_s_ps"), 1)

            def values(g):
                pe.wait_ge(sig("m_probn"), g + 1)
                if g >= 2:
                    pe.wait_ge(sig("m_probT"), g - 1)
                for h in range(H0):
                    last = pe.transpose(ps[:, 4 + g % 2, h * P:(h + 1) * P], probn[:, g % 2, h, :], core.p("ident"))
                last.then_inc(sig("m_probT_ps"), 1)
                pe.wait_ge(sig("m_probT"), g + 1)
                if g >= 2:
                    pe.wait_ge(sig("m_oT_a"), g - 1)
                    pe.wait_ge(sig("m_oT_d"), g - 1)
                for q in range(H0):
                    h, r = 2 * (q % 2) + q // 2, 64 * (q // 2)
                    last = pe.matmul(ps[r:r + 64, 6 + g % 2, (h // 2) * P:(h // 2 + 1) * P],
                                     vG[:, g, h * HD0:(h + 1) * HD0], probT[:, g % 2, q, :],
                                     start=True, stop=True, tile_position=(0, r))
                last.then_inc(sig("m_oT_ps"), 1)

            for sm, n in both(sig, "m_kT"):
                pe.wait_ge(sm, n)
            scores(0)
            pe.wait_ge(sig("m_vG"), G // 2)
            for g in range(G):
                if g + 1 < G:
                    scores(g + 1)
                values(g)
            rows_tensor(pe, core, "m_proj", oT, core.w("mha_woT"), 0, both(sig, "m_oT", G) + [(sig("m_probT"), G)])

        @block.scalar
        def _(act):
            norm_scalar(act, sig, "m_ln", scratch)
            turn_scalar(act, core, "m_xfT", xfT, 0, group=True)
            act.wait_ge(sig("m_params_in"), 16)
            project_scalar(act, core, "m_qT", qT, 4, core.p("mha_bq"))
            project_scalar(act, core, "m_kT", kT, 0, core.p("mha_bk"))

            def exps(g):
                act.wait_ge(sig("m_s1"), g + 1)
                act.activation(prob[:, g % 2, :, :], s1[:, g % 2, :, :], ACT.Exp).then_inc(sig("m_prob"), 1)

            exps(0)
            for g in range(G):
                if g + 1 < G:
                    exps(g + 1)
                act.wait_ge(sig("m_probT_ps"), g + 1)
                act.activation(probT[:, g % 2, :, :], ps[:, 4 + g % 2, :], ACT.Copy).then_inc(sig("m_probT"), 1)
                act.wait_ge(sig("m_oT_ps"), g + 1)
                act.activation(group(oT, g)[:, 0, :, :], ps[:, 6 + g % 2, 0:P].rearrange("p (l j) -> p l j", j=J),
                               ACT.Copy).then_inc(sig("m_oT_a"), 1)
            norm_scalar(act, sig, "m_ln2", scratch2)

        @block.vector
        def _(dve):
            norm_vector(dve, sig, "m_ln", scratch, x, xf)
            turn_vector(dve, core, "m_xfT", xfT, 0, group=True)
            dve.wait_ge(sig("m_params_in"), 16)
            project_vector(dve, core, "m_qT", qT, 4, core.p("mha_bq"))
            project_vector(dve, core, "m_kT", kT, 0, core.p("mha_bk"))
            bv = core.p("mha_bv").unsqueeze(1).broadcast_to([P, 2, D])
            for i in range(G // 2):
                dve.wait_ge(sig("m_vG_ps"), i + 1)
                dve.tensor_tensor(vG[:, 2 * i:2 * i + 2, :], two(ps[:, 4 + i, :]), bv, ALU.add).then_inc(sig("m_vG"), 1)
            mask = core.p("mha_mask").unsqueeze(1).broadcast_to([P, 2, 2 * P])

            def masked(g):
                u = g % 2
                dve.wait_ge(sig("m_s_ps"), g + 1)
                dve.scalar_tensor_tensor(s[:, u, :, :].rearrange("p (r m) n -> p r (m n)", r=2),
                                         ps[:, 2 * u:2 * u + 2, 0:2 * P],
                                         HD0 ** -0.5, mask, ALU.mult, ALU.add).then_inc(sig("m_s"), 1)
                dve.wait_ge(sig("m_s"), g + 1)
                dve.tensor_reduce(negmax[:, u, :], s[:, u, :, :], X, ALU.max, negate=True)\
                   .then_inc(sig("m_negmax"), 1)
                dve.wait_ge(sig("m_negmax"), g + 1)
                if g >= 2:
                    dve.wait_ge(sig("m_prob"), g - 1)
                dve.tensor_tensor(s1[:, u, :, :], s[:, u, :, :],
                                  negmax[:, u, :].unsqueeze(2).broadcast_to([P, H0, P]), ALU.add)\
                   .then_inc(sig("m_s1"), 1)

            def normed(g):
                u = g % 2
                dve.wait_ge(sig("m_prob"), g + 1)
                dve.tensor_reduce(total[:, u, :], prob[:, u, :, :], X, ALU.add).then_inc(sig("m_total"), 1)
                dve.wait_ge(sig("m_total"), g + 1)
                dve.reciprocal(inv[:, u, :], total[:, u, :]).then_inc(sig("m_inv"), 1)
                dve.wait_ge(sig("m_inv"), g + 1)
                if g >= 2:
                    dve.wait_ge(sig("m_probT_ps"), g - 1)
                dve.tensor_tensor(probn[:, u, :, :], prob[:, u, :, :],
                                  inv[:, u, :].unsqueeze(2).broadcast_to([P, H0, P]), ALU.mult)\
                   .then_inc(sig("m_probn"), 1)

            def out(g):
                dve.wait_ge(sig("m_oT_ps"), g + 1)
                dve.wait_ge(sig("m_oT_a"), g + 1)
                dve.tensor_copy(group(oT, g)[:, 1, :, :], ps[:, 6 + g % 2, P:2 * P].rearrange("p (l j) -> p l j", j=J))\
                   .then_inc(sig("m_oT_d"), 1)

            masked(0)
            for g in range(G):
                if g + 1 < G:
                    masked(g + 1)
                normed(g)
                if g:
                    out(g - 1)
            out(G - 1)
            for i in range(NT // 2):
                dve.wait_ge(sig("m_proj_ps"), i + 1)
                dve.tensor_tensor(y1[:, 2 * i:2 * i + 2, :], two(ps[:, i, :]), xf[:, 2 * i:2 * i + 2, :], ALU.add)\
                   .then_inc(sig("m_res"), 1)
            for t in range(NT):
                dve.wait_ge(sig("m_res"), t // 2 + 1)
                dve.tensor_tensor(y1[:, t, :], y1[:, t, :], core.p("mha_bo"), ALU.add).then_inc(sig("m_y"), 1)
            norm_vector(dve, sig, "m_ln2", scratch2, y1, y1, [(sig("m_y"), NT)], core.p("ln1_g"), core.p("ln1_b"))


def phase_experts(core, x, y1, w1, w2, drams):
    nc, sig, ps = core.nc, core.sig, core.psum
    with ExitStack() as ctx:
        params = core.load_pack(ctx, "pc")
        scratch = scratch_of(core, ctx, "c_ln")
        y1T = core.tensor(ctx, "c_y1T", [P, KD, N])
        logit = core.tensor(ctx, "c_logit", [P, NT, E])
        tmp = core.tensor(ctx, "c_tmp", [P, NT, E])
        pref = core.tensor(ctx, "c_pref", [P, NT, E])
        oneh = core.tensor(ctx, "c_oneh", [P, NT, E])
        expl = core.tensor(ctx, "c_expl", [P, NT, E])
        col = core.tensor(ctx, "c_col", [P, 8, NT])
        gate, slot = col[:, 0, :], col[:, 1, :]
        place = core.tensor(ctx, "c_place", [P, NT, E * CAP])
        placeT = core.tensor(ctx, "c_placeT", [P, E, N])
        disp = core.tensor(ctx, "c_disp", [P, KD, E * CAP])
        hT = core.tensor(ctx, "c_hT", [P, 2, FC, CAP])
        y = core.tensor(ctx, "c_y", [P, E, D])
        y2 = y1T[:, :, :].rearrange("p k n -> p (k n)").rearrange("p (t d) -> p t d", t=NT)
        block = ctx.enter_context(nc.Block())

        @block.sync
        def _(sp):
            sp.dma_start(params[:, :], drams["pc"]).then_inc(sig("c_params_in"), 16)
            with sp.Fori(1, E // 2) as i:
                for u in range(2):
                    sp.wait_ge(sig("c_y_ps"), 2 * i + u - 1)
                    load_expert(sp, sig, w1, w2, drams, bass.ds(2 * i + u, 1), u)

        @block.tensor
        def _(pe):
            turn_tensor(pe, core, "c_y1T", y1, 0, [])
            pe.wait_ge(sig("c_params_in"), 16)
            for c in range(2):
                for s, n in both(sig, "c_y1T", c + 1):
                    pe.wait_ge(s, n)
                for t in range(4 * c, 4 * c + 4):
                    for k in range(KD):
                        last = pe.matmul(ps[:, 4, t * E:(t + 1) * E], y1T[:, k, t * P:(t + 1) * P],
                                         core.w("moe_wg")[:, k, :], start=(k == 0), stop=(k == KD - 1))
            last.then_inc(sig("c_logit_ps"), 1)
            pe.wait_ge(sig("c_oneh"), 1)
            for t in range(NT):
                for b in range(t + 1):
                    last = pe.matmul(ps[:, 5, t * E:(t + 1) * E], core.p("moe_tri" if b == t else "moe_ones"),
                                     oneh[:, b, :], start=(b == 0), stop=(b == t))
            last.then_inc(sig("c_count_ps"), 1)
            for t in range(NT):
                pe.wait_ge(sig("c_place"), t + 1)
                for k in range(KD):
                    for c in range(2):
                        last = pe.matmul(ps[:, 2 * k + c, :], y1[:, t, k * P:(k + 1) * P],
                                         place[:, t, c * HALF:(c + 1) * HALF], start=(t == 0), stop=(t == NT - 1))
            last.then_inc(sig("c_disp_ps"), 1)

            def turn_place(e, c, n):
                if n >= 2:
                    pe.wait_ge(sig("c_placeT"), n - 1)
                for j in range(4):
                    last = pe.transpose(ps[:, 6 + n % 2, j * P:(j + 1) * P],
                                        place[:, 4 * c + j, e * CAP:(e + 1) * CAP], core.p("ident"))
                last.then_inc(sig("c_placeT_ps"), 1)

            for n in range(2 * E):
                turn_place(n // 2, n % 2, n)
            pe.wait_ge(sig("c_disp"), 4)
            pe.wait_ge(sig("c_slot"), 1)

            def hidden(i, u, first=False):
                n = 2 * i + u
                pe.wait_ge(sig(f"c_w1_in{u}"), 16 * i + 16)
                for q in range(2):
                    if not first:
                        pe.wait_ge(sig("c_hT"), 2 * n + q - 1)
                    for f in range(4 * q, 4 * q + 4):
                        for k in range(KD):
                            last = pe.matmul(ps[:, q, (f % 4) * P:(f % 4 + 1) * P], w1[:, u, k, f * P:(f + 1) * P],
                                             disp[:, k, bass.ds(n * CAP, CAP)], start=(k == 0), stop=(k == KD - 1))
                    last.then_inc(sig("c_hT_ps"), 1)

            def output(i, u, first=False):
                n = 2 * i + u
                pe.wait_ge(sig(f"c_w2_in{u}"), 16 * i + 16)
                pe.wait_ge(sig("c_hT"), 2 * n + 2)
                if not first:
                    pe.wait_ge(sig("c_y"), n - 1)
                for f in range(FC):
                    last = pe.matmul(ps[:, 2 + u, 0:D], hT[:, u, f, :], w2[:, u, f, :], start=(f == 0),
                                     stop=(f == FC - 1))
                last.then_inc(sig("c_y_ps"), 1)

            hidden(0, 0, first=True)
            hidden(0, 1)
            output(0, 0, first=True)
            with pe.Fori(1, E // 2) as i:
                hidden(i, 0)
                output(i - 1, 1)
                hidden(i, 1)
                output(i, 0)
            output(E // 2 - 1, 1)
            pe.wait_ge(sig("c_y"), E)
            pe.wait_ge(sig("c_placeT"), 2 * E)
            for t in range(NT):
                for e in range(E):
                    last = pe.matmul(ps[:, 4 + t // 2, (t % 2) * D:(t % 2 + 1) * D], placeT[:, e, t * P:(t + 1) * P],
                                     y[:, e, :], start=(e == 0), stop=(e == E - 1))
                if t % 2:
                    last.then_inc(sig("c_back_ps"), 1)

        @block.scalar
        def _(act):
            turn_scalar(act, core, "c_y1T", y1T, 0)
            act.wait_ge(sig("c_less"), 1)
            act.activation(expl[:, :, :], tmp[:, :, :], ACT.Exp).then_inc(sig("c_expl"), 1)
            for n in range(2 * E):
                act.wait_ge(sig("c_placeT_ps"), n + 1)
                act.activation(placeT[:, n // 2, (n % 2) * HALF:(n % 2 + 1) * HALF], ps[:, 6 + n % 2, :], ACT.Copy)\
                   .then_inc(sig("c_placeT"), 1)
            norm_scalar(act, sig, "c_ln", scratch)

        @block.vector
        def _(dve):
            turn_vector(dve, core, "c_y1T", y1T, 0)
            wide = lambda a: a.unsqueeze(2).broadcast_to([P, NT, E])
            row = lambda name: core.p(name).unsqueeze(1).broadcast_to([P, NT, E])
            small = [0]

            def step(ins):
                small[0] += 1
                ins.then_inc(sig("c_small"), 1)
                dve.wait_ge(sig("c_small"), small[0])

            dve.wait_ge(sig("c_params_in"), 16)
            dve.wait_ge(sig("c_logit_ps"), 1)
            step(dve.tensor_copy(logit[:, :, :], ps[:, 4, 0:NT * E].rearrange("p (t e) -> p t e", t=NT)))
            step(dve.tensor_reduce(col[:, 2, :], logit[:, :, :], X, ALU.max))
            step(dve.tensor_tensor(pref[:, :, :], logit[:, :, :], wide(col[:, 2, :]), ALU.is_equal))
            step(dve.tensor_tensor(pref[:, :, :], pref[:, :, :], row("moe_prefer"), ALU.mult))
            step(dve.tensor_reduce(col[:, 3, :], pref[:, :, :], X, ALU.max))
            dve.tensor_tensor(oneh[:, :, :], pref[:, :, :], wide(col[:, 3, :]), ALU.is_equal).then_inc(sig("c_oneh"), 1)
            dve.tensor_tensor(tmp[:, :, :], logit[:, :, :], wide(col[:, 2, :]), ALU.subtract).then_inc(sig("c_less"), 1)
            dve.wait_ge(sig("c_expl"), 1)
            step(dve.tensor_reduce(col[:, 4, :], expl[:, :, :], X, ALU.add))
            step(dve.reciprocal(gate, col[:, 4, :]))
            dve.wait_ge(sig("c_oneh"), 1)
            step(dve.tensor_tensor(tmp[:, :, :], oneh[:, :, :], row("moe_base"), ALU.mult))
            step(dve.tensor_reduce(col[:, 5, :], tmp[:, :, :], X, ALU.add))
            dve.wait_ge(sig("c_count_ps"), 1)
            step(dve.tensor_tensor(tmp[:, :, :], ps[:, 5, 0:NT * E].rearrange("p (t e) -> p t e", t=NT),
                                   oneh[:, :, :], ALU.mult))
            step(dve.tensor_reduce(col[:, 6, :], tmp[:, :, :], X, ALU.add))
            step(dve.tensor_scalar(col[:, 7, :], col[:, 6, :], float(CAP), float(4 * E * CAP), ALU.is_gt, ALU.mult))
            step(dve.scalar_tensor_tensor(col[:, 3, :], col[:, 6, :], -1.0, col[:, 5, :], ALU.add, ALU.add))
            dve.tensor_tensor(slot, col[:, 3, :], col[:, 7, :], ALU.add).then_inc(sig("c_slot"), 1)
            dve.wait_ge(sig("c_slot"), 1)
            for t in range(NT):
                dve.tensor_scalar(place[:, t, :], core.p("moe_iota"), slot[:, t:t + 1], None, ALU.is_equal)\
                   .then_inc(sig("c_place"), 1)
            dve.wait_ge(sig("c_disp_ps"), 1)
            for k in range(KD):
                for c in range(2):
                    dve.tensor_copy(disp[:, k, c * HALF:(c + 1) * HALF], ps[:, 2 * k + c, :]).then_inc(sig("c_disp"), 1)

            b1 = core.p("moe_b1").rearrange("p (e f) -> p e f", e=E)
            b2 = core.p("moe_b2").rearrange("p (e d) -> p e d", e=E)

            def hidden(i, u, first=False):
                n = 2 * i + u
                if not first:
                    dve.wait_ge(sig("c_y_ps"), n - 1)
                for q in range(2):
                    dve.wait_ge(sig("c_hT_ps"), 2 * n + q + 1)
                    bias = b1[:, bass.ds(n, 1), 4 * q:4 * q + 4].rearrange("p a f -> p (a f)")
                    dve.tensor_tensor(hT[:, u, 4 * q:4 * q + 4, :], ps[:, q, :].rearrange("p (f n) -> p f n", f=4),
                                      bias.unsqueeze(2).broadcast_to([P, 4, CAP]), ALU.add).then_inc(sig("c_hT"), 1)

            def output(i, u):
                n = 2 * i + u
                dve.wait_ge(sig("c_y_ps"), n + 1)
                at = bass.ds(n, 1)
                dve.tensor_tensor(y[:, at, :].rearrange("p a d -> p (a d)"), ps[:, 2 + u, 0:D],
                                  b2[:, at, :].rearrange("p a d -> p (a d)"), ALU.add).then_inc(sig("c_y"), 1)

            hidden(0, 0, first=True)
            hidden(0, 1, first=True)
            output(0, 0)
            with dve.Fori(1, E // 2) as i:
                hidden(i, 0)
                output(i - 1, 1)
                hidden(i, 1)
                output(i, 0)
            output(E // 2 - 1, 1)
            for t in range(NT):
                dve.wait_ge(sig("c_back_ps"), t // 2 + 1)
                dve.scalar_tensor_tensor(y2[:, t, :], ps[:, 4 + t // 2, (t % 2) * D:(t % 2 + 1) * D], gate[:, t:t + 1],
                                         y1[:, t, :], ALU.mult, ALU.add).then_inc(sig("c_y2"), 1)
            norm_vector(dve, sig, "c_ln", scratch, y2, y2, [(sig("c_y2"), NT)], core.p("ln2_g"), core.p("ln2_b"))
            for t in range(NT):
                dve.wait_ge(sig("c_ln_shifted"), t + 1)
                dve.tensor_tensor(x[:, t, :], x[:, t, :], y2[:, t, :], ALU.add).then_inc(sig("c_x"), 1)


def phase_heads_read(core, x, drams, cstats):
    nc, sig, ps = core.nc, core.sig, core.psum
    PAIRS = H1 // 2
    SE = S + S % 2
    EVEN_QUARTERS = [(0, 402), (402, 400), (802, 400), (1202, 400)]
    ORDER = [("r", g, k) for g in range(4) for k in range(KD)] + [("v", 0, 0), ("v", 1, 0)]
    ORDER += [("k", 0, q) for q in range(4)] + [("v", c, 0) for c in range(2, 7)] + [("k", 1, q) for q in range(4)]
    FILLS = len(ORDER)
    SLOT_FILLS = [range(0, 4), range(4, 8), range(8, 10), range(10, 14),
                  range(14, 16), range(16, 18), range(18, 19), range(19, 23)]
    ROWS_END, KEYS0_END, KEYS1, VALUES_END = 8, 14, 19, 19
    T_BANK, V_BANK = 4, 7

    def fill_bank(n):
        return 7 - (n if n < KEYS1 else n - KEYS1) % 2

    def fill_before(b, n):
        if n < 2:
            return b - 1, n + 21
        return b, {KEYS1: 18, KEYS1 + 1: 17}.get(n, n - 2)

    with ExitStack() as ctx:
        params = core.load_pack(ctx, "pd")
        scratch, scratch2, scratch3 = (scratch_of(core, ctx, f"d_ln{i}") for i in range(3))
        mean = core.tensor(ctx, "d_mean", [P, B * NC])
        rstd = core.tensor(ctx, "d_rstd", [P, B * NC])
        diff = core.tensor(ctx, "d_diff", [P, B * NC])
        wk = core.tensor(ctx, "d_wk", [P, KD, D])
        wv = core.tensor(ctx, "d_wv", [P, KD, D])
        bk = core.tensor(ctx, "d_bk", [P, KD])
        bv = core.tensor(ctx, "d_bv", [P, KD])
        rowsN = core.tensor(ctx, "d_rowsN", [P, 2, NC, D])
        rowsT = core.tensor(ctx, "d_rowsT", [P, KD, SE])
        keys = core.tensor(ctx, "d_keys", [P, KD, 2, SE], F32R)
        val = core.tensor(ctx, "d_val", [P, 2, NC, D])
        moments = core.tensor(ctx, "d_rowmoments", [P, 2, 2, NC])
        QT = core.tensor(ctx, "d_QT", [P, KD, N])
        OT = core.tensor(ctx, "d_OT", [P, KD, N])
        pairq = core.tensor(ctx, "d_pairq", [P, 2, 2, KD, 4, 2, L], F32R)
        tileq = core.tensor(ctx, "d_tileq", [P, 2, KD, L])
        tileqH = core.tensor(ctx, "d_tileqH", [P, 2, 2, KD, L], F32R)
        tileqL = core.tensor(ctx, "d_tileqL", [P, 2, 2, KD, L], F32R)
        exps = core.tensor(ctx, "d_exps", [P, 2, S])
        probT = core.tensor(ctx, "d_probT", [P, 4, NC, P])
        top = core.tensor(ctx, "d_top", [P, 2, 4])
        negmax = core.tensor(ctx, "d_negmax", [P, 2])
        sums = core.tensor(ctx, "d_sums", [P, 2, 4, 4])
        total = core.tensor(ctx, "d_total", [P, 4])
        inv = core.tensor(ctx, "d_inv", [P, 4])
        invw = core.tensor(ctx, "d_invw", [P, P])
        invT = core.tensor(ctx, "d_invT", [P, P])
        on = core.tensor(ctx, "d_on", [P, P])
        even = core.tensor(ctx, "d_even", [P, L])
        fence = core.tensor(ctx, "d_fence", [P, 4])
        early = probT[:, :, :, :].rearrange("p g c n -> p (g c n)")
        nat = early[:, 0:NT * D].rearrange("p (t d) -> p t d", t=NT)
        natT = early[:, NT * D:2 * NT * D].rearrange("p (k n) -> p k n", k=KD)
        late = rowsN[:, :, :, :].rearrange("p u c d -> p (u c d)")
        nat2 = late[:, 0:NT * D].rearrange("p (t d) -> p t d", t=NT)
        res = late[:, NT * D:2 * NT * D].rearrange("p (t d) -> p t d", t=NT)
        QL = L // HD1
        mixed = probT[:, :, :, :].rearrange("p g c n -> p (g c n)")[0:B * QL, 0:H1 * D]\
            .rearrange("p (h r d) -> p h r d", h=H1, r=HD1)
        outT = OT
        block = ctx.enter_context(nc.Block())

        def mixed_pair(f):
            return mixed[:, :, 2 * f:2 * f + 2, :].rearrange("p h r d -> p r h d")

        def bank_pair(f):
            return ps[0:B * QL, f, :].rearrange("p (r h d) -> p r h d", r=2, h=H1)

        def batches(eng, one, last):
            one(0, 0)
            one(0, 1)
            with eng.Fori(1, B // 2 - 1) as i:
                one(i, 0)
                one(i, 1)
            one(B // 2 - 1, 0)
            last()

        def wait(eng, name, value):
            if not (isinstance(value, int) and value <= 0):
                eng.wait_ge(sig(name), value)

        @block.sync
        def _(sp):
            sp.dma_start(params[:, :], drams["pd"]).then_inc(sig("d_params_in"), 16)

            def load(b, u):
                sp.dma_start(rowsN[:, u, :, :], drams["ctx_rows"][bass.ds(b, 1)].rearrange("b (c p) d -> p (b c) d", p=P))\
                  .then_inc(sig(f"d_rows_in{u}"), 16)

            load(0, 0)
            load(1, 1)
            with sp.Fori(1, B // 2) as i:
                for u in range(2):
                    b = 2 * i + u
                    sp.wait_ge(sig("d_fill_ps"), FILLS * (b - 2) + ROWS_END)
                    load(b, u)
            sp.wait_ge(sig("d_mixed_a"), 4)
            sp.wait_ge(sig("d_mixed_d"), 4)
            for q in range(QL):
                sp.dma_start(drams["mixed"].rearrange("b (h q) d -> q b h d", q=QL)[q],
                             mixed[q:B * QL:QL, :, :, :].rearrange("p h r d -> p h (r d)"))\
                  .then_inc(sig("d_mixed_out"), 16)
            sp.wait_ge(sig("d_mixed_out"), 16 * QL)
            sp.dma_start(res, natural(drams["mixed"])).then_inc(sig("d_nat"), 16)

        @block.gpsimd
        def _(pool):
            def normalise(i, u, first=False):
                b = 2 * i + u
                pool.wait_ge(sig(f"d_rows_in{u}"), 16 * i + 16)
                if not first:
                    pool.wait_ge(sig("d_fill_ps"), FILLS * (b - 2) + ROWS_END)
                pool.tensor_tensor(fence[:, 0:1], mean[:, 0:1], mean[:, 0:1], ALU.add)
                for n, src in enumerate((mean, rstd)):
                    last = pool.tensor_copy(moments[:, u, n, :], src[:, bass.ds(b * NC, NC)])
                last.then_inc(sig("d_moments"), 1)
                pool.wait_ge(sig("d_moments"), b + 1)
                pool.tensor_tensor(fence[:, 1:2], mean[:, 0:1], mean[:, 0:1], ALU.add)
                for c in range(NC):
                    pool.tensor_scalar(rowsN[:, u, c, :], rowsN[:, u, c, :], moments[:, u, 0, c:c + 1],
                                       moments[:, u, 1, c:c + 1], ALU.subtract, ALU.mult).then_inc(sig("d_normed"), 1)

            def spread_queries(i, u, first=False):
                b = 2 * i + u
                if not first:
                    pool.wait_ge(sig("d_s_ps"), 4 * PAIRS * (b - 1))
                wait(pool, "d_pairq", b)
                pool.wait_ge(sig("d_tileq"), b + 1)
                pool.tensor_tensor(fence[:, 2:3], mean[:, 0:1], mean[:, 0:1], ALU.add)
                mask = core.p("head_mask").rearrange("p (a c) -> p a c", a=2)
                for part, q in enumerate((tileqH, tileqL)):
                    out = pairq[:, u, part, :, :, :, :].rearrange("p m g r q -> p m (g r) q")
                    for m in range(KD):
                        for a in range(2):
                            last = pool.tensor_tensor(out[:, m, 4 * a:4 * a + 4, :],
                                                      q[:, u, a, m, :].bitcast(F32).unsqueeze(1).broadcast_to([P, 4, L]),
                                                      mask[:, a, :].unsqueeze(2).broadcast_to([P, 4, L]), ALU.mult)
                last.then_inc(sig("d_pairq"), 1)

            pool.wait_ge(sig("d_rstd"), 1)
            normalise(0, 0, first=True)
            normalise(0, 1, first=True)
            spread_queries(0, 0, first=True)
            spread_queries(0, 1, first=True)
            with pool.Fori(1, B // 2) as i:
                for u in range(2):
                    normalise(i, u)
                    spread_queries(i, u)

        @block.tensor
        def _(pe):
            pe.wait_ge(sig("d_params_in"), 16)
            for w, col in (("l1_wk", 0), ("l1_wv", 2)):
                for m in range(KD):
                    for k in range(KD):
                        last = pe.matmul(ps[:, V_BANK, col + m:col + m + 1], core.w(w)[:, k, m * P:(m + 1) * P],
                                         core.p("n_bcol")[:, k:k + 1], start=(k == 0), stop=(k == KD - 1))
            last.then_inc(sig("d_shift_ps"), 1)

            def taken(b, n):
                wait(pe, "d_fill", FILLS * b + n + 1)
                kind, m, q = ORDER[n]
                if kind == "k":
                    wait(pe, "d_lows", 8 * b + 4 * m + q + 1)

            def fill(i, u, n):
                b = 2 * i + u
                bank = fill_bank(n)
                kind, j, q = ORDER[n]
                taken(*fill_before(b, n))
                if n == 0:
                    wait(pe, "d_weighed", 2 * (b - 1))
                elif n == KEYS0_END:
                    wait(pe, "d_weighed", 2 * (b - 1) + 1)
                if kind == "r":
                    for c in range(4 * j, min(4 * j + 4, NC)):
                        w = P if c < NC - 1 else SL + S % 2
                        if q == 0:
                            wait(pe, "d_normed", NC * b + c + 1)
                        last = pe.transpose(ps[:, bank, (c % 4) * P:(c % 4) * P + w],
                                            rowsN[0:w, u, c, q * P:(q + 1) * P], core.p("ident")[0:w, 0:w])
                elif kind == "k":
                    s0, w = EVEN_QUARTERS[q]
                    if n == KEYS0_END - 4:
                        wait(pe, "d_fill", FILLS * b + ROWS_END)
                    for k in range(KD):
                        last = pe.matmul(ps[:, bank, 0:w], wk[:, k, j * P:(j + 1) * P], rowsT[:, k, s0:s0 + w],
                                         start=(k == 0), stop=(k == KD - 1))
                else:
                    if j == 0:
                        wait(pe, "d_fill", FILLS * b + ROWS_END)
                    for c in range(2 * j, min(2 * j + 2, NC)):
                        w = P if c < NC - 1 else SL
                        for k in range(KD):
                            last = pe.matmul(ps[0:w, bank, (c % 2) * D:(c % 2 + 1) * D], rowsT[:, k, c * P:c * P + w],
                                             wv[:, k, :], start=(k == 0), stop=(k == KD - 1))
                last.then_inc(sig("d_fill_ps"), 1)

            def score(i, u, p):
                b = 2 * i + u
                n = PAIRS * b + p
                m, g = p // 4, p % 4
                if p == 0:
                    wait(pe, "d_pairq", b + 1)
                if g == 0:
                    wait(pe, "d_lows", 8 * b + 4 * m + 4)
                for c, (s0, w) in enumerate(EVEN_QUARTERS):
                    wait(pe, "d_exps", 4 * n + c - 3)
                    for part in range(2):
                        last = pe.matmul(ps[:, c, 0:w], pairq[:, u, part, m, g, :, :], keys[:, m, g // 2, s0:s0 + w],
                                         start=(part == 0), stop=(part == 1))
                    last.then_inc(sig("d_s_ps"), 1)

            def turn(i, u, p, t):
                n = PAIRS * (2 * i + u) + p
                if t == 0:
                    wait(pe, "d_exps", 4 * n + 4)
                wait(pe, "d_probT", 4 * n + t - 1)
                for c in range(4 * t, min(4 * t + 4, NC)):
                    w = P if c < NC - 1 else SL
                    last = pe.transpose(ps[0:w, T_BANK + t % 2, (c % 4) * P:(c % 4 + 1) * P],
                                        exps[:, p % 2, c * P:c * P + w], core.p("ident"))
                last.then_inc(sig("d_probT_ps"), 1)

            def weigh(i, u, m, fills):
                b = 2 * i + u
                quad = 2 * b + m
                wait(pe, "d_probT", 4 * PAIRS * b + 16 * m + 16)
                wait(pe, "d_fill", FILLS * b + VALUES_END)
                taken(*((b + 1, (KEYS0_END - 2, FILLS - 2)[m]) if fills else (b, FILLS - 2)))
                wait(pe, "d_weighed", quad)
                for c in range(NC):
                    w = P if c < NC - 1 else SL
                    for g in range(4):
                        f = m * P + 32 * g
                        last = pe.matmul(ps[32 * g:32 * g + 32, V_BANK, m * P:(m + 1) * P], val[0:w, u, c, f:f + 32],
                                         probT[0:w, g, c, :], start=(c == 0), stop=(c == NC - 1),
                                         tile_position=(0, 32 * g))
                last.then_inc(sig("d_weigh_ps"), 1)
                wait(pe, "d_invw", quad + 1)
                pe.matmul(ps[:, V_BANK, 2 * P + m * P:3 * P + m * P], invw[:, :], core.p("ident"), start=True,
                          stop=True).then_inc(sig("d_invT_ps"), 1)

            def batch(i, u, fills=True):
                nxt = (i, 1) if u == 0 else (i + 1, 0)
                for p in range(PAIRS):
                    if p + 1 < PAIRS:
                        score(i, u, p + 1)
                    elif fills:
                        score(*nxt, 0)
                    these = list(SLOT_FILLS[p]) if fills else []
                    for t in range(4):
                        turn(i, u, p, t)
                        if t < len(these):
                            fill(*nxt, these[t])
                    if p % 4 == 3:
                        weigh(i, u, p // 4, fills)

            pe.wait_ge(sig("d_weights"), 4)
            pe.wait_ge(sig("d_shift"), 2)
            for n in range(FILLS):
                fill(0, 0, n)
            turn_tensor(pe, core, "d_natT", nat, 0, [(sig("d_ln1_shifted"), True)])
            project_tensor(pe, core, "d_QT", core.w("l1_wq"), natT, 0, "d_natT", ready=both(sig, "d_natT"))
            for s, n in both(sig, "d_QT"):
                pe.wait_ge(s, n)
            score(0, 0, 0)
            batches(pe, batch, lambda: batch(B // 2 - 1, 1, fills=False))
            pe.wait_ge(sig("d_out"), 2)
            for r in range(HD1):
                for m in range(KD):
                    last = pe.transpose(ps[0:B * QL, r // 2, (r % 2) * D + m * P:(r % 2) * D + (m + 1) * P],
                                        OT[:, m, r:N:HD1], core.p("ident"))
                if r % 2:
                    last.then_inc(sig("d_mixed_ps"), 1)
            turn_tensor(pe, core, "d_outT", nat2, 4, [(sig("d_ln2_shifted"), True)])
            rows_tensor(pe, core, "d_proj", outT, core.w("l1_wo"), 0, both(sig, "d_outT"))

        @block.scalar
        def _(act):
            act.wait_ge(sig("d_rowvar"), 1)
            act.activation(diff[:, :], rstd[:, :], ACT.Sqrt).then_inc(sig("d_rowstd"), 1)
            norm_scalar(act, sig, "d_ln0", scratch)
            norm_scalar(act, sig, "d_ln1", scratch2)

            def take_fill(i, u, n):
                b = 2 * i + u
                bank = fill_bank(n)
                kind, j, q = ORDER[n]
                wait(act, "d_fill_ps", FILLS * b + n + 1)
                if kind == "r":
                    w = min(4 * P, SE - 4 * P * j)
                    act.activation(rowsT[:, q, 4 * P * j:4 * P * j + w], ps[:, bank, 0:w], ACT.Copy)\
                       .then_inc(sig("d_fill"), 1)
                elif kind == "k":
                    s0, w = EVEN_QUARTERS[q]
                    for half in range(2):
                        r = slice(64 * half, 64 * half + 64)
                        last = act.activation(keys[r, j, half, s0:s0 + w], ps[r, bank, 0:w], ACT.Identity,
                                              bias=bk[r, j:j + 1])
                    last.then_inc(sig("d_fill"), 1)
                else:
                    c = 2 * j
                    if c + 1 < NC:
                        act.activation(val[:, u, c:c + 2, :], two(ps[:, bank, :]), ACT.Copy).then_inc(sig("d_fill"), 1)
                    else:
                        act.activation(val[0:SL, u, c, :], ps[0:SL, bank, 0:D], ACT.Copy).then_inc(sig("d_fill"), 1)

            def exp(i, u, p, c):
                n = PAIRS * (2 * i + u) + p
                s0, w = EVEN_QUARTERS[c]
                w = min(w, S - s0)
                if c == 0:
                    wait(act, "d_negmax", n + 1)
                    wait(act, "d_probT_ps", 4 * (n - 1))
                act.activation(exps[:, p % 2, s0:s0 + w], ps[:, c, 0:w], ACT.Exp, bias=negmax[:, p % 2:p % 2 + 1],
                               accum_out=sums[:, p // 4, p % 4, c:c + 1]).then_inc(sig("d_exps"), 1)

            def batch(i, u, fills=True):
                nxt = (i, 1) if u == 0 else (i + 1, 0)
                for p in range(PAIRS):
                    these = list(SLOT_FILLS[p]) if fills else []
                    for t in range(4):
                        if p + 1 < PAIRS:
                            exp(i, u, p + 1, t)
                        elif fills:
                            exp(*nxt, 0, t)
                        if t < len(these):
                            take_fill(*nxt, these[t])

            for n in range(FILLS):
                if n == ROWS_END:
                    act.wait_ge(sig("d_shift"), 2)
                take_fill(0, 0, n)
            turn_scalar(act, core, "d_natT", natT, 0)
            project_scalar(act, core, "d_QT", QT, 0, core.p("l1_bq"))
            for c in range(4):
                exp(0, 0, 0, c)
            batches(act, batch, lambda: batch(B // 2 - 1, 1, fills=False))
            for f in range(0, HD1 // 2, 2):
                act.wait_ge(sig("d_mixed_ps"), f + 1)
                act.activation(mixed_pair(f), bank_pair(f), ACT.Copy).then_inc(sig("d_mixed_a"), 1)
            norm_scalar(act, sig, "d_ln2", scratch3)
            turn_scalar(act, core, "d_outT", outT, 4)

        @block.vector
        def _(dve):
            m_even, m_odd, v_even, v_odd = (cstats[:, :, j] for j in (1, 4, 2, 5))
            small = [0]

            def step(ins):
                small[0] += 1
                ins.then_inc(sig("d_small"), 1)
                dve.wait_ge(sig("d_small"), small[0])

            step(dve.tensor_tensor(mean[:, :], m_even, m_odd, ALU.add))
            step(dve.tensor_tensor(diff[:, :], m_even, m_odd, ALU.subtract))
            step(dve.tensor_scalar(mean[:, :], mean[:, :], 0.5, None, ALU.mult))
            step(dve.tensor_tensor(diff[:, :], diff[:, :], diff[:, :], ALU.mult))
            step(dve.tensor_tensor(rstd[:, :], v_even, v_odd, ALU.add))
            step(dve.tensor_scalar(diff[:, :], diff[:, :], 0.25, EPS, ALU.mult, ALU.add))
            dve.scalar_tensor_tensor(rstd[:, :], rstd[:, :], 1.0 / D, diff[:, :], ALU.mult, ALU.add)\
               .then_inc(sig("d_rowvar"), 1)
            dve.wait_ge(sig("d_rowstd"), 1)
            dve.reciprocal(rstd[:, :], diff[:, :]).then_inc(sig("d_rstd"), 1)
            dve.wait_ge(sig("d_params_in"), 16)
            for dst, w in ((wk, "l1_wk"), (wv, "l1_wv")):
                for k in range(KD):
                    dve.tensor_scalar(dst[:, k, :], core.w(w)[:, k, :], core.p("n_wcol")[:, k:k + 1], None, ALU.mult)\
                       .then_inc(sig("d_weights"), 1)
            dve.wait_ge(sig("d_shift_ps"), 1)
            dve.tensor_tensor(bk[:, :], ps[:, V_BANK, 0:2], core.p("l1_bk"), ALU.add).then_inc(sig("d_shift"), 1)
            dve.tensor_tensor(bv[:, :], ps[:, V_BANK, 2:4], core.p("l1_bv"), ALU.add).then_inc(sig("d_shift"), 1)
            norm_vector(dve, sig, "d_ln0", scratch, x, nat)
            norm_vector(dve, sig, "d_ln1", scratch2, nat, nat, [(sig("d_ln0_out"), NT)], core.p("n_wrow"),
                        core.p("n_brow"))

            def top_of(i, u, p):
                n = PAIRS * (2 * i + u) + p
                for c, (s0, w) in enumerate(EVEN_QUARTERS):
                    w = min(w, S - s0)
                    wait(dve, "d_s_ps", 4 * n + c + 1)
                    dve.tensor_reduce(top[:, p % 2, c:c + 1], ps[:, c, 0:w], X, ALU.max).then_inc(sig("d_top"), 1)
                wait(dve, "d_top", 4 * n + 4)
                wait(dve, "d_exps", 4 * (n - 1))
                dve.tensor_reduce(negmax[:, p % 2:p % 2 + 1], top[:, p % 2, :], X, ALU.max, negate=True)\
                   .then_inc(sig("d_negmax"), 1)

            def take_turn(i, u, p, t):
                n = PAIRS * (2 * i + u) + p
                if t == 0 and p % 4 == 0:
                    wait(dve, "d_weigh_ps", 2 * (2 * i + u) + p // 4)
                wait(dve, "d_probT_ps", 4 * n + t + 1)
                g = p % 4
                if t < 3:
                    dve.tensor_copy(probT[:, g, 4 * t:4 * t + 4, :],
                                    ps[:, T_BANK + t % 2, :].rearrange("p (c n) -> p c n", c=4)).then_inc(sig("d_probT"), 1)
                else:
                    dve.tensor_copy(probT[0:SL, g, NC - 1, :], ps[0:SL, T_BANK + 1, 0:P]).then_inc(sig("d_probT"), 1)

            def take_lows(i, u, m, q):
                b = 2 * i + u
                n = ORDER.index(("k", m, q))
                bank = fill_bank(n)
                s0, w = EVEN_QUARTERS[q]
                wait(dve, "d_fill", FILLS * b + n + 1)
                for half in range(2):
                    r, o = slice(64 * half, 64 * half + 64), slice(64 - 64 * half, 128 - 64 * half)
                    last = dve.scalar_tensor_tensor(keys[o, m, half, s0:s0 + w], ps[r, bank, 0:w], bk[r, m:m + 1],
                                                    keys[r, m, half, s0:s0 + w].bitcast(F32), ALU.add, ALU.subtract)
                last.then_inc(sig("d_lows"), 1)

            def tile_queries(i, u):
                b = 2 * i + u
                wait(dve, "d_pairq", b - 1)
                wait(dve, "d_tileq", b)
                cols = bass.ds(b * L, L)
                for a in range(2):
                    src = slice(64 * a, 64 * a + 64)
                    for o in (slice(0, 64), slice(64, 128)):
                        dve.tensor_copy(tileq[o, a, :, :], QT[src, :, cols]).then_inc(sig("d_tileq_whole"), 1)
                wait(dve, "d_tileq_whole", 4 * b + 4)
                dve.tensor_copy(tileqH[:, u, :, :, :], tileq[:, :, :, :]).then_inc(sig("d_tileqH"), 1)
                wait(dve, "d_tileqH", b + 1)
                dve.tensor_tensor(tileqL[:, u, :, :, :], tileq[:, :, :, :], tileqH[:, u, :, :, :].bitcast(F32),
                                  ALU.subtract).then_inc(sig("d_tileq"), 1)

            def inverses(i, u, m):
                quad = 2 * (2 * i + u) + m
                wait(dve, "d_exps", 4 * PAIRS * (2 * i + u) + 16 * m + 16)
                dve.tensor_reduce(total[:, :], sums[:, m, :, :], X, ALU.add).then_inc(sig("d_total"), 1)
                wait(dve, "d_total", quad + 1)
                dve.reciprocal(inv[:, :], total[:, :]).then_inc(sig("d_inv"), 1)
                wait(dve, "d_inv", quad + 1)
                dve.tensor_copy(invw[:, :].rearrange("p (g n) -> p g n", g=4),
                                inv[:, :].unsqueeze(2).broadcast_to([P, 4, 32])).then_inc(sig("d_invw"), 1)

            def take_heads(i, u, m):
                b = 2 * i + u
                quad = 2 * b + m
                wait(dve, "d_invT_ps", quad + 1)
                dve.tensor_copy(invT[:, :], ps[:, V_BANK, 2 * P + m * P:3 * P + m * P]).then_inc(sig("d_invT"), 1)
                wait(dve, "d_invT", quad + 1)
                dve.tensor_tensor(on[:, :], ps[:, V_BANK, m * P:(m + 1) * P], invT[:, :], ALU.mult)\
                   .then_inc(sig("d_weighed"), 1)
                wait(dve, "d_weighed", quad + 1)
                dve.tensor_scalar(even[:, :], on[:, 0:L], core.p("parity")[:, 0:1], None, ALU.mult)\
                   .then_inc(sig("d_even"), 1)
                wait(dve, "d_even", quad + 1)
                dve.scalar_tensor_tensor(OT[:, m, bass.ds(b * L, L)], on[:, L:2 * L], core.p("parity")[:, 1:2],
                                         even[:, :], ALU.mult, ALU.add).then_inc(sig("d_OT"), 1)

            def batch(i, u, fills=True):
                nxt = (i, 1) if u == 0 else (i + 1, 0)
                for p in range(PAIRS):
                    if p + 1 < PAIRS:
                        top_of(i, u, p + 1)
                    elif fills:
                        top_of(*nxt, 0)
                    if p % 4 == 3:
                        inverses(i, u, p // 4)
                    for t in range(4):
                        take_turn(i, u, p, t)
                        if p % 4 == 3 and fills:
                            take_lows(*nxt, p // 4, t)
                    if p % 4 == 3:
                        take_heads(i, u, p // 4)
                    if p == 4 and not (isinstance(i, int) and i + 1 == B // 2):
                        tile_queries(i + 1, u)

            for m in range(KD):
                for q in range(4):
                    take_lows(0, 0, m, q)
            turn_vector(dve, core, "d_natT", natT, 0)
            project_vector(dve, core, "d_QT", QT, 0, core.p("l1_bq"))
            for s, n in both(sig, "d_QT"):
                dve.wait_ge(s, n)
            tile_queries(0, 0)
            tile_queries(0, 1)
            top_of(0, 0, 0)
            batches(dve, batch, lambda: batch(B // 2 - 1, 1, fills=False))
            dve.wait_ge(sig("d_OT"), 2 * B)
            for m in range(KD):
                dve.scalar_tensor_tensor(OT[:, m, :], OT[:, m, :], bv[:, m:m + 1], QT[:, m, :], ALU.add, ALU.add)\
                   .then_inc(sig("d_out"), 1)
            for f in range(1, HD1 // 2, 2):
                dve.wait_ge(sig("d_mixed_ps"), f + 1)
                dve.tensor_copy(mixed_pair(f), bank_pair(f)).then_inc(sig("d_mixed_d"), 1)
            norm_vector(dve, sig, "d_ln2", scratch3, res, nat2, [(sig("d_nat"), 16)], core.p("n1_w"), core.p("n1_b"))
            turn_vector(dve, core, "d_outT", outT, 4)
            for t in range(NT):
                dve.tensor_tensor(res[:, t, :], res[:, t, :], core.p("l1_bo"), ALU.add).then_inc(sig("d_res"), 1)
            for i in range(NT // 2):
                dve.wait_ge(sig("d_proj_ps"), i + 1)
                dve.wait_ge(sig("d_res"), 2 * i + 2)
                dve.tensor_tensor(res[:, 2 * i:2 * i + 2, :], two(ps[:, i, :]), res[:, 2 * i:2 * i + 2, :], ALU.add)\
                   .then_inc(sig("d_sum"), 1)
                dve.wait_ge(sig("d_sum"), i + 1)
                dve.tensor_tensor(x[:, 2 * i:2 * i + 2, :], x[:, 2 * i:2 * i + 2, :], res[:, 2 * i:2 * i + 2, :], ALU.add)\
                   .then_inc(sig("d_x"), 1)


def phase_features(core, x, drams):
    nc, sig, ps = core.nc, core.sig, core.psum
    with ExitStack() as ctx:
        params = core.load_pack(ctx, "pe")
        scratch = scratch_of(core, ctx, "e_ln")
        xn = core.tensor(ctx, "e_xn", [P, NT, D])
        xnT = core.tensor(ctx, "e_xnT", [P, KD, N])
        sqT = core.tensor(ctx, "e_sqT", [P, KD, N])
        wsqT = core.tensor(ctx, "e_wsqT", [P, KD, D])
        gw = core.tensor(ctx, "e_gw", [P, KD, D])
        half = core.tensor(ctx, "e_half", [P, D])
        amp = core.tensor(ctx, "e_amp", [P, 2, KD])
        feats = core.tensor(ctx, "e_feats", [P, KD, N])
        wfeats = core.tensor(ctx, "e_wfeats", [P, KD, D])
        block = ctx.enter_context(nc.Block())

        @block.sync
        def _(sp):
            sp.dma_start(params[:, :], drams["pe"]).then_inc(sig("e_params_in"), 16)

        def exponent(pe, bank, m, rhs, square, width):
            for k in range(KD):
                pe.matmul(ps[:, bank, 0:width], gw[:, k, m * P:(m + 1) * P], rhs[:, k], start=(k == 0), stop=False)
            for k in range(KD):
                last = pe.matmul(ps[:, bank, 0:width], half[:, m * P:(m + 1) * P], square[:, k], start=False,
                                 stop=(k == KD - 1))
            return last

        @block.tensor
        def _(pe):
            pe.wait_ge(sig("e_gw"), KD)
            pe.wait_ge(sig("e_half"), 1)
            pe.wait_ge(sig("e_wsqT"), 1)
            for m in range(KD):
                exponent(pe, 4 + m, m, core.w("rf_iwT"), wsqT, D).then_inc(sig("e_wexp_ps"), 1)
            turn_tensor(pe, core, "e_xnT", xn, 0, [(sig("e_ln_out"), True)])
            pe.wait_ge(sig("e_wfeats_raw"), KD)
            for c in range(2):
                for s, n in both(sig, "e_xnT", c + 1):
                    pe.wait_ge(s, n)
                pe.wait_ge(sig("e_sqT"), c + 1)
                cols = slice(c * HALF, (c + 1) * HALF)
                for m in range(KD):
                    exponent(pe, 4 + 2 * c + m, m, xnT[:, :, cols], sqT[:, :, cols], HALF).then_inc(sig("e_exp_ps"), 1)
            pe.wait_ge(sig("e_wfeats"), KD)
            rows_tensor(pe, core, "e_out", feats, wfeats, 0, [(sig("e_feats"), 4)])

        @block.scalar
        def _(act):
            norm_scalar(act, sig, "e_ln", scratch)
            act.wait_ge(sig("e_params_in"), 16)
            act.activation(amp[:, 0, :], core.p("rf_abcol"), ACT.Exp).then_inc(sig("e_amp"), 1)
            for m in range(KD):
                act.wait_ge(sig("e_wexp_ps"), m + 1)
                act.activation(wfeats[:, m, :], ps[:, 4 + m, 0:D], ACT.Exp).then_inc(sig("e_wfeats_raw"), 1)
            turn_scalar(act, core, "e_xnT", xnT, 0)
            for i in range(4):
                act.wait_ge(sig("e_exp_ps"), i + 1)
                act.activation(feats[:, i % 2, (i // 2) * HALF:(i // 2 + 1) * HALF], ps[:, 4 + i, :], ACT.Exp)\
                   .then_inc(sig("e_feats_raw"), 1)

        @block.vector
        def _(dve):
            dve.wait_ge(sig("e_params_in"), 16)
            ab = core.p("rf_ab")
            dve.tensor_tensor(half[:, :], ab, ab, ALU.mult).then_inc(sig("e_absq"), 1)
            dve.wait_ge(sig("e_absq"), 1)
            dve.tensor_scalar(half[:, :], half[:, :], -0.5, None, ALU.mult).then_inc(sig("e_half"), 1)
            for k in range(KD):
                dve.tensor_tensor(gw[:, k, :], core.w("rf_gsT")[:, k, :], ab, ALU.mult).then_inc(sig("e_gw"), 1)
            dve.tensor_tensor(wsqT[:, :, :], core.w("rf_iwT"), core.w("rf_iwT"), ALU.mult).then_inc(sig("e_wsqT"), 1)
            norm_vector(dve, sig, "e_ln", scratch, x, xn)
            dve.wait_ge(sig("e_amp"), 1)
            dve.tensor_scalar(amp[:, 1, :], amp[:, 0, :], 256.0 ** -0.5, None, ALU.mult).then_inc(sig("e_amp2"), 1)
            dve.wait_ge(sig("e_amp2"), 1)
            for m in range(KD):
                dve.wait_ge(sig("e_wfeats_raw"), m + 1)
                dve.tensor_scalar(wfeats[:, m, :], wfeats[:, m, :], amp[:, 1, m:m + 1], None, ALU.mult)\
                   .then_inc(sig("e_wfeats"), 1)
            turn_vector(dve, core, "e_xnT", xnT, 0)
            for c in range(2):
                for s, n in both(sig, "e_xnT", c + 1):
                    dve.wait_ge(s, n)
                cols = slice(c * HALF, (c + 1) * HALF)
                dve.tensor_tensor(sqT[:, :, cols], xnT[:, :, cols], xnT[:, :, cols], ALU.mult).then_inc(sig("e_sqT"), 1)
            for i in range(4):
                cols = slice((i // 2) * HALF, (i // 2 + 1) * HALF)
                dve.wait_ge(sig("e_feats_raw"), i + 1)
                dve.tensor_scalar(feats[:, i % 2, cols], feats[:, i % 2, cols], amp[:, 1, i % 2:i % 2 + 1], None,
                                  ALU.mult).then_inc(sig("e_feats"), 1)
            for i in range(NT // 2):
                dve.wait_ge(sig("e_out_ps"), i + 1)
                dve.tensor_tensor(x[:, 2 * i:2 * i + 2, :], x[:, 2 * i:2 * i + 2, :], two(ps[:, i, :]), ALU.add)\
                   .then_inc(sig("e_x"), 1)


def phase_trees(core, x, drams):
    nc, sig, ps = core.nc, core.sig, core.psum
    HC = 8
    with ExitStack() as ctx:
        params = core.load_pack(ctx, "pf")
        scratch = scratch_of(core, ctx, "f_ln")
        xn = core.tensor(ctx, "f_xn", [P, NT, D])
        xnT = core.tensor(ctx, "f_xnT", [P, KD, N])
        right = core.tensor(ctx, "f_right", [P, NT, TREES, NNODE])
        levels = [core.tensor(ctx, f"f_level{d}", [P, NT, TREES, 2 ** d]) for d in range(1, DEPTH + 1)]
        leaf = levels[-1]
        leafT = core.tensor(ctx, "f_leafT", [NLEAF, TREES, N])
        leafB = core.tensor(ctx, "f_leafB", [NLEAF, TREES, N], BF16)
        member = core.tensor(ctx, "f_member", [NLEAF, HC, P], BF16)
        hid = core.tensor(ctx, "f_hid", [P, 2, HALF])
        own = core.tensor(ctx, "f_own", [P, 2, HALF])
        outT = core.tensor(ctx, "f_outT", [P, TREES, KD, N])
        val = core.tensor(ctx, "f_val", [P, NT, D])
        s = core.tensor(ctx, "f_s", [P, 2, 4, P])
        s1 = core.tensor(ctx, "f_s1", [P, 2, 4, P])
        prob = core.tensor(ctx, "f_prob", [P, 2, 4, P])
        probT = core.tensor(ctx, "f_probT", [P, NT, P])
        negmax = core.tensor(ctx, "f_negmax", [P, NT])
        total = core.tensor(ctx, "f_total", [P, NT])
        inv = core.tensor(ctx, "f_inv", [P, NT])
        w1 = core.p("ff_w1").rearrange("p (j k n) -> p j k n", j=TREES, k=KD)
        w2 = core.p("ff_w2").rearrange("p (j c d) -> p j c d", j=TREES, c=HC)
        b1 = core.p("ff_b1").rearrange("p (j c) -> p j c", j=TREES)
        b2 = core.p("ff_b2").rearrange("p (j d) -> p j d", j=TREES)
        NN = TREES * NNODE
        work = [(j, c, h) for j in range(TREES) for c in range(2) for h in range(HC)]
        block = ctx.enter_context(nc.Block())

        @block.sync
        def _(sp):
            sp.dma_start(params[:, :], drams["pf"]).then_inc(sig("f_params_in"), 16)

        @block.tensor
        def _(pe):
            pe.wait_ge(sig("f_params_in"), 16)
            turn_tensor(pe, core, "f_xnT", xn, 0, [(sig("f_ln_out"), True)])
            for c in range(2):
                for sm, n in both(sig, "f_xnT", c + 1):
                    pe.wait_ge(sm, n)
                for t in range(4 * c, 4 * c + 4):
                    for k in range(KD):
                        last = pe.matmul(ps[:, 4, t * NN:(t + 1) * NN], xnT[:, k, t * P:(t + 1) * P],
                                         core.w("ff_nodes")[:, k, :], start=(k == 0), stop=(k == KD - 1))
            last.then_inc(sig("f_node_ps"), 1)
            pe.wait_ge(sig("f_leaf"), 1)
            for j in range(TREES):
                for c in range(2):
                    n = 2 * j + c
                    if n >= 2:
                        pe.wait_ge(sig("f_leafT"), n - 1)
                    for q in range(4):
                        last = pe.transpose(ps[0:NLEAF, 5 + n % 2, q * P:(q + 1) * P], leaf[:, 4 * c + q, j, :],
                                            core.p("ident"))
                    last.then_inc(sig("f_leafT_ps"), 1)
            pe.wait_ge(sig("f_leafT"), 2 * TREES)
            pe.wait_ge(sig("f_leafB"), 2 * TREES)
            pe.wait_ge(sig("f_member"), 1)

            def first(n):
                j, c, h = work[n]
                cols = slice(c * HALF, (c + 1) * HALF)
                if n >= 2:
                    pe.wait_ge(sig("f_hid"), n - 1)
                    pe.wait_ge(sig("f_own"), n - 1)
                for k in range(KD):
                    last = pe.matmul(ps[:, n % 2, :], w1[:, j, k, h * P:(h + 1) * P], xnT[:, k, cols],
                                     start=(k == 0), stop=(k == KD - 1))
                last.then_inc(sig("f_hid_ps"), 1)
                pe.matmul(ps[:, 2 + n % 2, :], member[:, h, :], leafB[:, j, cols], start=True, stop=True)\
                  .then_inc(sig("f_mask_ps"), 1)

            def second(n):
                j, c, h = work[n]
                cols = slice(c * HALF, (c + 1) * HALF)
                if h == 0:
                    if j:
                        pe.wait_ge(sig("f_outT"), 2 * (2 * (j - 1) + c) + 2)
                    for m in range(KD):
                        pe.matmul(ps[:, 4 + 2 * c + m, :], b2[0:NLEAF, j, m * P:(m + 1) * P], leafT[:, j, cols],
                                  start=True, stop=False)
                pe.wait_ge(sig("f_own"), n + 1)
                for m in range(KD):
                    last = pe.matmul(ps[:, 4 + 2 * c + m, :], w2[:, j, h, m * P:(m + 1) * P], own[:, n % 2, :],
                                     start=False, stop=(h == HC - 1))
                last.then_inc(sig("f_second_ps"), 1)

            first(0)
            for n in range(len(work)):
                if n + 1 < len(work):
                    first(n + 1)
                second(n)
            pe.wait_ge(sig("f_outT"), 4 * TREES)
            for t in range(NT):
                for m in range(KD):
                    last = pe.transpose(ps[:, t // 2, (t % 2) * D + m * P:(t % 2) * D + (m + 1) * P],
                                        outT[:, 2, m, t * P:(t + 1) * P], core.p("ident"))
                if t % 2:
                    last.then_inc(sig("f_val_ps"), 1)
            for t in range(NT):
                for m in range(KD):
                    last = pe.matmul(ps[:, 4 + t // 4, (t % 4) * P:(t % 4 + 1) * P], outT[:, 0, m, t * P:(t + 1) * P],
                                     outT[:, 1, m, t * P:(t + 1) * P], start=(m == 0), stop=(m == KD - 1))
                if t % 4 == 3:
                    last.then_inc(sig("f_s_ps"), 1)
            for i in range(2):
                pe.wait_ge(sig("f_prob"), i + 1)
                for q in range(4):
                    last = pe.transpose(ps[:, 6 + i, q * P:(q + 1) * P], prob[:, i, q, :], core.p("ident"))
                last.then_inc(sig("f_probT_ps"), 1)
            pe.wait_ge(sig("f_val"), NT // 2)
            for t in range(NT):
                pe.wait_ge(sig("f_probT"), t // 4 + 1)
                last = pe.matmul(ps[:, t // 2, (t % 2) * D:(t % 2 + 1) * D], probT[:, t, :], val[:, t, :],
                                 start=True, stop=True)
                if t % 2:
                    last.then_inc(sig("f_out_ps"), 1)

        @block.scalar
        def _(act):
            act.wait_ge(sig("f_params_in"), 16)
            act.activation(member[:, :, :], core.p("ff_leaf")[0:NLEAF, :].rearrange("p (c n) -> p c n", c=HC), ACT.Copy)\
               .then_inc(sig("f_member"), 1)
            norm_scalar(act, sig, "f_ln", scratch)
            turn_scalar(act, core, "f_xnT", xnT, 0)
            for j in range(TREES):
                for c in range(2):
                    cols = slice(c * HALF, (c + 1) * HALF)
                    act.wait_ge(sig("f_leafT"), 2 * j + c + 1)
                    act.activation(leafB[:, j, cols], leafT[:, j, cols], ACT.Copy).then_inc(sig("f_leafB"), 1)
            for n, (j, c, h) in enumerate(work):
                act.wait_ge(sig("f_hid_ps"), n + 1)
                if n >= 2:
                    act.wait_ge(sig("f_own"), n - 1)
                act.activation(hid[:, n % 2, :], ps[:, n % 2, :], ACT.Relu, bias=b1[:, j, h:h + 1])\
                   .then_inc(sig("f_hid"), 1)
                if h == HC - 1:
                    act.wait_ge(sig("f_second_ps"), n + 1)
                    for m in range(KD):
                        act.activation(outT[:, j, m, c * HALF:(c + 1) * HALF], ps[:, 4 + 2 * c + m, :], ACT.Copy)\
                           .then_inc(sig("f_outT"), 1)
            for i in range(NT // 2):
                act.wait_ge(sig("f_val_ps"), i + 1)
                act.activation(val[:, 2 * i:2 * i + 2, :], two(ps[:, i, :]), ACT.Copy).then_inc(sig("f_val"), 1)
            for i in range(2):
                act.wait_ge(sig("f_s1"), i + 1)
                act.activation(s[:, i, :, :], s1[:, i, :, :], ACT.Exp).then_inc(sig("f_exp"), 1)
            for i in range(2):
                act.wait_ge(sig("f_probT_ps"), i + 1)
                act.activation(probT[:, 4 * i:4 * i + 4, :], ps[:, 6 + i, :], ACT.Copy).then_inc(sig("f_probT"), 1)

        @block.vector
        def _(dve):
            norm_vector(dve, sig, "f_ln", scratch, x, xn)
            turn_vector(dve, core, "f_xnT", xnT, 0)
            dve.wait_ge(sig("f_params_in"), 16)
            dve.wait_ge(sig("f_node_ps"), 1)
            flat = right[:, :, :, :].rearrange("p t j n -> p t (j n)")
            dve.tensor_tensor(flat, ps[:, 4, 0:NT * NN].rearrange("p (t n) -> p t n", t=NT),
                              core.p("ff_nodeb").unsqueeze(1).broadcast_to([P, NT, NN]), ALU.add)\
               .then_inc(sig("f_node"), 1)
            dve.wait_ge(sig("f_node"), 1)
            dve.tensor_scalar(flat, flat, 0.0, None, ALU.is_ge).then_inc(sig("f_right"), 1)
            dve.wait_ge(sig("f_right"), 1)
            for d in range(DEPTH):
                w = 2 ** d
                bit = right[:, :, :, w - 1:2 * w - 1]
                kids = levels[d][:, :, :, :].rearrange("p t j (n b) -> p t j n b", b=2)
                if d:
                    dve.tensor_tensor(kids[:, :, :, :, 1], levels[d - 1][:, :, :, :], bit, ALU.mult)\
                       .then_inc(sig("f_kid"), 1)
                    dve.wait_ge(sig("f_kid"), 2 * d + 1)
                    last = dve.tensor_tensor(kids[:, :, :, :, 0], levels[d - 1][:, :, :, :], kids[:, :, :, :, 1],
                                             ALU.subtract)
                else:
                    dve.tensor_copy(kids[:, :, :, :, 1], bit).then_inc(sig("f_kid"), 1)
                    last = dve.tensor_scalar(kids[:, :, :, :, 0], bit, -1.0, 1.0, ALU.mult, ALU.add)
                if d == DEPTH - 1:
                    last.then_inc(sig("f_leaf"), 1)
                else:
                    last.then_inc(sig("f_kid"), 1)
                    dve.wait_ge(sig("f_kid"), 2 * d + 2)
            for n in range(2 * TREES):
                dve.wait_ge(sig("f_leafT_ps"), n + 1)
                dve.tensor_copy(leafT[:, n // 2, (n % 2) * HALF:(n % 2 + 1) * HALF], ps[0:NLEAF, 5 + n % 2, :])\
                   .then_inc(sig("f_leafT"), 1)
            for n in range(len(work)):
                dve.wait_ge(sig("f_hid"), n + 1)
                dve.wait_ge(sig("f_mask_ps"), n + 1)
                if n >= 2:
                    dve.wait_ge(sig("f_second_ps"), n - 1)
                dve.tensor_tensor(own[:, n % 2, :], hid[:, n % 2, :], ps[:, 2 + n % 2, :], ALU.mult)\
                   .then_inc(sig("f_own"), 1)
            mask = core.p("pair_mask").unsqueeze(1).broadcast_to([P, 4, P])
            for i in range(2):
                bank = ps[:, 4 + i, :].rearrange("p (t n) -> p t n", t=4)
                tiles = slice(4 * i, 4 * i + 4)
                dve.wait_ge(sig("f_s_ps"), i + 1)
                dve.scalar_tensor_tensor(s[:, i, :, :], bank, D ** -0.5, mask, ALU.mult, ALU.add)\
                   .then_inc(sig("f_s"), 1)
                dve.wait_ge(sig("f_s"), i + 1)
                dve.tensor_reduce(negmax[:, tiles], s[:, i, :, :], X, ALU.max, negate=True).then_inc(sig("f_negmax"), 1)
                dve.wait_ge(sig("f_negmax"), i + 1)
                dve.tensor_tensor(s1[:, i, :, :], s[:, i, :, :],
                                  negmax[:, tiles].unsqueeze(2).broadcast_to([P, 4, P]), ALU.add)\
                   .then_inc(sig("f_s1"), 1)
            for i in range(2):
                tiles = slice(4 * i, 4 * i + 4)
                dve.wait_ge(sig("f_exp"), i + 1)
                dve.tensor_reduce(total[:, tiles], s[:, i, :, :], X, ALU.add).then_inc(sig("f_total"), 1)
                dve.wait_ge(sig("f_total"), i + 1)
                dve.reciprocal(inv[:, tiles], total[:, tiles]).then_inc(sig("f_inv"), 1)
                dve.wait_ge(sig("f_inv"), i + 1)
                dve.tensor_tensor(prob[:, i, :, :], s[:, i, :, :],
                                  inv[:, tiles].unsqueeze(2).broadcast_to([P, 4, P]), ALU.mult)\
                   .then_inc(sig("f_prob"), 1)
            for i in range(NT // 2):
                dve.wait_ge(sig("f_out_ps"), i + 1)
                dve.tensor_tensor(x[:, 2 * i:2 * i + 2, :], x[:, 2 * i:2 * i + 2, :], two(ps[:, i, :]), ALU.add)\
                   .then_inc(sig("f_x"), 1)


def perceiver(nc, drams, out):
    with ExitStack() as ctx:
        core = Core(nc, ctx)
        x = core.tensor(ctx, "x", [P, NT, D])
        cstats = core.tensor(ctx, "cstats", [P, B * NC, 6])
        core.load_pack(ctx, "pk")
        core.phase(phase_topk_read, x, drams, cstats)
        core.phase(phase_retention, x, drams)
        core.phase(phase_moe, x, drams)
        core.phase(phase_heads_read, x, drams, cstats)
        core.phase(phase_features, x, drams)
        core.phase(phase_trees, x, drams)
        core.phase(store, x, out)


def store(core, x, out):
    sig = core.sig
    with ExitStack() as ctx:
        block = ctx.enter_context(core.nc.Block())

        @block.sync
        def _(sp):
            sp.dma_start(out, x[:, :, :]).then_inc(sig("x_out"), 16)
            sp.wait_ge(sig("x_out"), 16)


def halves(w):
    return w.reshape(KD, P, -1).transpose(1, 0, 2).reshape(P, -1)


def column(v):
    return v.reshape(-1, P).T


def rows(v):
    return np.broadcast_to(v.reshape(1, -1), (P, v.size))


def lay_out(a):
    p = np.arange(P)
    zeros = np.zeros((P, 1), np.float32)
    v = {"ident": np.eye(P, dtype=np.float32)}
    v["l0_wqT"] = halves(a["L0_xattn_Wq"].T)
    v["l0_wk"] = halves(a["L0_xattn_Wk"])
    v["l0_wvT"] = halves(a["L0_xattn_Wv"].T)
    v["l0_woT"] = halves(a["L0_xattn_Wo"].T)
    for n in ("bq", "bk", "bv"):
        v[f"l0_{n}"] = column(a[f"L0_xattn_{n}"])
    v["l0_bo"] = rows(a["L0_xattn_bo"])
    for n in "qkv":
        v[f"ret_w{n}"] = halves(a[f"L0_attn_weight_{n}"])
    v["ret_theta"] = column(a["L0_attn_theta"])
    j, i = p[:, None], p[None, :]
    same = (i // L) == (j // L)
    decay = np.float32(0.96875) ** (i - j).astype(np.float32)
    v["ret_decay"] = np.where(same & (i >= j), decay, 0).astype(np.float32)
    for k, n in enumerate("qkv"):
        v[f"mha_w{n}T"] = halves(a["L0_ffn_in_proj_w"][k * D:(k + 1) * D].T)
    v["mha_bq"] = column(a["L0_ffn_in_proj_b"][0:D])
    v["mha_bk"] = column(a["L0_ffn_in_proj_b"][D:2 * D])
    v["mha_bv"] = rows(a["L0_ffn_in_proj_b"][2 * D:])
    v["mha_mask"] = np.tile(np.where(i % 8 == j % 8, 0, MASKED).astype(np.float32), (1, 2))
    v["mha_woT"] = halves(a["L0_ffn_out_proj_w"].T)
    v["mha_bo"] = rows(a["L0_ffn_out_proj_b"])
    for n in ("ln1_g", "ln1_b", "ln2_g", "ln2_b"):
        v[n] = rows(a[f"L0_ffn_{n}"])
    v["moe_wg"] = halves(a["L0_ffn_wg"])
    v["moe_prefer"] = rows(np.arange(E, 0, -1).astype(np.float32))
    v["moe_base"] = rows((np.arange(E) * CAP).astype(np.float32))
    v["moe_tri"] = (j <= i).astype(np.float32)
    v["moe_ones"] = np.ones((P, P), np.float32)
    v["moe_iota"] = rows(np.arange(E * CAP).astype(np.float32))
    v["moe_b1"] = a["L0_ffn_b1"].reshape(E, FC, P).transpose(2, 0, 1).reshape(P, -1)
    v["moe_b2"] = rows(a["L0_ffn_b2"])
    v["n_wrow"], v["n_brow"] = rows(a["L1_xattn_norm_w"]), rows(a["L1_xattn_norm_b"])
    v["n_wcol"], v["n_bcol"] = column(a["L1_xattn_norm_w"]), column(a["L1_xattn_norm_b"])
    v["n1_w"], v["n1_b"] = rows(a["L1_xattn_norm1_w"]), rows(a["L1_xattn_norm1_b"])
    for n in "qkvo":
        v[f"l1_w{n}"] = halves(a[f"L1_xattn_W{n}"])
    for n in ("bq", "bk", "bv"):
        v[f"l1_{n}"] = column(a[f"L1_xattn_{n}"])
    v["l1_bo"] = rows(a["L1_xattn_bo"])
    own = (p[:, None] // HD1 == np.arange(8)[None, :]) | ((p[:, None] + 64) % P // HD1 == np.arange(8)[None, :])
    v["head_mask"] = np.where(own, HD1 ** -0.5, 0).astype(np.float32)
    v["parity"] = (p[:, None] // HD1 % 2 == np.arange(2)[None, :]).astype(np.float32)
    v["rf_gsT"] = halves(a["L1_attn_proj_matrix"].T)
    v["rf_iwT"] = halves(a["L1_attn_input_weights"].T)
    v["rf_ab"], v["rf_abcol"] = rows(a["L1_attn_xis"]), column(a["L1_attn_xis"])
    trees = "qkv"
    v["ff_nodes"] = halves(np.concatenate([a[f"L1_ffn_{n}_node_w"] for n in trees]).T)
    v["ff_nodeb"] = rows(np.concatenate([a[f"L1_ffn_{n}_node_b"] for n in trees]))
    v["ff_w1"] = np.concatenate([halves(a[f"L1_ffn_{n}_w1"].transpose(1, 0, 2).reshape(D, -1)) for n in trees], 1)
    v["ff_w2"] = np.concatenate([a[f"L1_ffn_{n}_w2"].reshape(8, P, D).transpose(1, 0, 2).reshape(P, -1)
                                 for n in trees], 1)
    v["ff_b1"] = np.concatenate([a[f"L1_ffn_{n}_b1"].reshape(8, P).T for n in trees], 1)
    b2 = np.zeros((P, TREES * D), np.float32)
    b2[0:NLEAF] = np.concatenate([a[f"L1_ffn_{n}_b2"] for n in trees], 1)
    v["ff_b2"] = b2
    leaf = np.zeros((P, 8 * P), np.float32)
    leaf[0:NLEAF] = np.arange(8 * P)[None, :] // 64 == np.arange(NLEAF)[:, None]
    v["ff_leaf"] = leaf
    v["pair_mask"] = np.where(same, 0, MASKED).astype(np.float32)
    packed = {}
    for pack, parts in PACKS.items():
        for name, n in parts:
            assert v[name].shape == (P, n), (name, v[name].shape)
        packed[pack] = np.ascontiguousarray(np.concatenate([v[name] for name, _ in parts], 1))
    ctx = a["ctx_1024"]
    padded = np.zeros((B, NC * P, D), ctx.dtype)
    padded[:, 0:S] = ctx
    packed["ctx_rows"] = padded
    packed["ctxT"] = np.ascontiguousarray(ctx.transpose(0, 2, 1))
    packed["x"] = a["x"]
    packed["moe_w1"] = a["L0_ffn_w1"]
    packed["moe_w2"] = a["L0_ffn_w2"]
    return packed


def kernel(**inputs):
    import concourse.bacc as _bacc
    from concourse.bass_utils import run_bass_kernel_spmd as _run

    nc = _bacc.Bacc("TRN2", target_bir_lowering=False, num_devices=1)
    arrays = lay_out({k: np.asarray(v) for k, v in inputs.items()})
    drams = {}
    for name, a in arrays.items():
        arrays[name] = np.ascontiguousarray(a)
        drams[name] = nc.dram_tensor(name + "_dram", a.shape, mybir.dt.from_np(a.dtype), kind="ExternalInput").ap()
    out = nc.dram_tensor("out_dram", (B, L, D), F32, kind="ExternalOutput").ap()
    drams["mixed"] = nc.dram_tensor("mixed_dram", (B, L, D), F32, kind="Internal").ap()
    perceiver(nc, drams, natural(out))
    r = _run(nc, [{k + "_dram": v for k, v in arrays.items()}], core_ids=[0])
    return r.results[0]["out_dram"]
```

```python
from contextlib import ExitStack

import concourse.bass as bass
import numpy as np
from concourse import mybir

F32 = mybir.dt.float32
BF16 = mybir.dt.bfloat16
F32R = mybir.dt.float32r
ALU = mybir.AluOpType
ACT = mybir.ActivationFunctionType
X = mybir.AxisListType.X
XY = mybir.AxisListType.XY

B, L, D = 16, 64, 256
S = 1601
P = 128
N = B * L
NT = N // P
KD = D // P
NC = -(-S // P)
SL = S - (NC - 1) * P
SW = -(-S // 4)
QUARTERS = [(i * SW, min(SW, S - i * SW)) for i in range(4)]
TOPK = 32
LOWEST = -3.0e38
MASKED = -1.0e30
EPS = 1e-5
H0, HD0 = 4, 64
E, CAP, FF = 8, N // 8, 1024
FC = FF // P
RING = 4
H1, HD1 = 16, 16
NLEAF, NNODE, DEPTH, TREES = 16, 15, 4, 3
HALF = N // 2

PACKS = {
    "pk": [("ident", P)],
    "pa": [("l0_wqT", 512), ("l0_wk", 512), ("l0_wvT", 512), ("l0_woT", 512),
           ("l0_bq", 2), ("l0_bk", 2), ("l0_bv", 2), ("l0_bo", 256)],
    "pb0": [("ret_wq", 512), ("ret_wk", 512), ("ret_wv", 512), ("ret_theta", 2), ("ret_decay", P)],
    "pb1": [("mha_wqT", 512), ("mha_wkT", 512), ("mha_wvT", 512), ("mha_bq", 2), ("mha_bk", 2),
           ("mha_bv", 256), ("mha_mask", 2 * P), ("mha_woT", 512), ("mha_bo", 256),
           ("ln1_g", 256), ("ln1_b", 256)],
    "pc": [("moe_wg", 16), ("moe_prefer", 8), ("moe_base", 8), ("moe_tri", P), ("moe_ones", P),
           ("moe_iota", E * CAP), ("moe_b1", E * FC), ("moe_b2", E * D), ("ln2_g", 256), ("ln2_b", 256)],
    "pd": [("n_wcol", 2), ("n_bcol", 2), ("n1_wcol", 2), ("n1_bcol", 2),
           ("l1_wq", 512), ("l1_wk", 512), ("l1_wv", 512), ("l1_wo", 512), ("l1_bq", 2), ("l1_bk", 2),
           ("l1_bv", 2), ("l1_bo", 256), ("head_mask", 8), ("parity", 2)],
    "pe": [("rf_gsT", 512), ("rf_iwT", 512), ("rf_ab", 256), ("rf_abcol", 2)],
    "pf": [("ff_nodes", 2 * TREES * NNODE), ("ff_nodeb", TREES * NNODE), ("ff_b1", TREES * 8), ("ff_b2", TREES * 256),
           ("ff_leaf", 8 * P), ("pair_mask", P)],
}
WIDTH = {k: sum(n for _, n in v) for k, v in PACKS.items()}


class Signals:

    def __init__(self, nc):
        self.nc, self.made = nc, {}

    def __call__(self, name):
        if name not in self.made:
            self.made[name] = self.nc.alloc_semaphore(name=name)
        return self.made[name]

    def close(self):
        self.nc.clear_and_free_semaphores(list(self.made.values()))
        self.nc.all_engine_barrier()


class Core:

    def __init__(self, nc, ctx):
        self.nc, self.sig = nc, None
        self.psum = ctx.enter_context(nc.psum_tensor("psum", [P, 8, 512], F32))
        self.params, self.packs = {}, {}

    def tensor(self, ctx, name, shape, dt=F32):
        return ctx.enter_context(self.nc.sbuf_tensor(name, shape, dt))

    def phase(self, build, *args):
        self.sig = Signals(self.nc)
        build(self, *args)
        self.sig.close()

    def load_pack(self, ctx, pack):
        tile = self.tensor(ctx, pack, [P, WIDTH[pack]])
        self.packs[pack] = tile
        at = 0
        for name, n in PACKS[pack]:
            self.params[name] = tile[:, at:at + n]
            at += n
        return tile

    def p(self, name):
        return self.params[name]

    def w(self, name):
        return self.params[name].rearrange("p (k n) -> p k n", k=KD)


def natural(dram):
    return dram.rearrange("(t b) l d -> (b l) t d", t=NT)


def norm_vector(dve, sig, tag, scratch, src, dst, ready=(), gain=None, shift=None):
    stats, moments, var, std, rstd = scratch
    for s, v in ready:
        dve.wait_ge(s, v)
    for t in range(NT):
        dve.bn_stats(stats[:, t, :], src[:, t, :]).then_inc(sig(f"{tag}_stats"), 1)
    for t in range(NT):
        dve.wait_ge(sig(f"{tag}_stats"), t + 1)
        dve.bn_aggr(moments[:, t, :], stats[:, t, :]).then_inc(sig(f"{tag}_moments"), 1)
    dve.wait_ge(sig(f"{tag}_moments"), NT)
    dve.tensor_scalar(var[:, :], moments[:, :, 1], EPS, None, ALU.add).then_inc(sig(f"{tag}_var"), 1)
    dve.wait_ge(sig(f"{tag}_std"), 1)
    dve.reciprocal(rstd[:, :], std[:, :]).then_inc(sig(f"{tag}_rstd"), 1)
    dve.wait_ge(sig(f"{tag}_rstd"), 1)
    for t in range(NT):
        dve.tensor_scalar(dst[:, t, :], src[:, t, :], moments[:, t, 0:1], rstd[:, t:t + 1],
                          ALU.subtract, ALU.mult).then_inc(sig(f"{tag}_out"), 1)
    if gain is not None:
        dve.wait_ge(sig(f"{tag}_out"), NT)
        for t in range(NT):
            dve.tensor_tensor(dst[:, t, :], dst[:, t, :], gain, ALU.mult).then_inc(sig(f"{tag}_gained"), 1)
        for t in range(NT):
            dve.wait_ge(sig(f"{tag}_gained"), t + 1)
            dve.tensor_tensor(dst[:, t, :], dst[:, t, :], shift, ALU.add).then_inc(sig(f"{tag}_shifted"), 1)


def norm_scalar(act, sig, tag, scratch):
    act.wait_ge(sig(f"{tag}_var"), 1)
    act.activation(scratch[3][:, :], scratch[2][:, :], ACT.Sqrt).then_inc(sig(f"{tag}_std"), 1)


def turn_tensor(pe, core, tag, src, first, ready, free=()):
    for s, v in free:
        pe.wait_ge(s, v)
    for c in range(2):
        for s, each in ready:
            pe.wait_ge(s, 4 * (c + 1) if each else 1)
        for k in range(KD):
            for j in range(4):
                last = pe.transpose(core.psum[:, first + 2 * c + k, j * P:(j + 1) * P],
                                    src[:, 4 * c + j, k * P:(k + 1) * P], core.p("ident"))
            last.then_inc(core.sig(f"{tag}_ps"), 1)


def by_group(T, k, c):
    return T[:, k, :].rearrange("p (g l j) -> p l g j", l=B, j=8)[:, 8 * c:8 * c + 8, :, :]


def grouped(psum_bank):
    return psum_bank.rearrange("p (l g j) -> p l g j", l=8, j=8)


def turn_scalar(act, core, tag, dst, first, group=False, affine=None):
    for c in range(2):
        act.wait_ge(core.sig(f"{tag}_ps"), 2 * c + 1)
        out, bank = dst[:, 0, c * HALF:(c + 1) * HALF], core.psum[:, first + 2 * c, :]
        if group:
            out, bank = by_group(dst, 0, c), grouped(bank)
        if affine:
            last = act.activation(out, bank, ACT.Identity, bias=affine[1][:, 0:1], scale=affine[0][:, 0:1])
        else:
            last = act.activation(out, bank, ACT.Copy)
        last.then_inc(core.sig(f"{tag}_a"), 1)


def turn_vector(dve, core, tag, dst, first, group=False, affine=None):
    for c in range(2):
        dve.wait_ge(core.sig(f"{tag}_ps"), 2 * c + 2)
        out, bank = dst[:, 1, c * HALF:(c + 1) * HALF], core.psum[:, first + 2 * c + 1, :]
        if group:
            out, bank = by_group(dst, 1, c), grouped(bank)
        if affine:
            last = dve.tensor_scalar(out, bank, affine[0][:, 1:2], affine[1][:, 1:2], ALU.mult, ALU.add)
        else:
            last = dve.tensor_copy(out, bank)
        last.then_inc(core.sig(f"{tag}_d"), 1)


def project_tensor(pe, core, tag, weight, src, first, src_tag, free=(), ready=()):
    for s, v in tuple(free) + tuple(ready):
        pe.wait_ge(s, v)
    for c in range(2):
        pe.wait_ge(core.sig(f"{src_tag}_a"), c + 1)
        pe.wait_ge(core.sig(f"{src_tag}_d"), c + 1)
        for m in range(KD):
            for k in range(KD):
                last = pe.matmul(core.psum[:, first + 2 * c + m, :], weight[:, k, m * P:(m + 1) * P],
                                 src[:, k, c * HALF:(c + 1) * HALF], start=(k == 0), stop=(k == KD - 1))
            last.then_inc(core.sig(f"{tag}_ps"), 1)


def project_scalar(act, core, tag, dst, first, bias=None, scale=1.0):
    for c in range(2):
        act.wait_ge(core.sig(f"{tag}_ps"), 2 * c + 1)
        b = 0.0 if bias is None else bias[:, 0:1]
        act.activation(dst[:, 0, c * HALF:(c + 1) * HALF], core.psum[:, first + 2 * c, :],
                       ACT.Identity, bias=b, scale=scale).then_inc(core.sig(f"{tag}_a"), 1)


def project_vector(dve, core, tag, dst, first, bias, op=ALU.add):
    for c in range(2):
        dve.wait_ge(core.sig(f"{tag}_ps"), 2 * c + 2)
        dve.tensor_scalar(dst[:, 1, c * HALF:(c + 1) * HALF], core.psum[:, first + 2 * c + 1, :],
                          bias[:, 1:2], None, op).then_inc(core.sig(f"{tag}_d"), 1)


def both(sig, tag, v=2):
    return [(sig(f"{tag}_a"), v), (sig(f"{tag}_d"), v)]


def rows_tensor(pe, core, tag, src, weight, first, waits):
    for s, v in waits:
        pe.wait_ge(s, v)
    for i in range(NT // 2):
        for j in range(2):
            t = 2 * i + j
            for k in range(KD):
                last = pe.matmul(core.psum[:, first + i, j * D:(j + 1) * D], src[:, k, t * P:(t + 1) * P],
                                 weight[:, k, :], start=(k == 0), stop=(k == KD - 1))
        last.then_inc(core.sig(f"{tag}_ps"), 1)


def two(psum_bank):
    return psum_bank.rearrange("p (j n) -> p j n", j=2)


def scratch_of(core, ctx, name):
    return (core.tensor(ctx, f"{name}_stats", [P, NT, 6]), core.tensor(ctx, f"{name}_moments", [P, NT, 2]),
            core.tensor(ctx, f"{name}_var", [P, NT]), core.tensor(ctx, f"{name}_std", [P, NT]),
            core.tensor(ctx, f"{name}_rstd", [P, NT]))


def phase_topk_read(core, x, drams, cstats):
    nc, sig, ps = core.nc, core.sig, core.psum
    with ExitStack() as ctx:
        ctx_rows, ctxT = drams["ctx_rows"], drams["ctxT"]
        params = core.load_pack(ctx, "pa")
        scratch = scratch_of(core, ctx, "a_ln")
        xn = core.tensor(ctx, "a_xn", [P, NT, D])
        xnT = core.tensor(ctx, "a_xnT", [P, KD, N])
        qT = core.tensor(ctx, "a_qT", [P, KD, N])
        keyqT = core.tensor(ctx, "a_keyqT", [P, KD, N])
        qbk = core.tensor(ctx, "a_qbk", [P, NT])
        cT = core.tensor(ctx, "a_cT", [P, 2, 2, KD, S])
        cR = core.tensor(ctx, "a_cR", [P, 2, 2, NC, D])
        pair_q = core.tensor(ctx, "a_pair_q", [P, 2, KD, P])
        pair_c = core.tensor(ctx, "a_pair_c", [P, 2])
        scores = core.tensor(ctx, "a_scores", [P, 2, S])
        left = core.tensor(ctx, "a_left", [P, S])
        probs = core.tensor(ctx, "a_probs", [P, S])
        probsT = core.tensor(ctx, "a_probsT", [P, NC, P])
        best = core.tensor(ctx, "a_best", [P, TOPK // 8, 8])
        negmax = core.tensor(ctx, "a_negmax", [P, 1])
        fence = core.tensor(ctx, "a_fence", [P, 1])
        total = core.tensor(ctx, "a_total", [P, 2])
        inv = core.tensor(ctx, "a_inv", [P, 2])
        read, readT, valT = xn, xnT, qT
        block = ctx.enter_context(nc.Block())
        T_BANK, V_BANK, SUM_BANK = 4, 6, 7
        SHARE = 4
        ones = core.tensor(ctx, "a_ones", [P, 1])
        negmean = core.tensor(ctx, "a_negmean", [P, 2, 2 * SHARE])
        spread = core.tensor(ctx, "a_spread", [P, 2 * SHARE])
        squared = core.tensor(ctx, "a_squared", [P, SHARE, D], BF16)

        @block.gpsimd
        def _(pool):
            pool.memset(ones[:, :], 1.0).then_inc(sig("a_cleared"), 1)
            pool.memset(cstats[:, :, :], 0.0).then_inc(sig("a_cleared"), 1)

        @block.sync
        def _(sp):
            sp.dma_start(x[:, :, :], natural(drams["x"])).then_inc(sig("a_x_in"), 16)
            sp.dma_start(core.packs["pk"][:, :], drams["pk"]).then_inc(sig("ident_in"), 16)
            sp.dma_start(params[:, :], drams["pa"]).then_inc(sig("a_params_in"), 16)

            def load(i, u, turn):
                for j in range(2):
                    at = bass.ds(4 * i + 2 * u + j, 1)
                    if turn is not None:
                        sp.wait_ge(sig("a_scores_ps"), 8 * i + 4 * u - 4)
                        sp.wait_ge(sig("a_sums_ps"), 8 * i + 4 * u - 4)
                    sp.dma_start(cT[:, u, j, :, :], ctxT[at].rearrange("b (k p) s -> p (b k) s", p=P))\
                      .then_inc(sig(f"a_cT_in{u}{j}"), 16)
                for j in range(2):
                    at = bass.ds(4 * i + 2 * u + j, 1)
                    if turn is not None:
                        sp.wait_ge(sig("a_pair_read"), 2 * i + u - 1)
                        sp.wait_ge(sig("a_pair_stats"), 2 * i + u - 1)
                        sp.wait_ge(sig("a_spread1"), 2 * i + u - 1)
                    sp.dma_start(cR[:, u, j, :, :], ctx_rows[at].rearrange("b (c p) d -> p (b c) d", p=P))\
                      .then_inc(sig(f"a_cR_in{u}{j}"), 16)

            load(0, 0, None)
            load(0, 1, None)
            with sp.Fori(1, NT // 2) as i:
                load(i, 0, i)
                load(i, 1, i)
            sp.dma_start(core.packs["pb0"][:, :], drams["pb0"]).then_inc(sig("b_params_in"), 16)
            sp.wait_ge(sig("b_params_in"), 16)

        @block.tensor
        def _(pe):
            pe.wait_ge(sig("ident_in"), 16)
            pe.wait_ge(sig("a_params_in"), 16)
            turn_tensor(pe, core, "a_xnT", xn, 0, [(sig("a_ln_out"), True)])
            project_tensor(pe, core, "a_qT", core.w("l0_wqT"), xnT, 4, "a_xnT")
            project_tensor(pe, core, "a_keyqT", core.w("l0_wk"), qT, 0, "a_qT", free=both(sig, "a_xnT"))
            for s, v in both(sig, "a_qT"):
                pe.wait_ge(s, v)
            for t in range(NT):
                for k in range(KD):
                    last = pe.matmul(ps[:, 4, t:t + 1], qT[:, k, t * P:(t + 1) * P],
                                     core.p("l0_bk")[:, k:k + 1], start=(k == 0), stop=(k == KD - 1))
            last.then_inc(sig("a_qbk_ps"), 1)
            for s, v in both(sig, "a_keyqT"):
                pe.wait_ge(s, v)
            pe.wait_ge(sig("a_qbk"), 1)

            def score(i, u, first=False):
                n = 2 * i + u
                pe.wait_ge(sig("a_pair_q"), n + 1)
                if not first:
                    pe.wait_ge(sig("a_scores"), 4 * n)
                for j in range(2):
                    pe.wait_ge(sig(f"a_cT_in{u}{j}"), 16 * i + 16)
                for c, (s0, w) in enumerate(QUARTERS):
                    for k in range(KD):
                        for j in range(2):
                            last = pe.matmul(ps[64 * j:64 * j + 64, c, 0:w],
                                             pair_q[:, u, k, 64 * j:64 * j + 64],
                                             cT[:, u, j, k, s0:s0 + w], start=(k == 0), stop=(k == KD - 1),
                                             tile_position=(0, 64 * j))
                    last.then_inc(sig("a_scores_ps"), 1)
                if not first:
                    pe.wait_ge(sig("a_means"), 5 * n)
                for j in range(2):
                    for c in range(SHARE):
                        for k in range(KD):
                            last = pe.matmul(ps[:, SUM_BANK, j * SHARE + c:j * SHARE + c + 1],
                                             cT[:, u, j, k, c * P:(c + 1) * P], ones[:, :], start=(k == 0),
                                             stop=(k == KD - 1))
                last.then_inc(sig("a_sums_ps"), 4)

            def value(i, u, first=False):
                n = 2 * i + u
                pe.wait_ge(sig("a_probs"), n + 1)
                for g in range(4):
                    if not (first and g < 2):
                        pe.wait_ge(sig("a_probsT"), 4 * n + g - 1)
                    for c in range(4 * g, min(4 * g + 4, NC)):
                        w = P if c < NC - 1 else SL
                        last = pe.transpose(ps[0:w, T_BANK + g % 2, (c % 4) * P:(c % 4 + 1) * P],
                                            probs[:, c * P:c * P + w], core.p("ident"))
                    last.then_inc(sig("a_probsT_ps"), 1)
                pe.wait_ge(sig("a_probsT"), 4 * n + 4)
                for j in range(2):
                    pe.wait_ge(sig(f"a_cR_in{u}{j}"), 16 * i + 16)
                if not first:
                    pe.wait_ge(sig("a_read"), n)
                for c in range(NC):
                    w = P if c < NC - 1 else SL
                    for j in range(2):
                        last = pe.matmul(ps[64 * j:64 * j + 64, V_BANK, 0:D], probsT[0:w, c, 64 * j:64 * j + 64],
                                         cR[0:w, u, j, c, :], start=(c == 0), stop=(c == NC - 1),
                                         tile_position=(0, 64 * j))
                last.then_inc(sig("a_pair_read"), 1)

            pe.wait_ge(sig("a_cleared"), 1)
            score(0, 0, first=True)
            score(0, 1)
            value(0, 0, first=True)
            with pe.Fori(1, NT // 2) as i:
                score(i, 0)
                value(i - 1, 1)
                score(i, 1)
                value(i, 0)
            value(NT // 2 - 1, 1)
            turn_tensor(pe, core, "a_readT", read, 0, [(sig("a_read"), True)])
            project_tensor(pe, core, "a_valT", core.w("l0_wvT"), readT, 4, "a_readT",
                           free=[(sig("a_read"), NT), (sig("a_probsT"), 4 * NT)])
            rows_tensor(pe, core, "a_out", valT, core.w("l0_woT"), 0, both(sig, "a_valT") + both(sig, "a_readT"))

        @block.scalar
        def _(act):
            norm_scalar(act, sig, "a_ln", scratch)
            turn_scalar(act, core, "a_xnT", xnT, 0)
            project_scalar(act, core, "a_qT", qT, 4, core.p("l0_bq"))
            project_scalar(act, core, "a_keyqT", keyqT, 0)
            act.wait_ge(sig("a_qbk_ps"), 1)
            act.mul(qbk[:, :], ps[:, 4, 0:NT], D ** -0.5).then_inc(sig("a_qbk"), 1)

            def gather(i, u, first=False):
                n = 2 * i + u
                act.wait_ge(sig("a_pair_q"), n + 1)
                if not first:
                    act.wait_ge(sig("a_probs"), n - 1)
                for c, (s0, w) in enumerate(QUARTERS):
                    act.wait_ge(sig("a_scores_ps"), 4 * n + c + 1)
                    act.activation(scores[:, u, s0:s0 + w], ps[:, c, 0:w], ACT.Identity,
                                   bias=pair_c[:, u:u + 1], scale=D ** -0.5).then_inc(sig("a_scores"), 1)

            def exps(i, u, first=False):
                n = 2 * i + u
                act.wait_ge(sig("a_negmax"), n + 1)
                act.wait_ge(sig("a_scores"), 4 * n + 4)
                if not first:
                    act.wait_ge(sig("a_probsT_ps"), 4 * n)
                act.activation(probs[:, :], scores[:, u, :], ACT.Exp, bias=negmax[:, 0:1])\
                   .then_inc(sig("a_exp"), 1)

            def row_means(i, u, first=False):
                n = 2 * i + u
                act.wait_ge(sig("a_sums_ps"), 4 * n + 4)
                if not first:
                    act.wait_ge(sig("a_squares"), 2 * SHARE * (n - 1))
                sums = ps[:, SUM_BANK, 0:2 * SHARE]
                act.activation(negmean[:, u, :], sums, ACT.Copy, scale=-1.0 / D).then_inc(sig("a_means"), 1)
                for j in range(2):
                    rows = bass.ds((2 * n + j) * NC, SHARE)
                    for half in (1, 4):
                        act.activation(cstats[:, rows, half], sums[:, j * SHARE:(j + 1) * SHARE], ACT.Copy,
                                       scale=1.0 / D).then_inc(sig("a_means"), 1)

            def row_squares(i, u, j, first=False):
                n = 2 * i + u
                act.wait_ge(sig("a_means"), 5 * n + 5)
                act.wait_ge(sig(f"a_cR_in{u}{j}"), 16 * i + 16)
                if j:
                    act.wait_ge(sig("a_spread0"), n + 1)
                elif not first:
                    act.wait_ge(sig("a_spread1"), n)
                for c in range(SHARE):
                    at = j * SHARE + c
                    act.activation(squared[:, c, :], cR[:, u, j, c, :], ACT.Square, bias=negmean[:, u, at:at + 1],
                                   accum_out=spread[:, at:at + 1]).then_inc(sig("a_squares"), 1)
                act.wait_ge(sig("a_squares"), 2 * SHARE * n + SHARE * (j + 1))
                act.activation(cstats[:, bass.ds((2 * n + j) * NC, SHARE), 2], spread[:, j * SHARE:(j + 1) * SHARE],
                               ACT.Copy).then_inc(sig(f"a_spread{j}"), 1)

            def take(i, u, first=False):
                n = 2 * i + u
                for g in range(4):
                    act.wait_ge(sig("a_probsT_ps"), 4 * n + g + 1)
                    if g == 0 and not first:
                        act.wait_ge(sig("a_pair_read"), n)
                    if g < 3:
                        act.activation(probsT[:, 4 * g:4 * g + 4, :], ps[:, T_BANK + g % 2, :], ACT.Copy)\
                           .then_inc(sig("a_probsT"), 1)
                    else:
                        act.activation(probsT[0:SL, 12, :], ps[0:SL, T_BANK + 1, 0:P], ACT.Copy)\
                           .then_inc(sig("a_probsT"), 1)
                row_squares(i, u, 0, first)
                act.wait_ge(sig("a_pair_read"), n + 1)
                act.wait_ge(sig("a_inv"), n + 1)
                act.activation(read[:, bass.ds(2 * i + u, 1), :].rearrange("p a d -> p (a d)"),
                               ps[:, V_BANK, 0:D], ACT.Copy, scale=inv[:, u:u + 1]).then_inc(sig("a_read"), 1)

            act.wait_ge(sig("a_cleared"), 2)
            gather(0, 0, first=True)
            exps(0, 0, first=True)
            row_means(0, 0, first=True)
            gather(0, 1, first=True)
            row_means(0, 1, first=True)

            def turn_of(i, u, first=False):
                take(i - 1, u, first)
                exps(*((i, 0) if u else (i - 1, 1)))
                row_squares(i - 1, u, 1)
                gather(i, u)
                row_means(i, u)

            turn_of(1, 0, first=True)
            with act.Fori(1, NT // 2 - 1) as i:
                turn_of(i, 1)
                turn_of(i + 1, 0)
            turn_of(NT // 2 - 1, 1)
            take(NT // 2 - 1, 0)
            exps(NT // 2 - 1, 1)
            row_squares(NT // 2 - 1, 0, 1)
            take(NT // 2 - 1, 1)
            row_squares(NT // 2 - 1, 1, 1)
            turn_scalar(act, core, "a_readT", readT, 0)
            project_scalar(act, core, "a_valT", valT, 4, core.p("l0_bv"))

        @block.vector
        def _(dve):
            norm_vector(dve, sig, "a_ln", scratch, x, xn, ready=[(sig("a_x_in"), 16)])
            dve.wait_ge(sig("a_params_in"), 16)
            turn_vector(dve, core, "a_xnT", xnT, 0)
            project_vector(dve, core, "a_qT", qT, 4, core.p("l0_bq"))
            for c in range(2):
                dve.wait_ge(sig("a_keyqT_ps"), 2 * c + 2)
                dve.tensor_copy(keyqT[:, 1, c * HALF:(c + 1) * HALF], ps[:, 2 * c + 1, :])\
                   .then_inc(sig("a_keyqT_d"), 1)
            dve.wait_ge(sig("a_qbk"), 1)
            for s, v in both(sig, "a_keyqT"):
                dve.wait_ge(s, v)

            def pair_inputs(i, u):
                t = 2 * i + u
                dve.tensor_copy(pair_c[:, u:u + 1], qbk[:, bass.ds(t, 1)]).then_inc(sig("a_pair_c"), 1)
                dve.wait_ge(sig("a_pair_c"), t + 1)
                dve.tensor_copy(pair_q[:, u, :, :], keyqT[:, :, bass.ds(t * P, P)]).then_inc(sig("a_pair_q"), 1)

            def choose(i, u, first=False):
                n = 2 * i + u
                dve.wait_ge(sig("a_scores"), 4 * n + 4)
                for r in range(TOPK // 8):
                    src = scores[:, u, :] if r == 0 else left[:, :]
                    if r:
                        dve.wait_ge(sig("a_left"), 4 * n + r)
                    dve.memset(fence[:, :], 0.0)
                    dve.max(best[:, r, :], src).then_inc(sig("a_best"), 1)
                    dve.wait_ge(sig("a_best"), 4 * n + r + 1)
                    if r == 0:
                        dve.tensor_scalar(negmax[:, :], best[:, 0, 0:1], -1.0, None, ALU.mult)\
                           .then_inc(sig("a_negmax"), 1)
                    dve.memset(fence[:, :], 0.0)
                    dve.match_replace(left[:, :], best[:, r, :], src, LOWEST).then_inc(sig("a_left"), 1)
                dve.wait_ge(sig("a_left"), 4 * n + 4)
                dve.wait_ge(sig("a_exp"), n + 1)
                dve.scalar_tensor_tensor(probs[:, :], left[:, :], LOWEST, probs[:, :], ALU.is_le, ALU.mult,
                                         accum_out=total[:, u:u + 1]).then_inc(sig("a_probs"), 1)
                dve.wait_ge(sig("a_probs"), n + 1)
                if not first:
                    dve.wait_ge(sig("a_read"), n)
                dve.reciprocal(inv[:, u:u + 1], total[:, u:u + 1]).then_inc(sig("a_inv"), 1)

            def row_stats(i, u):
                for j in range(2):
                    dve.wait_ge(sig(f"a_cR_in{u}{j}"), 16 * i + 16)
                    for c in range(SHARE, NC):
                        col = (4 * i + 2 * u + j) * NC + c
                        last = dve.bn_stats(cstats[:, bass.ds(col, 1), :].rearrange("p a n -> p (a n)"),
                                            cR[:, u, j, c, :])
                last.then_inc(sig("a_pair_stats"), 1)

            dve.wait_ge(sig("a_cleared"), 2)
            pair_inputs(0, 0)
            pair_inputs(0, 1)
            row_stats(0, 0)
            choose(0, 0, first=True)
            with dve.Fori(1, NT // 2) as i:
                for u, (ci, cu) in enumerate(((i - 1, 1), (i, 0))):
                    dve.wait_ge(sig("a_scores_ps"), 8 * i + 4 * u - 4)
                    dve.wait_ge(sig("a_scores"), 8 * i + 4 * u - 4)
                    pair_inputs(i, u)
                    choose(ci, cu)
                    row_stats(ci, cu)
            choose(NT // 2 - 1, 1)
            row_stats(NT // 2 - 1, 1)
            turn_vector(dve, core, "a_readT", readT, 0)
            project_vector(dve, core, "a_valT", valT, 4, core.p("l0_bv"))
            for i in range(NT // 2):
                dve.wait_ge(sig("a_out_ps"), i + 1)
                dve.tensor_tensor(x[:, 2 * i:2 * i + 2, :], x[:, 2 * i:2 * i + 2, :], two(ps[:, i, :]), ALU.add)\
                   .then_inc(sig("a_x_sum"), 1)
            for t in range(NT):
                dve.wait_ge(sig("a_x_sum"), t // 2 + 1)
                dve.tensor_tensor(x[:, t, :], x[:, t, :], core.p("l0_bo"), ALU.add).then_inc(sig("a_x"), 1)


def phase_retention(core, x, drams, cstats, mean, rstd):
    nc, sig, ps = core.nc, core.sig, core.psum
    with ExitStack() as ctx:
        scratch = scratch_of(core, ctx, "b_ln")
        xn = core.tensor(ctx, "b_xn", [P, NT, D])
        xnT = core.tensor(ctx, "b_xnT", [P, KD, N])
        theta = core.tensor(ctx, "b_theta", [P, KD])
        qT = core.tensor(ctx, "b_qT", [P, KD, N])
        kT = core.tensor(ctx, "b_kT", [P, KD, N])
        v = core.tensor(ctx, "b_v", [P, NT, D])
        diff = core.tensor(ctx, "b_diff", [P, B * NC])
        sT = core.tensor(ctx, "b_sT", [P, NT, P])
        block = ctx.enter_context(nc.Block())

        @block.tensor
        def _(pe):
            turn_tensor(pe, core, "b_xnT", xn, 0, [(sig("b_ln_out"), True)])
            project_tensor(pe, core, "b_qT", core.w("ret_wq"), xnT, 4, "b_xnT")
            project_tensor(pe, core, "b_kT", core.w("ret_wk"), xnT, 0, "b_xnT", free=both(sig, "b_xnT"))
            rows_tensor(pe, core, "b_v", xnT, core.w("ret_wv"), 4, both(sig, "b_qT"))
            for s, n in both(sig, "b_kT"):
                pe.wait_ge(s, n)
            for t in range(NT):
                for k in range(KD):
                    last = pe.matmul(ps[:, t // 4, (t % 4) * P:(t % 4 + 1) * P], kT[:, k, t * P:(t + 1) * P],
                                     qT[:, k, t * P:(t + 1) * P], start=(k == 0), stop=(k == KD - 1))
                if t % 4 == 3:
                    last.then_inc(sig("b_sT_ps"), 1)
            pe.wait_ge(sig("b_v"), NT // 2)
            for t in range(NT):
                pe.wait_ge(sig("b_sT"), t // 4 + 1)
                last = pe.matmul(ps[:, 4 + t // 2, (t % 2) * D:(t % 2 + 1) * D], sT[:, t, :], v[:, t, :],
                                 start=True, stop=True)
                if t % 2:
                    last.then_inc(sig("b_out_ps"), 1)

        @block.scalar
        def _(act):
            act.activation(theta[:, :], core.p("ret_theta"), ACT.Exp, scale=0.0).then_inc(sig("b_theta"), 1)
            norm_scalar(act, sig, "b_ln", scratch)
            turn_scalar(act, core, "b_xnT", xnT, 0)
            act.wait_ge(sig("b_theta"), 1)
            project_scalar(act, core, "b_qT", qT, 4, scale=theta[:, 0:1])
            project_scalar(act, core, "b_kT", kT, 0, scale=theta[:, 0:1])
            for i in range(NT // 2):
                act.wait_ge(sig("b_v_ps"), i + 1)
                act.activation(v[:, 2 * i:2 * i + 2, :], two(ps[:, 4 + i, :]), ACT.Copy).then_inc(sig("b_v"), 1)
            act.wait_ge(sig("b_rowvar"), 1)
            act.activation(diff[:, :], rstd[:, :], ACT.Sqrt).then_inc(sig("b_rowstd"), 1)

        @block.vector
        def _(dve):
            norm_vector(dve, sig, "b_ln", scratch, x, xn)
            turn_vector(dve, core, "b_xnT", xnT, 0)
            dve.wait_ge(sig("b_theta"), 1)
            project_vector(dve, core, "b_qT", qT, 4, theta, ALU.mult)
            project_vector(dve, core, "b_kT", kT, 0, theta, ALU.mult)
            m_even, m_odd, v_even, v_odd = (cstats[:, :, j] for j in (1, 4, 2, 5))
            small = [0]

            def step(ins):
                small[0] += 1
                ins.then_inc(sig("b_small"), 1)
                dve.wait_ge(sig("b_small"), small[0])

            step(dve.tensor_tensor(mean[:, :], m_even, m_odd, ALU.add))
            step(dve.tensor_tensor(diff[:, :], m_even, m_odd, ALU.subtract))
            step(dve.tensor_scalar(mean[:, :], mean[:, :], 0.5, None, ALU.mult))
            step(dve.tensor_tensor(diff[:, :], diff[:, :], diff[:, :], ALU.mult))
            step(dve.tensor_tensor(rstd[:, :], v_even, v_odd, ALU.add))
            step(dve.tensor_scalar(diff[:, :], diff[:, :], 0.25, EPS, ALU.mult, ALU.add))
            dve.scalar_tensor_tensor(rstd[:, :], rstd[:, :], 1.0 / D, diff[:, :], ALU.mult, ALU.add)\
               .then_inc(sig("b_rowvar"), 1)
            decay = core.p("ret_decay").unsqueeze(1).broadcast_to([P, 4, P])
            for i in range(2):
                dve.wait_ge(sig("b_sT_ps"), i + 1)
                dve.tensor_tensor(sT[:, 4 * i:4 * i + 4, :], ps[:, i, :].rearrange("p (t n) -> p t n", t=4), decay,
                                  ALU.mult).then_inc(sig("b_sT"), 1)
            for i in range(NT // 2):
                dve.wait_ge(sig("b_out_ps"), i + 1)
                dve.tensor_tensor(x[:, 2 * i:2 * i + 2, :], x[:, 2 * i:2 * i + 2, :], two(ps[:, 4 + i, :]), ALU.add)\
                   .then_inc(sig("b_x"), 1)
            dve.wait_ge(sig("b_rowstd"), 1)
            dve.reciprocal(rstd[:, :], diff[:, :]).then_inc(sig("b_rstd"), 1)


def phase_moe(core, x, drams):
    with ExitStack() as ctx:
        w1 = core.tensor(ctx, "moe_w1", [P, RING, KD, FF])
        w2 = core.tensor(ctx, "moe_w2", [P, RING, FC, D])
        y1 = core.tensor(ctx, "moe_in", [P, NT, D])
        core.load_pack(ctx, "pc")
        phase_mha(core, x, y1, w1, w2, drams)
        phase_experts(core, x, y1, w1, w2, drams)


def load_expert(sp, sig, w1, w2, drams, e, u):
    sp.dma_start(w1[:, u, :, :], drams["moe_w1"][e].rearrange("e (k p) f -> p (e k) f", p=P))\
      .then_inc(sig(f"c_w1_in{u}"), 16)
    sp.dma_start(w2[:, u, :, :], drams["moe_w2"][e].rearrange("e (c p) d -> p (e c) d", p=P))\
      .then_inc(sig(f"c_w2_in{u}"), 16)


def phase_mha(core, x, y1, w1, w2, drams):
    nc, sig, ps = core.nc, core.sig, core.psum
    G, J = 8, 8
    with ExitStack() as ctx:
        params = core.load_pack(ctx, "pb1")
        scratch = scratch_of(core, ctx, "m_ln")
        scratch2 = scratch_of(core, ctx, "m_ln2")
        xf = core.tensor(ctx, "m_xf", [P, NT, D])
        xfT = core.tensor(ctx, "m_xfT", [P, KD, N])
        qT = core.tensor(ctx, "m_qT", [P, KD, N])
        kT = core.tensor(ctx, "m_kT", [P, KD, N])
        vG = core.tensor(ctx, "m_vG", [P, G, D])
        oT = core.tensor(ctx, "m_oT", [P, KD, N])
        s = core.tensor(ctx, "m_s", [P, 2, H0, P])
        s1 = core.tensor(ctx, "m_s1", [P, 2, H0, P])
        prob = core.tensor(ctx, "m_prob", [P, 2, H0, P])
        probn = core.tensor(ctx, "m_probn", [P, 2, H0, P])
        probT = core.tensor(ctx, "m_probT", [P, 2, H0, P])
        negmax = core.tensor(ctx, "m_negmax", [P, 2, H0])
        total = core.tensor(ctx, "m_total", [P, 2, H0])
        inv = core.tensor(ctx, "m_inv", [P, 2, H0])
        block = ctx.enter_context(nc.Block())

        def group(T, g):
            return T[:, :, :].rearrange("p k (l n) -> p k l n", l=B)[:, :, :, J * g:J * g + J]

        @block.sync
        def _(sp):
            sp.dma_start(params[:, :], drams["pb1"]).then_inc(sig("m_params_in"), 16)
            sp.dma_start(core.packs["pc"][:, :], drams["pc"]).then_inc(sig("c_params_in"), 16)
            for u in range(RING):
                load_expert(sp, sig, w1, w2, drams, bass.ds(u, 1), u)

        @block.tensor
        def _(pe):
            pe.wait_ge(sig("m_params_in"), 16)
            turn_tensor(pe, core, "m_xfT", xf, 0, [(sig("m_ln_out"), True)])
            project_tensor(pe, core, "m_qT", core.w("mha_wqT"), xfT, 4, "m_xfT", ready=both(sig, "m_xfT"))
            project_tensor(pe, core, "m_kT", core.w("mha_wkT"), xfT, 0, "m_xfT", free=both(sig, "m_xfT"))
            for sm, n in both(sig, "m_qT"):
                pe.wait_ge(sm, n)
            for g in range(G):
                for k in range(KD):
                    last = pe.matmul(ps[:, 4 + g // 2, (g % 2) * D:(g % 2 + 1) * D], xfT[:, k, g * P:(g + 1) * P],
                                     core.w("mha_wvT")[:, k, :], start=(k == 0), stop=(k == KD - 1))
                if g % 2:
                    last.then_inc(sig("m_vG_ps"), 1)

            def scores(g):
                if g >= 2:
                    pe.wait_ge(sig("m_s"), g - 1)
                for h in range(H0):
                    r = 64 * (h % 2)
                    last = pe.matmul(ps[:, 2 * (g % 2) + h % 2, (h // 2) * P:(h // 2 + 1) * P], qT[r:r + 64, h // 2, g * P:(g + 1) * P],
                                     kT[r:r + 64, h // 2, g * P:(g + 1) * P], start=True, stop=True,
                                     tile_position=(r, 0))
                last.then_inc(sig("m_s_ps"), 1)

            def values(g):
                pe.wait_ge(sig("m_probn"), g + 1)
                if g >= 2:
                    pe.wait_ge(sig("m_probT"), g - 1)
                for h in range(H0):
                    last = pe.transpose(ps[:, 4 + g % 2, h * P:(h + 1) * P], probn[:, g % 2, h, :], core.p("ident"))
                last.then_inc(sig("m_probT_ps"), 1)
                pe.wait_ge(sig("m_probT"), g + 1)
                if g >= 2:
                    pe.wait_ge(sig("m_oT_a"), g - 1)
                    pe.wait_ge(sig("m_oT_d"), g - 1)
                for q in range(H0):
                    h, r = 2 * (q % 2) + q // 2, 64 * (q // 2)
                    last = pe.matmul(ps[r:r + 64, 6 + g % 2, (h // 2) * P:(h // 2 + 1) * P],
                                     vG[:, g, h * HD0:(h + 1) * HD0], probT[:, g % 2, q, :],
                                     start=True, stop=True, tile_position=(0, r))
                last.then_inc(sig("m_oT_ps"), 1)

            for sm, n in both(sig, "m_kT"):
                pe.wait_ge(sm, n)
            scores(0)
            scores(1)
            pe.wait_ge(sig("m_vG"), G // 2)
            for g in range(G):
                if g + 2 < G:
                    scores(g + 2)
                values(g)
            rows_tensor(pe, core, "m_proj", oT, core.w("mha_woT"), 0, both(sig, "m_oT", G) + [(sig("m_probT"), G)])

        @block.scalar
        def _(act):
            norm_scalar(act, sig, "m_ln", scratch)
            turn_scalar(act, core, "m_xfT", xfT, 0, group=True)
            act.wait_ge(sig("m_params_in"), 16)
            project_scalar(act, core, "m_qT", qT, 4, core.p("mha_bq"))
            project_scalar(act, core, "m_kT", kT, 0, core.p("mha_bk"))

            def exps(g):
                act.wait_ge(sig("m_s1"), g + 1)
                act.activation(prob[:, g % 2, :, :], s1[:, g % 2, :, :], ACT.Exp).then_inc(sig("m_prob"), 1)

            exps(0)
            for g in range(G):
                if g + 1 < G:
                    exps(g + 1)
                act.wait_ge(sig("m_probT_ps"), g + 1)
                act.activation(probT[:, g % 2, :, :], ps[:, 4 + g % 2, :], ACT.Copy).then_inc(sig("m_probT"), 1)
                act.wait_ge(sig("m_oT_ps"), g + 1)
                act.activation(group(oT, g)[:, 0, :, :], ps[:, 6 + g % 2, 0:P].rearrange("p (l j) -> p l j", j=J),
                               ACT.Copy).then_inc(sig("m_oT_a"), 1)
            norm_scalar(act, sig, "m_ln2", scratch2)

        @block.vector
        def _(dve):
            norm_vector(dve, sig, "m_ln", scratch, x, xf)
            turn_vector(dve, core, "m_xfT", xfT, 0, group=True)
            dve.wait_ge(sig("m_params_in"), 16)
            project_vector(dve, core, "m_qT", qT, 4, core.p("mha_bq"))
            project_vector(dve, core, "m_kT", kT, 0, core.p("mha_bk"))
            bv = core.p("mha_bv").unsqueeze(1).broadcast_to([P, 2, D])
            for i in range(G // 2):
                dve.wait_ge(sig("m_vG_ps"), i + 1)
                dve.tensor_tensor(vG[:, 2 * i:2 * i + 2, :], two(ps[:, 4 + i, :]), bv, ALU.add).then_inc(sig("m_vG"), 1)
            mask = core.p("mha_mask").unsqueeze(1).broadcast_to([P, 2, 2 * P])

            def masked(g):
                u = g % 2
                dve.wait_ge(sig("m_s_ps"), g + 1)
                dve.scalar_tensor_tensor(s[:, u, :, :].rearrange("p (r m) n -> p r (m n)", r=2),
                                         ps[:, 2 * u:2 * u + 2, 0:2 * P],
                                         HD0 ** -0.5, mask, ALU.mult, ALU.add).then_inc(sig("m_s"), 1)
                dve.wait_ge(sig("m_s"), g + 1)
                dve.tensor_reduce(negmax[:, u, :], s[:, u, :, :], X, ALU.max, negate=True)\
                   .then_inc(sig("m_negmax"), 1)
                dve.wait_ge(sig("m_negmax"), g + 1)
                if g >= 2:
                    dve.wait_ge(sig("m_prob"), g - 1)
                dve.tensor_tensor(s1[:, u, :, :], s[:, u, :, :],
                                  negmax[:, u, :].unsqueeze(2).broadcast_to([P, H0, P]), ALU.add)\
                   .then_inc(sig("m_s1"), 1)

            def normed(g):
                u = g % 2
                dve.wait_ge(sig("m_prob"), g + 1)
                dve.tensor_reduce(total[:, u, :], prob[:, u, :, :], X, ALU.add).then_inc(sig("m_total"), 1)
                dve.wait_ge(sig("m_total"), g + 1)
                dve.reciprocal(inv[:, u, :], total[:, u, :]).then_inc(sig("m_inv"), 1)
                dve.wait_ge(sig("m_inv"), g + 1)
                if g >= 2:
                    dve.wait_ge(sig("m_probT_ps"), g - 1)
                dve.tensor_tensor(probn[:, u, :, :], prob[:, u, :, :],
                                  inv[:, u, :].unsqueeze(2).broadcast_to([P, H0, P]), ALU.mult)\
                   .then_inc(sig("m_probn"), 1)

            def out(g):
                dve.wait_ge(sig("m_oT_ps"), g + 1)
                dve.wait_ge(sig("m_oT_a"), g + 1)
                dve.tensor_copy(group(oT, g)[:, 1, :, :], ps[:, 6 + g % 2, P:2 * P].rearrange("p (l j) -> p l j", j=J))\
                   .then_inc(sig("m_oT_d"), 1)

            masked(0)
            for g in range(G):
                if g + 1 < G:
                    masked(g + 1)
                normed(g)
                if g:
                    out(g - 1)
            out(G - 1)
            for i in range(NT // 2):
                dve.wait_ge(sig("m_proj_ps"), i + 1)
                dve.tensor_tensor(y1[:, 2 * i:2 * i + 2, :], two(ps[:, i, :]), xf[:, 2 * i:2 * i + 2, :], ALU.add)\
                   .then_inc(sig("m_res"), 1)
            for t in range(NT):
                dve.wait_ge(sig("m_res"), t // 2 + 1)
                dve.tensor_tensor(y1[:, t, :], y1[:, t, :], core.p("mha_bo"), ALU.add).then_inc(sig("m_y"), 1)
            norm_vector(dve, sig, "m_ln2", scratch2, y1, y1, [(sig("m_y"), NT)], core.p("ln1_g"), core.p("ln1_b"))


def phase_experts(core, x, y1, w1, w2, drams):
    nc, sig, ps = core.nc, core.sig, core.psum
    with ExitStack() as ctx:
        scratch = scratch_of(core, ctx, "c_ln")
        y1T = core.tensor(ctx, "c_y1T", [P, KD, N])
        logit = core.tensor(ctx, "c_logit", [P, NT, E])
        tmp = core.tensor(ctx, "c_tmp", [P, NT, E])
        pref = core.tensor(ctx, "c_pref", [P, NT, E])
        oneh = core.tensor(ctx, "c_oneh", [P, NT, E])
        expl = core.tensor(ctx, "c_expl", [P, NT, E])
        onehB = core.tensor(ctx, "c_onehB", [P, NT, E], BF16)
        triB = core.tensor(ctx, "c_triB", [P, P], BF16)
        onesB = core.tensor(ctx, "c_onesB", [P, P], BF16)
        col = core.tensor(ctx, "c_col", [P, 8, NT])
        gate, slot = col[:, 0, :], col[:, 1, :]
        place = core.tensor(ctx, "c_place", [P, NT, E * CAP], F32R)
        placeT = core.tensor(ctx, "c_placeT", [P, E, N], F32R)
        part = [core.tensor(ctx, f"c_part{c}", [P, NT, D], F32R) for c in "HL"]
        disp = core.tensor(ctx, "c_disp", [P, KD, E * CAP])
        hT = core.tensor(ctx, "c_hT", [P, 2, FC, CAP])
        y = y1T[:, 0, 0:2 * D].rearrange("p (u d) -> p u d", u=2)
        y2 = y1T[:, :, :].rearrange("p k n -> p (k n)").rearrange("p (t d) -> p t d", t=NT)
        block = ctx.enter_context(nc.Block())

        def experts(eng, hidden, output):
            hidden(0, 0, first=True)
            for u in range(1, RING):
                hidden(0, u, first=True)
                output(0, u - 1, first=True)
            with eng.Fori(1, E // RING) as i:
                for u in range(RING):
                    hidden(i, u)
                    if u:
                        output(i, u - 1)
                    else:
                        output(i - 1, RING - 1)
            output(E // RING - 1, RING - 1)

        @block.sync
        def _(sp):
            with sp.Fori(1, E // RING) as i:
                for u in range(RING):
                    sp.wait_ge(sig("c_y_ps"), RING * (i - 1) + u + 1)
                    load_expert(sp, sig, w1, w2, drams, bass.ds(RING * i + u, 1), u)

        @block.gpsimd
        def _(pool):
            for t in range(NT):
                pool.wait_ge(sig("c_y1H"), t + 1)
                pool.tensor_tensor(part[1][:, t, :], y1[:, t, :], part[0][:, t, :].bitcast(F32), ALU.subtract)\
                    .then_inc(sig("c_y1L"), 1)

        @block.tensor
        def _(pe):
            turn_tensor(pe, core, "c_y1T", y1, 0, [])
            pe.wait_ge(sig("c_params_in"), 16)
            for c in range(2):
                for s, n in both(sig, "c_y1T", c + 1):
                    pe.wait_ge(s, n)
                for t in range(4 * c, 4 * c + 4):
                    for k in range(KD):
                        last = pe.matmul(ps[:, 4, t * E:(t + 1) * E], y1T[:, k, t * P:(t + 1) * P],
                                         core.w("moe_wg")[:, k, :], start=(k == 0), stop=(k == KD - 1))
            last.then_inc(sig("c_logit_ps"), 1)
            pe.wait_ge(sig("c_onehB"), 1)
            pe.wait_ge(sig("c_countB"), 2)
            for t in range(NT):
                for b in range(t + 1):
                    last = pe.matmul(ps[:, 5, t * E:(t + 1) * E], (triB if b == t else onesB)[:, :],
                                     onehB[:, b, :], start=(b == 0), stop=(b == t))
            last.then_inc(sig("c_count_ps"), 1)
            for t in range(NT):
                pe.wait_ge(sig("c_y1L"), t + 1)
                pe.wait_ge(sig("c_place"), t + 1)
                for k in range(KD):
                    for c in range(2):
                        for h in range(2):
                            last = pe.matmul(ps[:, 2 * k + c, :], part[h][:, t, k * P:(k + 1) * P],
                                             place[:, t, c * HALF:(c + 1) * HALF], start=(t == 0 and h == 0),
                                             stop=(t == NT - 1 and h == 1))
            last.then_inc(sig("c_disp_ps"), 1)

            def turn_place(e, c, n):
                if n >= 2:
                    pe.wait_ge(sig("c_placeT"), n - 1)
                for j in range(4):
                    last = pe.transpose(ps[:, 6 + n % 2, j * P:(j + 1) * P],
                                        place[:, 4 * c + j, e * CAP:(e + 1) * CAP].bitcast(F32), core.p("ident"))
                last.then_inc(sig("c_placeT_ps"), 1)

            for n in range(2 * E):
                turn_place(n // 2, n % 2, n)
            pe.wait_ge(sig("c_disp"), 4)
            pe.wait_ge(sig("c_slot"), 1)

            def hidden(i, u, first=False):
                n = RING * i + u
                pe.wait_ge(sig(f"c_w1_in{u}"), 16 * i + 16)
                for q in range(2):
                    if not (first and u == 0):
                        pe.wait_ge(sig("c_hT"), 2 * n + q - 1)
                    for f in range(4 * q, 4 * q + 4):
                        for k in range(KD):
                            last = pe.matmul(ps[:, q, (f % 4) * P:(f % 4 + 1) * P], w1[:, u, k, f * P:(f + 1) * P],
                                             disp[:, k, bass.ds(n * CAP, CAP)], start=(k == 0), stop=(k == KD - 1))
                    last.then_inc(sig("c_hT_ps"), 1)

            def output(i, u, first=False):
                n = RING * i + u
                pe.wait_ge(sig(f"c_w2_in{u}"), 16 * i + 16)
                pe.wait_ge(sig("c_hT"), 2 * n + 2)
                if not (first and u < 2):
                    pe.wait_ge(sig("c_y"), n - 1)
                for f in range(FC):
                    last = pe.matmul(ps[:, 2 + u % 2, 0:D], hT[:, u % 2, f, :], w2[:, u, f, :], start=(f == 0),
                                     stop=(f == FC - 1))
                last.then_inc(sig("c_y_ps"), 1)

            experts(pe, hidden, output)
            pe.wait_ge(sig("c_yL"), E)
            pe.wait_ge(sig("c_placeT"), 2 * E)
            for t in range(NT):
                for e in range(E):
                    for h in range(2):
                        last = pe.matmul(ps[:, 4 + t // 2, (t % 2) * D:(t % 2 + 1) * D],
                                         placeT[:, e, t * P:(t + 1) * P], part[h][:, e, :],
                                         start=(e == 0 and h == 0), stop=(e == E - 1 and h == 1))
                if t % 2:
                    last.then_inc(sig("c_back_ps"), 1)

        @block.scalar
        def _(act):
            for t in range(NT):
                act.activation(part[0][:, t, :], y1[:, t, :], ACT.Copy).then_inc(sig("c_y1H"), 1)
            turn_scalar(act, core, "c_y1T", y1T, 0)
            act.wait_ge(sig("c_params_in"), 16)
            for dst, name in ((triB, "moe_tri"), (onesB, "moe_ones")):
                act.activation(dst[:, :], core.p(name), ACT.Copy).then_inc(sig("c_countB"), 1)
            act.wait_ge(sig("c_less"), 1)
            act.activation(expl[:, :, :], tmp[:, :, :], ACT.Exp).then_inc(sig("c_expl"), 1)
            for n in range(2 * E):
                act.wait_ge(sig("c_placeT_ps"), n + 1)
                act.activation(placeT[:, n // 2, (n % 2) * HALF:(n % 2 + 1) * HALF], ps[:, 6 + n % 2, :], ACT.Copy)\
                   .then_inc(sig("c_placeT"), 1)
            norm_scalar(act, sig, "c_ln", scratch)

        @block.vector
        def _(dve):
            turn_vector(dve, core, "c_y1T", y1T, 0)
            wide = lambda a: a.unsqueeze(2).broadcast_to([P, NT, E])
            row = lambda name: core.p(name).unsqueeze(1).broadcast_to([P, NT, E])
            small = [0]

            def step(ins):
                small[0] += 1
                ins.then_inc(sig("c_small"), 1)
                dve.wait_ge(sig("c_small"), small[0])

            dve.wait_ge(sig("c_params_in"), 16)
            dve.wait_ge(sig("c_logit_ps"), 1)
            step(dve.tensor_copy(logit[:, :, :], ps[:, 4, 0:NT * E].rearrange("p (t e) -> p t e", t=NT)))
            step(dve.tensor_reduce(col[:, 2, :], logit[:, :, :], X, ALU.max))
            step(dve.tensor_tensor(pref[:, :, :], logit[:, :, :], wide(col[:, 2, :]), ALU.is_equal))
            step(dve.tensor_tensor(pref[:, :, :], pref[:, :, :], row("moe_prefer"), ALU.mult))
            step(dve.tensor_reduce(col[:, 3, :], pref[:, :, :], X, ALU.max))
            dve.tensor_tensor(onehB[:, :, :], pref[:, :, :], wide(col[:, 3, :]), ALU.is_equal)\
               .then_inc(sig("c_onehB"), 1)
            dve.tensor_tensor(oneh[:, :, :], pref[:, :, :], wide(col[:, 3, :]), ALU.is_equal).then_inc(sig("c_oneh"), 1)
            dve.tensor_tensor(tmp[:, :, :], logit[:, :, :], wide(col[:, 2, :]), ALU.subtract).then_inc(sig("c_less"), 1)
            dve.wait_ge(sig("c_expl"), 1)
            step(dve.tensor_reduce(col[:, 4, :], expl[:, :, :], X, ALU.add))
            step(dve.reciprocal(gate, col[:, 4, :]))
            dve.wait_ge(sig("c_oneh"), 1)
            step(dve.tensor_tensor(tmp[:, :, :], oneh[:, :, :], row("moe_base"), ALU.mult))
            step(dve.tensor_reduce(col[:, 5, :], tmp[:, :, :], X, ALU.add))
            dve.wait_ge(sig("c_count_ps"), 1)
            step(dve.tensor_tensor(tmp[:, :, :], ps[:, 5, 0:NT * E].rearrange("p (t e) -> p t e", t=NT),
                                   oneh[:, :, :], ALU.mult))
            step(dve.tensor_reduce(col[:, 6, :], tmp[:, :, :], X, ALU.add))
            step(dve.tensor_scalar(col[:, 7, :], col[:, 6, :], float(CAP), float(4 * E * CAP), ALU.is_gt, ALU.mult))
            step(dve.scalar_tensor_tensor(col[:, 3, :], col[:, 6, :], -1.0, col[:, 5, :], ALU.add, ALU.add))
            dve.tensor_tensor(slot, col[:, 3, :], col[:, 7, :], ALU.add).then_inc(sig("c_slot"), 1)
            dve.wait_ge(sig("c_slot"), 1)
            for t in range(NT):
                dve.tensor_scalar(place[:, t, :], core.p("moe_iota"), slot[:, t:t + 1], None, ALU.is_equal)\
                   .then_inc(sig("c_place"), 1)
            dve.wait_ge(sig("c_disp_ps"), 1)
            for k in range(KD):
                for c in range(2):
                    dve.tensor_copy(disp[:, k, c * HALF:(c + 1) * HALF], ps[:, 2 * k + c, :]).then_inc(sig("c_disp"), 1)

            b1 = core.p("moe_b1").rearrange("p (e f) -> p e f", e=E)
            b2 = core.p("moe_b2").rearrange("p (e d) -> p e d", e=E)

            def hidden(i, u, first=False):
                n = RING * i + u
                if not (first and u < 2):
                    dve.wait_ge(sig("c_y_ps"), n - 1)
                for q in range(2):
                    dve.wait_ge(sig("c_hT_ps"), 2 * n + q + 1)
                    bias = b1[:, bass.ds(n, 1), 4 * q:4 * q + 4].rearrange("p a f -> p (a f)")
                    dve.tensor_tensor(hT[:, u % 2, 4 * q:4 * q + 4, :], ps[:, q, :].rearrange("p (f n) -> p f n", f=4),
                                      bias.unsqueeze(2).broadcast_to([P, 4, CAP]), ALU.add).then_inc(sig("c_hT"), 1)

            def output(i, u, first=False):
                n = RING * i + u
                dve.wait_ge(sig("c_y_ps"), n + 1)
                at = bass.ds(n, 1)
                if not (first and u < 2):
                    dve.wait_ge(sig("c_yL"), n - 1)
                dve.tensor_tensor(y[:, u % 2, :], ps[:, 2 + u % 2, 0:D], b2[:, at, :].rearrange("p a d -> p (a d)"),
                                  ALU.add).then_inc(sig("c_y"), 1)
                high, low = (part[h][:, at, :].rearrange("p a d -> p (a d)") for h in range(2))
                dve.wait_ge(sig("c_y"), n + 1)
                dve.tensor_copy(high, y[:, u % 2, :]).then_inc(sig("c_yH"), 1)
                dve.wait_ge(sig("c_yH"), n + 1)
                dve.tensor_tensor(low, y[:, u % 2, :], high.bitcast(F32), ALU.subtract).then_inc(sig("c_yL"), 1)

            experts(dve, hidden, output)
            for t in range(NT):
                dve.wait_ge(sig("c_back_ps"), t // 2 + 1)
                dve.scalar_tensor_tensor(y2[:, t, :], ps[:, 4 + t // 2, (t % 2) * D:(t % 2 + 1) * D], gate[:, t:t + 1],
                                         y1[:, t, :], ALU.mult, ALU.add).then_inc(sig("c_y2"), 1)
            norm_vector(dve, sig, "c_ln", scratch, y2, y2, [(sig("c_y2"), NT)], core.p("ln2_g"), core.p("ln2_b"))
            for t in range(NT):
                dve.wait_ge(sig("c_ln_shifted"), t + 1)
                dve.tensor_tensor(x[:, t, :], x[:, t, :], y2[:, t, :], ALU.add).then_inc(sig("c_x"), 1)


def phase_heads_read(core, x, drams, mean, rstd):
    nc, sig, ps = core.nc, core.sig, core.psum
    PAIRS = H1 // 2
    SE = S + S % 2
    EVEN_QUARTERS = [(0, 402), (402, 400), (802, 400), (1202, 400)]
    SCORED = (SE - 2) // 4 + 2
    QUARTER = SCORED - 2
    ORDER = [("r", g, k) for g in range(4) for k in range(KD)]
    for j in range(7):
        ORDER += [("k", j // 4, j % 4), ("v", j, 0)]
    ORDER += [("k", 1, 3)]
    FILLS, ROWS_END = len(ORDER), 8
    EARLY = 19
    SLOT_FILLS = [[(0, 19), (0, 20)], [(0, 21), (0, 22)]]
    SLOT_FILLS += [[(1, n) for n in range(a, b)] for a, b in ((0, 4), (4, 8), (8, 11), (11, 14), (14, 16), (16, 19))]
    PE_STEPS = ["SW012a3b", "S0a1b23", "S0a1b2c3d", "S0a1b2c3d", "SW0a1b2c3", "S0a1b2c3", "S0a1b23", "S0a1b2c3"]
    ACT_STEPS = ["0Eab", "0aEb", "0abEcd", "0abEcd", "0aEbc", "0abEc", "0aEb", "0aEbc"]
    DVE_STEPS = ["MH12a3b", "M1a2b3", "M1ab23cd", "IM1ab23cd", "MH1a23bc", "M1ab23c", "M1a23b", "IM1a23bc"]
    TURNS, LETTERS = "0123", "abcd"
    QUERIES = ROWS_END + 1
    KEYS_END = ROWS_END + 6
    T_BANK, V_BANK = 4, 7
    PRODUCTS = [(0, 0), (0, 1), (1, 0)]

    def fill_bank(n):
        return 6 + n % 2

    def fill_before(b, n):
        return (b, n - 2) if n >= 2 else (b - 1, FILLS - 1 - n)

    def its_fill(i, u, p, letter, fills):
        these = [(i + (u + ahead) // 2, (u + ahead) % 2, n) for ahead, n in SLOT_FILLS[p] if fills or not ahead]
        return these[LETTERS.index(letter):][:1]

    def is_first(b):
        return isinstance(b, int) and b == 0

    with ExitStack() as ctx:
        params = core.load_pack(ctx, "pd")
        scratch, scratch2, scratch3 = (scratch_of(core, ctx, f"d_ln{i}") for i in range(3))
        wk = core.tensor(ctx, "d_wk", [P, 2, KD, D], F32R)
        wv = core.tensor(ctx, "d_wv", [P, 2, KD, D], F32R)
        bk = core.tensor(ctx, "d_bk", [P, KD])
        bv = core.tensor(ctx, "d_bv", [P, KD])
        rowsN = core.tensor(ctx, "d_rowsN", [P, 2, NC, D])
        rowsT = core.tensor(ctx, "d_rowsT", [P, 2, KD, SE], F32R)
        keys = core.tensor(ctx, "d_keys", [P, KD, 2, SE], F32R)
        val = core.tensor(ctx, "d_val", [P, 2, NC, D])
        moments = core.tensor(ctx, "d_rowmoments", [P, 2, 2, NC])
        QT = core.tensor(ctx, "d_QT", [P, KD, N])
        OT = core.tensor(ctx, "d_OT", [P, KD, N])
        pairq = core.tensor(ctx, "d_pairq", [P, 2, KD, 4, 2, L], F32R)
        tileq = core.tensor(ctx, "d_tileq", [P, 2, KD, L])
        tileqH = core.tensor(ctx, "d_tileqH", [P, 2, 2, KD, L], F32R)
        tileqL = core.tensor(ctx, "d_tileqL", [P, 2, 2, KD, L], F32R)
        exps = core.tensor(ctx, "d_exps", [P, 2, S])
        probT = core.tensor(ctx, "d_probT", [P, 4, NC, P])
        negmax = core.tensor(ctx, "d_negmax", [P, 2])
        sums = core.tensor(ctx, "d_sums", [P, 2, 4, 4])
        total = core.tensor(ctx, "d_total", [P, 4])
        inv = core.tensor(ctx, "d_inv", [P, 4])
        invw, invT, on = (core.p("l1_wk")[:, i * P:(i + 1) * P] for i in range(3))
        even = core.p("l1_wk")[:, 3 * P:3 * P + L]
        fence = core.tensor(ctx, "d_fence", [P, 4])
        early = probT[:, :, :, :].rearrange("p g c n -> p (g c n)")
        nat = early[:, 0:NT * D].rearrange("p (t d) -> p t d", t=NT)
        natT = early[:, NT * D:2 * NT * D].rearrange("p (k n) -> p k n", k=KD)
        late = rowsN[:, :, :, :].rearrange("p u c d -> p (u c d)")
        nat2 = late[:, 0:NT * D].rearrange("p (t d) -> p t d", t=NT)
        res = late[:, NT * D:2 * NT * D].rearrange("p (t d) -> p t d", t=NT)
        QL = L // HD1
        mixed = probT[:, :, :, :].rearrange("p g c n -> p (g c n)")[0:B * QL, 0:H1 * D]\
            .rearrange("p (h r d) -> p h r d", h=H1, r=HD1)
        outT = OT
        block = ctx.enter_context(nc.Block())

        def mixed_pair(f):
            return mixed[:, :, 2 * f:2 * f + 2, :].rearrange("p h r d -> p r h d")

        def bank_pair(f):
            return ps[0:B * QL, f, :].rearrange("p (r h d) -> p r h d", r=2, h=H1)

        def batches(eng, one, last):
            one(0, 0)
            one(0, 1)
            with eng.Fori(1, B // 2 - 1) as i:
                one(i, 0)
                one(i, 1)
            one(B // 2 - 1, 0)
            last()

        def wait(eng, name, value):
            if not (isinstance(value, int) and value <= 0):
                eng.wait_ge(sig(name), value)

        @block.sync
        def _(sp):
            sp.dma_start(params[:, :], drams["pd"]).then_inc(sig("d_params_in"), 16)

            def load(b, u):
                sp.dma_start(rowsN[:, u, :, :], drams["ctx_rows"][bass.ds(b, 1)].rearrange("b (c p) d -> p (b c) d", p=P))\
                  .then_inc(sig(f"d_rows_in{u}"), 16)

            load(0, 0)
            load(1, 1)
            with sp.Fori(1, B // 2) as i:
                for u in range(2):
                    b = 2 * i + u
                    sp.wait_ge(sig("d_fill_ps"), FILLS * (b - 2) + ROWS_END)
                    load(b, u)
            sp.wait_ge(sig("d_mixed_a"), 4)
            sp.wait_ge(sig("d_mixed_d"), 4)
            for q in range(QL):
                sp.dma_start(drams["mixed"].rearrange("b (h q) d -> q b h d", q=QL)[q],
                             mixed[q:B * QL:QL, :, :, :].rearrange("p h r d -> p h (r d)"))\
                  .then_inc(sig("d_mixed_out"), 16)
            sp.wait_ge(sig("d_mixed_out"), 16 * QL)
            sp.dma_start(res, natural(drams["mixed"])).then_inc(sig("d_nat"), 16)

        @block.gpsimd
        def _(pool):
            def moments_of(b, u, first=False):
                pool.wait_ge(sig(f"d_rows_in{u}"), 8 * (b - u) + 16)
                if not first:
                    pool.wait_ge(sig("d_fill_ps"), FILLS * (b - 2) + ROWS_END)
                pool.tensor_tensor(fence[:, 0:1], mean[:, 0:1], mean[:, 0:1], ALU.add)
                for n, src in enumerate((mean, rstd)):
                    last = pool.tensor_copy(moments[:, u, n, :], src[:, bass.ds(b * NC, NC)])
                last.then_inc(sig("d_moments"), 1)
                pool.wait_ge(sig("d_moments"), b)
                pool.tensor_tensor(fence[:, 1:2], mean[:, 0:1], mean[:, 0:1], ALU.add)

            def normalise(u):
                for c in range(NC):
                    pool.tensor_scalar(rowsN[:, u, c, :], rowsN[:, u, c, :], moments[:, u, 0, c:c + 1],
                                       moments[:, u, 1, c:c + 1], ALU.subtract, ALU.mult).then_inc(sig("d_normed"), 1)

            def spread_queries(b, u, m, first=False):
                if not first:
                    pool.wait_ge(sig("d_s_ps"), 4 * PAIRS * (b - 1) + 16 * m + 16)
                wait(pool, "d_pairq", 2 * b + m)
                pool.wait_ge(sig("d_tileq"), b + 1)
                pool.tensor_tensor(fence[:, 2:3], mean[:, 0:1], mean[:, 0:1], ALU.add)
                mask = core.p("head_mask").rearrange("p (a c) -> p a c", a=2)
                for part, q in enumerate((tileqH, tileqL)):
                    out = pairq[:, part, m, :, :, :].rearrange("p g r q -> p (g r) q")
                    for a in range(2):
                        last = pool.tensor_tensor(out[:, 4 * a:4 * a + 4, :],
                                                  q[:, u, a, m, :].bitcast(F32).unsqueeze(1).broadcast_to([P, 4, L]),
                                                  mask[:, a, :].unsqueeze(2).broadcast_to([P, 4, L]), ALU.mult)
                last.then_inc(sig("d_pairq"), 1)

            moments_of(1, 1, first=True)
            normalise(1)
            for m in range(KD):
                spread_queries(0, 0, m, first=True)
            with pool.Fori(1, B // 2) as i:
                for u in range(2):
                    b = 2 * i + u
                    moments_of(b, u)
                    spread_queries(b - 1, 1 - u, 0)
                    normalise(u)
                    spread_queries(b - 1, 1 - u, 1)
            for m in range(KD):
                spread_queries(B - 1, 1, m)

        @block.tensor
        def _(pe):
            pe.wait_ge(sig("d_params_in"), 16)
            for w, col in (("l1_wk", 0), ("l1_wv", 2)):
                for m in range(KD):
                    for k in range(KD):
                        last = pe.matmul(ps[:, V_BANK, col + m:col + m + 1], core.w(w)[:, k, m * P:(m + 1) * P],
                                         core.p("n_bcol")[:, k:k + 1], start=(k == 0), stop=(k == KD - 1))
            last.then_inc(sig("d_shift_ps"), 1)

            def taken(b, n):
                wait(pe, "d_fill", FILLS * b + n + 1)
                kind, m, q = ORDER[n]
                if kind == "k":
                    wait(pe, "d_lows", 8 * b + 4 * m + q + 1)
                elif kind == "r":
                    wait(pe, "d_rowlows", ROWS_END * b + n + 1)

            def fill(i, u, n):
                b = 2 * i + u
                bank = fill_bank(n)
                kind, j, q = ORDER[n]
                taken(*fill_before(b, n))
                if n == ROWS_END + 1:
                    wait(pe, "d_weighed", 2 * (b - 1) + 1)
                elif n == EARLY:
                    wait(pe, "d_weighed", 2 * b)
                elif n == ROWS_END:
                    wait(pe, "d_fill", FILLS * b + ROWS_END)
                    wait(pe, "d_rowlows", ROWS_END * (b + 1))
                if kind == "r":
                    for c in range(4 * j, min(4 * j + 4, NC)):
                        w = P if c < NC - 1 else SL + S % 2
                        if q == 0:
                            if is_first(b):
                                pe.wait_ge(sig("d_normed0"), c + 1)
                            else:
                                wait(pe, "d_normed", NC * (b - 1) + c + 1)
                        last = pe.transpose(ps[:, bank, (c % 4) * P:(c % 4) * P + w],
                                            rowsN[0:w, u, c, q * P:(q + 1) * P], core.p("ident")[0:w, 0:w])
                elif kind == "k":
                    s0, w = EVEN_QUARTERS[q]
                    steps = [(k, a, c) for k in range(KD) for a, c in PRODUCTS]
                    for k, a, c in steps:
                        last = pe.matmul(ps[:, bank, 0:w], wk[:, a, k, j * P:(j + 1) * P], rowsT[:, c, k, s0:s0 + w],
                                         start=((k, a, c) == steps[0]), stop=((k, a, c) == steps[-1]))
                else:
                    for c in range(2 * j, min(2 * j + 2, NC)):
                        w = P if c < NC - 1 else SL + S % 2
                        steps = [(k, e, f) for k in range(KD) for e, f in PRODUCTS]
                        for k, e, f in steps:
                            last = pe.matmul(ps[0:w, bank, (c % 2) * D:(c % 2 + 1) * D],
                                             rowsT[:, f, k, c * P:c * P + w], wv[:, e, k, :],
                                             start=((k, e, f) == steps[0]), stop=((k, e, f) == steps[-1]))
                last.then_inc(sig("d_fill_ps"), 1)

            def score(i, u, p):
                b = 2 * i + u
                n = PAIRS * b + p
                m, g = p // 4, p % 4
                if g == 0:
                    wait(pe, "d_pairq", 2 * b + m + 1)
                    wait(pe, "d_lows", 8 * b + 4 * m + 4)
                for c in range(4):
                    s0 = c * QUARTER
                    wait(pe, "d_exps", 4 * n + c - 3)
                    for part in range(2):
                        last = pe.matmul(ps[:, c, 0:SCORED], pairq[:, part, m, g, :, :],
                                         keys[:, m, g // 2, s0:s0 + SCORED],
                                         start=(part == 0), stop=(part == 1))
                    last.then_inc(sig("d_s_ps"), 1)

            def turn(i, u, p, t):
                n = PAIRS * (2 * i + u) + p
                if t == 0:
                    wait(pe, "d_exps", 4 * n + 4)
                if t == 2:
                    wait(pe, "d_probT_a", n + 1)
                else:
                    wait(pe, "d_probT_d", 3 * n + (-1, 0, None, 1)[t])
                if t == 3 and p % 4 == 3:
                    wait(pe, "d_invw", 2 * (2 * i + u) + p // 4 + 1)
                    pe.matmul(ps[:, T_BANK + 1, P:2 * P], invw[:, :], core.p("ident"), start=True, stop=True)
                for c in range(4 * t, min(4 * t + 4, NC)):
                    w = P if c < NC - 1 else SL
                    last = pe.transpose(ps[0:w, T_BANK + t % 2, (c % 4) * P:(c % 4 + 1) * P],
                                        exps[:, p % 2, c * P:c * P + w], core.p("ident"))
                last.then_inc(sig("d_probT_ps"), 1)

            def weigh(b, u, m, fills):
                quad = 2 * b + m
                if fills:
                    taken(b + 1, (ROWS_END - 1, EARLY - 2)[m])
                wait(pe, "d_weighed", quad)
                wait(pe, "d_probT_a", 4 * quad + 4)
                wait(pe, "d_probT_d", 12 * quad + 12)
                wait(pe, "d_fill", FILLS * b + FILLS - 1)
                for c in range(NC):
                    w = P if c < NC - 1 else SL
                    for g in range(4):
                        f = m * P + 32 * g
                        last = pe.matmul(ps[32 * g:32 * g + 32, V_BANK, m * P:(m + 1) * P], val[0:w, u, c, f:f + 32],
                                         probT[0:w, g, c, :], start=(c == 0), stop=(c == NC - 1),
                                         tile_position=(0, 32 * g))
                last.then_inc(sig("d_weigh_ps"), 1)

            def batch(i, u, fills=True):
                nxt = (i, 1) if u == 0 else (i + 1, 0)
                b = 2 * i + u
                for p in range(PAIRS):
                    for step in PE_STEPS[p]:
                        if step == "S" and p + 1 < PAIRS:
                            score(i, u, p + 1)
                        elif step == "S" and fills:
                            score(*nxt, 0)
                        elif step == "W" and p == 4:
                            weigh(b, u, 0, fills)
                        elif step == "W" and not is_first(b):
                            weigh(b - 1, 1 - u, 1, True)
                        elif step in TURNS:
                            turn(i, u, p, TURNS.index(step))
                        elif step in LETTERS:
                            for f in its_fill(i, u, p, step, fills):
                                fill(*f)

            pe.wait_ge(sig("d_weights"), 8)
            pe.wait_ge(sig("d_shift"), 2)
            for n in range(EARLY):
                fill(0, 0, n)
                if n == QUERIES:
                    turn_tensor(pe, core, "d_natT", nat, 0, [(sig("d_ln1_out"), True)])
                    project_tensor(pe, core, "d_QT", core.w("l1_wq"), natT, 0, "d_natT", ready=both(sig, "d_natT"))
                elif n == KEYS_END:
                    for s, v in both(sig, "d_QT"):
                        pe.wait_ge(s, v)
                    score(0, 0, 0)
            batches(pe, batch, lambda: batch(B // 2 - 1, 1, fills=False))
            weigh(B - 1, 1, 1, False)
            pe.wait_ge(sig("d_out"), 2)
            for r in range(HD1):
                for m in range(KD):
                    last = pe.transpose(ps[0:B * QL, r // 2, (r % 2) * D + m * P:(r % 2) * D + (m + 1) * P],
                                        OT[:, m, r:N:HD1], core.p("ident"))
                if r % 2:
                    last.then_inc(sig("d_mixed_ps"), 1)
            turn_tensor(pe, core, "d_outT", nat2, 4, [(sig("d_ln2_out"), True)])
            rows_tensor(pe, core, "d_proj", outT, core.w("l1_wo"), 0, both(sig, "d_outT"))

        @block.scalar
        def _(act):
            def take_fill(i, u, n):
                b = 2 * i + u
                bank = fill_bank(n)
                kind, j, q = ORDER[n]
                wait(act, "d_fill_ps", FILLS * b + n + 1)
                if kind == "r":
                    w = min(4 * P, SE - 4 * P * j)
                    act.activation(rowsT[:, 0, q, 4 * P * j:4 * P * j + w], ps[:, bank, 0:w], ACT.Copy)\
                       .then_inc(sig("d_fill"), 1)
                elif kind == "k":
                    s0, w = EVEN_QUARTERS[q]
                    for half in range(2):
                        r = slice(64 * half, 64 * half + 64)
                        last = act.activation(keys[r, j, half, s0:s0 + w], ps[r, bank, 0:w], ACT.Identity,
                                              bias=bk[r, j:j + 1])
                    last.then_inc(sig("d_fill"), 1)
                else:
                    c = 2 * j
                    if c + 1 < NC:
                        act.activation(val[:, u, c:c + 2, :], two(ps[:, bank, :]), ACT.Copy).then_inc(sig("d_fill"), 1)
                    else:
                        act.activation(val[0:SL, u, c, :], ps[0:SL, bank, 0:D], ACT.Copy).then_inc(sig("d_fill"), 1)

            def exp(i, u, p, c):
                n = PAIRS * (2 * i + u) + p
                s0 = c * QUARTER
                w = QUARTER if c < 3 else S - s0
                if c == 0:
                    wait(act, "d_negmax", n + 1)
                    wait(act, "d_probT_ps", 4 * (n - 1))
                act.activation(exps[:, p % 2, s0:s0 + w], ps[:, c, 0:w], ACT.Exp, bias=negmax[:, p % 2:p % 2 + 1],
                               accum_out=sums[:, p // 4, p % 4, c:c + 1]).then_inc(sig("d_exps"), 1)

            def take_first(i, u, p):
                if p % 4 == 0:
                    wait(act, "d_weigh_ps", 2 * (2 * i + u) + p // 4)
                wait(act, "d_probT_ps", 4 * (PAIRS * (2 * i + u) + p) + 1)
                act.activation(probT[:, p % 4, 0:4, :], ps[:, T_BANK, :].rearrange("p (c n) -> p c n", c=4),
                               ACT.Copy).then_inc(sig("d_probT_a"), 1)

            def batch(i, u, fills=True):
                nxt = (i, 1) if u == 0 else (i + 1, 0)
                for p in range(PAIRS):
                    for step in ACT_STEPS[p]:
                        if step == "0":
                            take_first(i, u, p)
                        elif step == "E":
                            for c in range(4):
                                if p + 1 < PAIRS:
                                    exp(i, u, p + 1, c)
                                elif fills:
                                    exp(*nxt, 0, c)
                        else:
                            for f in its_fill(i, u, p, step, fills):
                                take_fill(*f)

            norm_scalar(act, sig, "d_ln0", scratch)
            for n in range(EARLY):
                if n == ROWS_END:
                    act.wait_ge(sig("d_shift"), 2)
                take_fill(0, 0, n)
                if n == QUERIES:
                    norm_scalar(act, sig, "d_ln1", scratch2)
                    turn_scalar(act, core, "d_natT", natT, 0, affine=(core.p("n_wcol"), core.p("n_bcol")))
                    project_scalar(act, core, "d_QT", QT, 0, core.p("l1_bq"))
                elif n == KEYS_END + 2:
                    for c in range(4):
                        exp(0, 0, 0, c)
            batches(act, batch, lambda: batch(B // 2 - 1, 1, fills=False))
            for f in range(0, HD1 // 2, 2):
                act.wait_ge(sig("d_mixed_ps"), f + 1)
                act.activation(mixed_pair(f), bank_pair(f), ACT.Copy).then_inc(sig("d_mixed_a"), 1)
            norm_scalar(act, sig, "d_ln2", scratch3)
            turn_scalar(act, core, "d_outT", outT, 4, affine=(core.p("n1_wcol"), core.p("n1_bcol")))

        @block.vector
        def _(dve):
            norm_vector(dve, sig, "d_ln0", scratch, x, nat)
            dve.wait_ge(sig("d_rows_in0"), 16)
            for c in range(NC):
                dve.tensor_scalar(rowsN[:, 0, c, :], rowsN[:, 0, c, :], mean[:, c:c + 1], rstd[:, c:c + 1],
                                  ALU.subtract, ALU.mult).then_inc(sig("d_normed0"), 1)
            dve.wait_ge(sig("d_params_in"), 16)
            for n, (dst, w) in enumerate(((wk, "l1_wk"), (wv, "l1_wv"))):
                for k in range(KD):
                    dve.tensor_scalar(dst[:, 0, k, :], core.w(w)[:, k, :], core.p("n_wcol")[:, k:k + 1], None, ALU.mult)\
                       .then_inc(sig("d_weights"), 1)
                for k in range(KD):
                    dve.wait_ge(sig("d_weights"), 4 * n + k + 1)
                    dve.scalar_tensor_tensor(dst[:, 1, k, :], core.w(w)[:, k, :], core.p("n_wcol")[:, k:k + 1],
                                             dst[:, 0, k, :].bitcast(F32), ALU.mult, ALU.subtract)\
                       .then_inc(sig("d_weights"), 1)
            dve.wait_ge(sig("d_shift_ps"), 1)
            dve.tensor_tensor(bk[:, :], ps[:, V_BANK, 0:2], core.p("l1_bk"), ALU.add).then_inc(sig("d_shift"), 1)
            dve.tensor_tensor(bv[:, :], ps[:, V_BANK, 2:4], core.p("l1_bv"), ALU.add).then_inc(sig("d_shift"), 1)

            def top_of(i, u, p):
                n = PAIRS * (2 * i + u) + p
                wait(dve, "d_s_ps", 4 * n + 4)
                wait(dve, "d_exps", 4 * (n - 1))
                wait(dve, "d_negmax", n - 1)
                dve.tensor_reduce(negmax[:, p % 2:p % 2 + 1], ps[:, 0:4, 0:SCORED], XY, ALU.max, negate=True)\
                   .then_inc(sig("d_negmax"), 1)

            def take_turn(i, u, p, t):
                n = PAIRS * (2 * i + u) + p
                if t == 1 and p % 4 == 0:
                    wait(dve, "d_weigh_ps", 2 * (2 * i + u) + p // 4)
                wait(dve, "d_probT_ps", 4 * n + t + 1)
                g = p % 4
                if t < 3:
                    dve.tensor_copy(probT[:, g, 4 * t:4 * t + 4, :], ps[:, T_BANK + t % 2, :].rearrange("p (c n) -> p c n", c=4))\
                       .then_inc(sig("d_probT_d"), 1)
                else:
                    if g == 3:
                        wait(dve, "d_weighed", 2 * (2 * i + u) + p // 4)
                        dve.tensor_copy(invT[:, :], ps[:, T_BANK + 1, P:2 * P]).then_inc(sig("d_invT"), 1)
                    dve.tensor_copy(probT[0:SL, g, NC - 1, :], ps[0:SL, T_BANK + 1, 0:P]).then_inc(sig("d_probT_d"), 1)

            def take_rowlows(i, u, n):
                b = 2 * i + u
                _, j, k = ORDER[n]
                w = min(4 * P, SE - 4 * P * j)
                cols = slice(4 * P * j, 4 * P * j + w)
                wait(dve, "d_fill", FILLS * b + n + 1)
                dve.tensor_tensor(rowsT[:, 1, k, cols], ps[:, fill_bank(n), 0:w], rowsT[:, 0, k, cols].bitcast(F32),
                                  ALU.subtract).then_inc(sig("d_rowlows"), 1)

            def take_lows(i, u, m, q):
                b = 2 * i + u
                n = ORDER.index(("k", m, q))
                bank = fill_bank(n)
                s0, w = EVEN_QUARTERS[q]
                wait(dve, "d_fill", FILLS * b + n + 1)
                for half in range(2):
                    r, o = slice(64 * half, 64 * half + 64), slice(64 - 64 * half, 128 - 64 * half)
                    last = dve.scalar_tensor_tensor(keys[o, m, half, s0:s0 + w], ps[r, bank, 0:w], bk[r, m:m + 1],
                                                    keys[r, m, half, s0:s0 + w].bitcast(F32), ALU.add, ALU.subtract)
                last.then_inc(sig("d_lows"), 1)

            def take_low(i, u, n):
                kind, m, q = ORDER[n]
                if kind == "r":
                    take_rowlows(i, u, n)
                elif kind == "k":
                    take_lows(i, u, m, q)

            def tile_queries(i, u):
                b = 2 * i + u
                wait(dve, "d_pairq", b - 1)
                wait(dve, "d_tileq", b)
                cols = bass.ds(b * L, L)
                for a in range(2):
                    src = slice(64 * a, 64 * a + 64)
                    for o in (slice(0, 64), slice(64, 128)):
                        dve.tensor_copy(tileq[o, a, :, :], QT[src, :, cols]).then_inc(sig("d_tileq_whole"), 1)
                wait(dve, "d_tileq_whole", 4 * b + 4)
                dve.tensor_copy(tileqH[:, u, :, :, :], tileq[:, :, :, :]).then_inc(sig("d_tileqH"), 1)
                wait(dve, "d_tileqH", b + 1)
                dve.tensor_tensor(tileqL[:, u, :, :, :], tileq[:, :, :, :], tileqH[:, u, :, :, :].bitcast(F32),
                                  ALU.subtract).then_inc(sig("d_tileq"), 1)

            def inverses(i, u, m):
                quad = 2 * (2 * i + u) + m
                wait(dve, "d_exps", 4 * PAIRS * (2 * i + u) + 16 * m + 16)
                dve.tensor_reduce(total[:, :], sums[:, m, :, :], X, ALU.add).then_inc(sig("d_total"), 1)
                wait(dve, "d_total", quad + 1)
                dve.reciprocal(inv[:, :], total[:, :]).then_inc(sig("d_inv"), 1)
                wait(dve, "d_inv", quad + 1)
                dve.tensor_copy(invw[:, :].rearrange("p (g n) -> p g n", g=4),
                                inv[:, :].unsqueeze(2).broadcast_to([P, 4, 32])).then_inc(sig("d_invw"), 1)

            def take_heads(b, m):
                quad = 2 * b + m
                wait(dve, "d_invT", quad + 1)
                wait(dve, "d_weigh_ps", quad + 1)
                dve.tensor_tensor(on[:, :], ps[:, V_BANK, m * P:(m + 1) * P], invT[:, :], ALU.mult)\
                   .then_inc(sig("d_weighed"), 1)
                wait(dve, "d_weighed", quad + 1)
                dve.tensor_scalar(even[:, :], on[:, 0:L], core.p("parity")[:, 0:1], None, ALU.mult)\
                   .then_inc(sig("d_even"), 1)
                wait(dve, "d_even", quad + 1)
                dve.scalar_tensor_tensor(OT[:, m, bass.ds(b * L, L)], on[:, L:2 * L], core.p("parity")[:, 1:2],
                                         even[:, :], ALU.mult, ALU.add).then_inc(sig("d_OT"), 1)

            def batch(i, u, fills=True):
                b = 2 * i + u
                nxt = (i, 1) if u == 0 else (i + 1, 0)
                for p in range(PAIRS):
                    for step in DVE_STEPS[p]:
                        if step == "I":
                            inverses(i, u, p // 4)
                        elif step == "M" and p + 1 < PAIRS:
                            top_of(i, u, p + 1)
                        elif step == "M" and fills:
                            top_of(*nxt, 0)
                        elif step == "H" and p == 4:
                            take_heads(b, 0)
                        elif step == "H" and not is_first(b):
                            take_heads(b - 1, 1)
                        elif step in TURNS:
                            take_turn(i, u, p, TURNS.index(step))
                        elif step in LETTERS:
                            for f in its_fill(i, u, p, step, fills):
                                take_low(*f)
                    if p == 4 and not (isinstance(i, int) and i + 1 == B // 2):
                        tile_queries(i + 1, u)

            for n in range(EARLY):
                take_low(0, 0, n)
                if n == ROWS_END:
                    norm_vector(dve, sig, "d_ln1", scratch2, nat, nat, [(sig("d_ln0_out"), NT)])
                    turn_vector(dve, core, "d_natT", natT, 0, affine=(core.p("n_wcol"), core.p("n_bcol")))
                    project_vector(dve, core, "d_QT", QT, 0, core.p("l1_bq"))
                    for s, v in both(sig, "d_QT"):
                        dve.wait_ge(s, v)
                    tile_queries(0, 0)
                    tile_queries(0, 1)
                elif n == KEYS_END + 1:
                    top_of(0, 0, 0)
            dve.wait_ge(sig("d_weights"), 8)
            batches(dve, batch, lambda: batch(B // 2 - 1, 1, fills=False))
            take_heads(B - 1, 1)
            dve.wait_ge(sig("d_OT"), 2 * B)
            for m in range(KD):
                dve.scalar_tensor_tensor(OT[:, m, :], OT[:, m, :], bv[:, m:m + 1], QT[:, m, :], ALU.add, ALU.add)\
                   .then_inc(sig("d_out"), 1)
            for f in range(1, HD1 // 2, 2):
                dve.wait_ge(sig("d_mixed_ps"), f + 1)
                dve.tensor_copy(mixed_pair(f), bank_pair(f)).then_inc(sig("d_mixed_d"), 1)
            norm_vector(dve, sig, "d_ln2", scratch3, res, nat2, [(sig("d_nat"), 16)])
            turn_vector(dve, core, "d_outT", outT, 4, affine=(core.p("n1_wcol"), core.p("n1_bcol")))
            for t in range(NT):
                dve.tensor_tensor(res[:, t, :], res[:, t, :], core.p("l1_bo"), ALU.add).then_inc(sig("d_res"), 1)
            for i in range(NT // 2):
                dve.wait_ge(sig("d_proj_ps"), i + 1)
                dve.wait_ge(sig("d_res"), 2 * i + 2)
                dve.tensor_tensor(res[:, 2 * i:2 * i + 2, :], two(ps[:, i, :]), res[:, 2 * i:2 * i + 2, :], ALU.add)\
                   .then_inc(sig("d_sum"), 1)
                dve.wait_ge(sig("d_sum"), i + 1)
                dve.tensor_tensor(x[:, 2 * i:2 * i + 2, :], x[:, 2 * i:2 * i + 2, :], res[:, 2 * i:2 * i + 2, :], ALU.add)\
                   .then_inc(sig("d_x"), 1)


def phase_features(core, x, drams):
    nc, sig, ps = core.nc, core.sig, core.psum
    with ExitStack() as ctx:
        params = core.load_pack(ctx, "pe")
        scratch = scratch_of(core, ctx, "e_ln")
        xn = core.tensor(ctx, "e_xn", [P, NT, D])
        xnT = core.tensor(ctx, "e_xnT", [P, KD, N])
        sqT = core.tensor(ctx, "e_sqT", [P, KD, N])
        wsqT = core.tensor(ctx, "e_wsqT", [P, KD, D])
        gw = core.tensor(ctx, "e_gw", [P, KD, D])
        half = core.tensor(ctx, "e_half", [P, D])
        amp = core.tensor(ctx, "e_amp", [P, 2, KD])
        feats = core.tensor(ctx, "e_feats", [P, KD, N])
        wfeats = core.tensor(ctx, "e_wfeats", [P, KD, D])
        block = ctx.enter_context(nc.Block())

        @block.sync
        def _(sp):
            sp.dma_start(params[:, :], drams["pe"]).then_inc(sig("e_params_in"), 16)

        def exponent(pe, bank, m, rhs, square, width):
            for k in range(KD):
                pe.matmul(ps[:, bank, 0:width], gw[:, k, m * P:(m + 1) * P], rhs[:, k], start=(k == 0), stop=False)
            for k in range(KD):
                last = pe.matmul(ps[:, bank, 0:width], half[:, m * P:(m + 1) * P], square[:, k], start=False,
                                 stop=(k == KD - 1))
            return last

        @block.tensor
        def _(pe):
            pe.wait_ge(sig("e_gw"), KD)
            pe.wait_ge(sig("e_half"), 1)
            pe.wait_ge(sig("e_wsqT"), 1)
            for m in range(KD):
                exponent(pe, 4 + m, m, core.w("rf_iwT"), wsqT, D).then_inc(sig("e_wexp_ps"), 1)
            turn_tensor(pe, core, "e_xnT", xn, 0, [(sig("e_ln_out"), True)])
            pe.wait_ge(sig("e_wfeats_raw"), KD)
            for c in range(2):
                for s, n in both(sig, "e_xnT", c + 1):
                    pe.wait_ge(s, n)
                pe.wait_ge(sig("e_sqT"), c + 1)
                cols = slice(c * HALF, (c + 1) * HALF)
                for m in range(KD):
                    exponent(pe, 4 + 2 * c + m, m, xnT[:, :, cols], sqT[:, :, cols], HALF).then_inc(sig("e_exp_ps"), 1)
            pe.wait_ge(sig("e_wfeats"), KD)
            rows_tensor(pe, core, "e_out", feats, wfeats, 0, [(sig("e_feats"), 4)])

        @block.scalar
        def _(act):
            norm_scalar(act, sig, "e_ln", scratch)
            act.wait_ge(sig("e_params_in"), 16)
            act.activation(amp[:, 0, :], core.p("rf_abcol"), ACT.Exp).then_inc(sig("e_amp"), 1)
            for m in range(KD):
                act.wait_ge(sig("e_wexp_ps"), m + 1)
                act.activation(wfeats[:, m, :], ps[:, 4 + m, 0:D], ACT.Exp).then_inc(sig("e_wfeats_raw"), 1)
            turn_scalar(act, core, "e_xnT", xnT, 0)
            for i in range(4):
                act.wait_ge(sig("e_exp_ps"), i + 1)
                act.activation(feats[:, i % 2, (i // 2) * HALF:(i // 2 + 1) * HALF], ps[:, 4 + i, :], ACT.Exp)\
                   .then_inc(sig("e_feats_raw"), 1)

        @block.vector
        def _(dve):
            dve.wait_ge(sig("e_params_in"), 16)
            ab = core.p("rf_ab")
            dve.tensor_tensor(half[:, :], ab, ab, ALU.mult).then_inc(sig("e_absq"), 1)
            dve.wait_ge(sig("e_absq"), 1)
            dve.tensor_scalar(half[:, :], half[:, :], -0.5, None, ALU.mult).then_inc(sig("e_half"), 1)
            for k in range(KD):
                dve.tensor_tensor(gw[:, k, :], core.w("rf_gsT")[:, k, :], ab, ALU.mult).then_inc(sig("e_gw"), 1)
            dve.tensor_tensor(wsqT[:, :, :], core.w("rf_iwT"), core.w("rf_iwT"), ALU.mult).then_inc(sig("e_wsqT"), 1)
            norm_vector(dve, sig, "e_ln", scratch, x, xn)
            dve.wait_ge(sig("e_amp"), 1)
            dve.tensor_scalar(amp[:, 1, :], amp[:, 0, :], 256.0 ** -0.5, None, ALU.mult).then_inc(sig("e_amp2"), 1)
            dve.wait_ge(sig("e_amp2"), 1)
            for m in range(KD):
                dve.wait_ge(sig("e_wfeats_raw"), m + 1)
                dve.tensor_scalar(wfeats[:, m, :], wfeats[:, m, :], amp[:, 1, m:m + 1], None, ALU.mult)\
                   .then_inc(sig("e_wfeats"), 1)
            turn_vector(dve, core, "e_xnT", xnT, 0)
            for c in range(2):
                for s, n in both(sig, "e_xnT", c + 1):
                    dve.wait_ge(s, n)
                cols = slice(c * HALF, (c + 1) * HALF)
                dve.tensor_tensor(sqT[:, :, cols], xnT[:, :, cols], xnT[:, :, cols], ALU.mult).then_inc(sig("e_sqT"), 1)
            for i in range(4):
                cols = slice((i // 2) * HALF, (i // 2 + 1) * HALF)
                dve.wait_ge(sig("e_feats_raw"), i + 1)
                dve.tensor_scalar(feats[:, i % 2, cols], feats[:, i % 2, cols], amp[:, 1, i % 2:i % 2 + 1], None,
                                  ALU.mult).then_inc(sig("e_feats"), 1)
            for i in range(NT // 2):
                dve.wait_ge(sig("e_out_ps"), i + 1)
                dve.tensor_tensor(x[:, 2 * i:2 * i + 2, :], x[:, 2 * i:2 * i + 2, :], two(ps[:, i, :]), ALU.add)\
                   .then_inc(sig("e_x"), 1)


def phase_trees(core, x, drams):
    nc, sig, ps = core.nc, core.sig, core.psum
    HC = 8
    with ExitStack() as ctx:
        params = core.load_pack(ctx, "pf")
        scratch = scratch_of(core, ctx, "f_ln")
        WIDE = 2 * D * NLEAF * 64 // P
        PIECE = WIDE // 4
        raw = core.tensor(ctx, "f_raw", [P, 2, WIDE])
        wH = core.tensor(ctx, "f_wH", [P, 2, WIDE], F32R)
        wL = core.tensor(ctx, "f_wL", [P, 2, WIDE], F32R)
        xnT = raw[:, 1, 0:KD * N].rearrange("p (k n) -> p k n", k=KD)
        xn = raw[:, 1, KD * N:].rearrange("p (t d) -> p t d", t=NT)
        xT = [core.tensor(ctx, f"f_xT{c}", [P, KD, N], F32R) for c in "HL"]
        right = core.tensor(ctx, "f_right", [P, NT, TREES, NNODE])
        levels = [core.tensor(ctx, f"f_level{d}", [P, NT, TREES, 2 ** d]) for d in range(1, DEPTH + 1)]
        leaf = levels[-1]
        leafT = core.tensor(ctx, "f_leafT", [NLEAF, TREES, N], F32R)
        leafB = core.tensor(ctx, "f_leafB", [NLEAF, TREES, N], BF16)
        member = core.tensor(ctx, "f_member", [NLEAF, HC, P], BF16)
        own = core.tensor(ctx, "f_own", [P, 2, HALF])
        ownS = [core.tensor(ctx, f"f_own{c}", [P, 3, HALF], F32R) for c in "HL"]
        outT = core.tensor(ctx, "f_outT", [P, TREES, KD, N])
        val = raw[:, 1, 0:NT * D].rearrange("p (t d) -> p t d", t=NT)
        s, s1 = (raw[:, 1, (2 + i) * N:(3 + i) * N].rearrange("p (i t n) -> p i t n", i=2, t=4) for i in range(2))
        prob = raw[:, 0, 0:N].rearrange("p (i t n) -> p i t n", i=2, t=4)
        probT = raw[:, 0, N:2 * N].rearrange("p (t n) -> p t n", t=NT)
        negmax = core.tensor(ctx, "f_negmax", [P, NT])
        total = core.tensor(ctx, "f_total", [P, NT])
        inv = core.tensor(ctx, "f_inv", [P, NT])
        b1 = core.p("ff_b1").rearrange("p (j c) -> p j c", j=TREES)
        b2 = [core.tensor(ctx, f"f_b2{c}", [NLEAF, TREES * D], F32R) for c in "HL"]
        PRODUCTS = [(0, 0), (0, 1), (1, 0)]

        def w1(j, part, k, h):
            at = k * NLEAF * 64 + h * P
            return (wH, wL)[part][:, j % 2, at:at + P]

        def w2(j, part, h, m):
            at = WIDE // 2 + h * D + m * P
            return (wH, wL)[part][:, j % 2, at:at + P]

        def piece(tensor, j, q):
            return tensor[:, j % 2, q * PIECE:(q + 1) * PIECE]

        NN = TREES * NNODE
        work = [(j, c, h) for j in range(TREES) for c in range(2) for h in range(HC)]
        block = ctx.enter_context(nc.Block())

        @block.sync
        def _(sp):
            sp.dma_start(params[:, :], drams["pf"]).then_inc(sig("f_params_in"), 16)
            for j in range(TREES):
                if j == 1:
                    sp.wait_ge(sig("f_xL"), KD)
                    sp.wait_ge(sig("f_node_ps"), 1)
                elif j > 1:
                    sp.wait_ge(sig("f_wL"), 4 * (j - 1))
                sp.dma_start(raw[:, j % 2, :], drams["trees"][j]).then_inc(sig(f"f_raw_in{j % 2}"), 16)

        @block.gpsimd
        def _(pool):
            def weights(j):
                for q in range(4):
                    pool.wait_ge(sig("f_wH"), 4 * j + q + 1)
                    pool.tensor_tensor(piece(wL, j, q), piece(raw, j, q), piece(wH, j, q).bitcast(F32), ALU.subtract)\
                        .then_inc(sig("f_wL"), 1)

            weights(0)
            for k in range(KD):
                pool.wait_ge(sig("f_xH"), k + 1)
                pool.tensor_tensor(xT[1][:, k, :], xnT[:, k, :], xT[0][:, k, :].bitcast(F32), ALU.subtract)\
                    .then_inc(sig("f_xL"), 1)
            pool.wait_ge(sig("f_b2H"), 1)
            pool.tensor_tensor(b2[1][:, :], core.p("ff_b2")[0:NLEAF, :], b2[0][:, :].bitcast(F32), ALU.subtract)\
                .then_inc(sig("f_b2L"), 1)
            for j in range(1, TREES):
                if j > 1:
                    pool.wait_ge(sig("f_second_ps"), 16 * (j - 1))
                weights(j)

        @block.tensor
        def _(pe):
            pe.wait_ge(sig("f_params_in"), 16)
            turn_tensor(pe, core, "f_xnT", xn, 0, [(sig("f_ln_out"), True)])
            for c in range(2):
                for sm, n in both(sig, "f_xnT", c + 1):
                    pe.wait_ge(sm, n)
                for t in range(4 * c, 4 * c + 4):
                    for k in range(KD):
                        last = pe.matmul(ps[:, 4, t * NN:(t + 1) * NN], xnT[:, k, t * P:(t + 1) * P],
                                         core.w("ff_nodes")[:, k, :], start=(k == 0), stop=(k == KD - 1))
            last.then_inc(sig("f_node_ps"), 1)
            pe.wait_ge(sig("f_leaf"), 1)
            for j in range(TREES):
                for c in range(2):
                    n = 2 * j + c
                    if n >= 2:
                        pe.wait_ge(sig("f_leafT"), n - 1)
                    for q in range(4):
                        last = pe.transpose(ps[0:NLEAF, 5 + n % 2, q * P:(q + 1) * P], leaf[:, 4 * c + q, j, :],
                                            core.p("ident"))
                    last.then_inc(sig("f_leafT_ps"), 1)
            pe.wait_ge(sig("f_leafT"), 2 * TREES)
            pe.wait_ge(sig("f_leafB"), 2 * TREES)
            pe.wait_ge(sig("f_member"), 1)

            pe.wait_ge(sig("f_xL"), KD)
            pe.wait_ge(sig("f_b2L"), 1)

            def first(n):
                j, c, h = work[n]
                cols = slice(c * HALF, (c + 1) * HALF)
                if c == 0 and h == 0:
                    pe.wait_ge(sig("f_wL"), 4 * j + 4)
                if n >= 4:
                    pe.wait_ge(sig("f_ownH"), n - 3)
                    pe.wait_ge(sig("f_own"), n - 3)
                for k in range(KD):
                    for a, b in PRODUCTS:
                        pe.matmul(ps[:, n % 4, :], w1(j, a, k, h), xT[b][:, k, cols],
                                  start=(k == 0 and (a, b) == PRODUCTS[0]), stop=False)
                pe.matmul(ps[:, n % 4, :], member[:, h, :], leafB[:, j, cols], start=False, stop=True)\
                  .then_inc(sig("f_hid_ps"), 1)

            def second(n):
                j, c, h = work[n]
                cols = slice(c * HALF, (c + 1) * HALF)
                if h == 0:
                    if j:
                        pe.wait_ge(sig("f_outT"), 2 * (2 * (j - 1) + c) + 2)
                    for m in range(KD):
                        for part in range(2):
                            at = j * D + m * P
                            pe.matmul(ps[:, 4 + 2 * c + m, :], b2[part][:, at:at + P], leafT[:, j, cols],
                                      start=(part == 0), stop=False)
                pe.wait_ge(sig("f_ownL"), n + 1)
                for m in range(KD):
                    for a, b in PRODUCTS:
                        last = pe.matmul(ps[:, 4 + 2 * c + m, :], w2(j, a, h, m), ownS[b][:, n % 3, :],
                                         start=False, stop=(h == HC - 1 and (a, b) == PRODUCTS[-1]))
                last.then_inc(sig("f_second_ps"), 1)

            first(0)
            first(1)
            for n in range(len(work)):
                if n + 2 < len(work):
                    first(n + 2)
                second(n)
            pe.wait_ge(sig("f_outT"), 4 * TREES)
            for t in range(NT):
                for m in range(KD):
                    last = pe.transpose(ps[:, t // 2, (t % 2) * D + m * P:(t % 2) * D + (m + 1) * P],
                                        outT[:, 2, m, t * P:(t + 1) * P], core.p("ident"))
                if t % 2:
                    last.then_inc(sig("f_val_ps"), 1)
            for t in range(NT):
                for m in range(KD):
                    last = pe.matmul(ps[:, 4 + t // 4, (t % 4) * P:(t % 4 + 1) * P], outT[:, 0, m, t * P:(t + 1) * P],
                                     outT[:, 1, m, t * P:(t + 1) * P], start=(m == 0), stop=(m == KD - 1))
                if t % 4 == 3:
                    last.then_inc(sig("f_s_ps"), 1)
            for i in range(2):
                pe.wait_ge(sig("f_prob"), i + 1)
                for q in range(4):
                    last = pe.transpose(ps[:, 6 + i, q * P:(q + 1) * P], prob[:, i, q, :], core.p("ident"))
                last.then_inc(sig("f_probT_ps"), 1)
            pe.wait_ge(sig("f_val"), NT // 2)
            for t in range(NT):
                pe.wait_ge(sig("f_probT"), t // 4 + 1)
                last = pe.matmul(ps[:, t // 2, (t % 2) * D:(t % 2 + 1) * D], probT[:, t, :], val[:, t, :],
                                 start=True, stop=True)
                if t % 2:
                    last.then_inc(sig("f_out_ps"), 1)

        @block.scalar
        def _(act):
            act.wait_ge(sig("f_params_in"), 16)
            act.activation(member[:, :, :], core.p("ff_leaf")[0:NLEAF, :].rearrange("p (c n) -> p c n", c=HC), ACT.Copy)\
               .then_inc(sig("f_member"), 1)
            norm_scalar(act, sig, "f_ln", scratch)
            turn_scalar(act, core, "f_xnT", xnT, 0)

            def split_weights(j, q):
                act.wait_ge(sig(f"f_raw_in{j % 2}"), 16 * (j // 2) + 16)
                if j > 1:
                    act.wait_ge(sig("f_second_ps"), 16 * (j - 1))
                act.activation(piece(wH, j, q), piece(raw, j, q), ACT.Copy).then_inc(sig("f_wH"), 1)

            for q in range(4):
                split_weights(0, q)
            for n, sm in ((0, "f_xnT_a"), (1, "f_xnT_d")):
                act.wait_ge(sig(sm), 2)
                act.activation(xT[0][:, n, :], xnT[:, n, :], ACT.Copy).then_inc(sig("f_xH"), 1)
            act.activation(b2[0][:, :], core.p("ff_b2")[0:NLEAF, :], ACT.Copy).then_inc(sig("f_b2H"), 1)
            for j in range(TREES):
                for c in range(2):
                    cols = slice(c * HALF, (c + 1) * HALF)
                    act.wait_ge(sig("f_leafT"), 2 * j + c + 1)
                    act.activation(leafB[:, j, cols], leafT[:, j, cols].bitcast(F32), ACT.Copy).then_inc(sig("f_leafB"), 1)
            SPLITS = (3, 6, 11, 14)

            def take_out(last):
                j, c, _ = last
                act.wait_ge(sig("f_second_ps"), 16 * j + 8 * c + 8)
                for m in range(KD):
                    act.activation(outT[:, j, m, c * HALF:(c + 1) * HALF], ps[:, 4 + 2 * c + m, :], ACT.Copy)\
                       .then_inc(sig("f_outT"), 1)

            for n, (j, c, h) in enumerate(work):
                act.wait_ge(sig("f_hid_ps"), n + 1)
                if n >= 3:
                    act.wait_ge(sig("f_second_ps"), n - 2)
                act.activation(ownS[0][:, n % 3, :], ps[:, n % 4, :], ACT.Relu, bias=b1[:, j, h:h + 1])\
                   .then_inc(sig("f_ownH"), 1)
                if j + 1 < TREES and n % 16 in SPLITS:
                    split_weights(j + 1, SPLITS.index(n % 16))
                if h == 2 and n > 2:
                    take_out(work[n - 3])
            take_out(work[-1])
            act.wait_ge(sig("f_wL"), 4 * TREES)
            for i in range(NT // 2):
                act.wait_ge(sig("f_val_ps"), i + 1)
                act.activation(val[:, 2 * i:2 * i + 2, :], two(ps[:, i, :]), ACT.Copy).then_inc(sig("f_val"), 1)
            for i in range(2):
                act.wait_ge(sig("f_s1"), i + 1)
                act.activation(s[:, i, :, :], s1[:, i, :, :], ACT.Exp).then_inc(sig("f_exp"), 1)
            for i in range(2):
                act.wait_ge(sig("f_probT_ps"), i + 1)
                act.activation(probT[:, 4 * i:4 * i + 4, :], ps[:, 6 + i, :], ACT.Copy).then_inc(sig("f_probT"), 1)

        @block.vector
        def _(dve):
            norm_vector(dve, sig, "f_ln", scratch, x, xn)
            turn_vector(dve, core, "f_xnT", xnT, 0)
            dve.wait_ge(sig("f_params_in"), 16)
            dve.wait_ge(sig("f_node_ps"), 1)
            flat = right[:, :, :, :].rearrange("p t j n -> p t (j n)")
            dve.tensor_tensor(flat, ps[:, 4, 0:NT * NN].rearrange("p (t n) -> p t n", t=NT),
                              core.p("ff_nodeb").unsqueeze(1).broadcast_to([P, NT, NN]), ALU.add)\
               .then_inc(sig("f_node"), 1)
            dve.wait_ge(sig("f_node"), 1)
            dve.tensor_scalar(flat, flat, 0.0, None, ALU.is_ge).then_inc(sig("f_right"), 1)
            dve.wait_ge(sig("f_right"), 1)
            for d in range(DEPTH):
                w = 2 ** d
                bit = right[:, :, :, w - 1:2 * w - 1]
                kids = levels[d][:, :, :, :].rearrange("p t j (n b) -> p t j n b", b=2)
                if d:
                    dve.tensor_tensor(kids[:, :, :, :, 1], levels[d - 1][:, :, :, :], bit, ALU.mult)\
                       .then_inc(sig("f_kid"), 1)
                    dve.wait_ge(sig("f_kid"), 2 * d + 1)
                    last = dve.tensor_tensor(kids[:, :, :, :, 0], levels[d - 1][:, :, :, :], kids[:, :, :, :, 1],
                                             ALU.subtract)
                else:
                    dve.tensor_copy(kids[:, :, :, :, 1], bit).then_inc(sig("f_kid"), 1)
                    last = dve.tensor_scalar(kids[:, :, :, :, 0], bit, -1.0, 1.0, ALU.mult, ALU.add)
                if d == DEPTH - 1:
                    last.then_inc(sig("f_leaf"), 1)
                else:
                    last.then_inc(sig("f_kid"), 1)
                    dve.wait_ge(sig("f_kid"), 2 * d + 2)
            for n in range(2 * TREES):
                dve.wait_ge(sig("f_leafT_ps"), n + 1)
                dve.tensor_copy(leafT[:, n // 2, (n % 2) * HALF:(n % 2 + 1) * HALF], ps[0:NLEAF, 5 + n % 2, :])\
                   .then_inc(sig("f_leafT"), 1)
            for n, (j, c, h) in enumerate(work):
                dve.wait_ge(sig("f_ownH"), n + 1)
                if n >= 2:
                    dve.wait_ge(sig("f_ownL"), n - 1)
                dve.tensor_scalar(own[:, n % 2, :], ps[:, n % 4, :], b1[:, j, h:h + 1], 0.0, ALU.add, ALU.max)\
                   .then_inc(sig("f_own"), 1)
                dve.wait_ge(sig("f_own"), n + 1)
                if n >= 3:
                    dve.wait_ge(sig("f_second_ps"), n - 2)
                dve.tensor_tensor(ownS[1][:, n % 3, :], own[:, n % 2, :], ownS[0][:, n % 3, :].bitcast(F32),
                                  ALU.subtract).then_inc(sig("f_ownL"), 1)
            dve.wait_ge(sig("f_wL"), 4 * TREES)
            mask = core.p("pair_mask").unsqueeze(1).broadcast_to([P, 4, P])
            for i in range(2):
                bank = ps[:, 4 + i, :].rearrange("p (t n) -> p t n", t=4)
                tiles = slice(4 * i, 4 * i + 4)
                dve.wait_ge(sig("f_s_ps"), i + 1)
                dve.scalar_tensor_tensor(s[:, i, :, :], bank, D ** -0.5, mask, ALU.mult, ALU.add)\
                   .then_inc(sig("f_s"), 1)
                dve.wait_ge(sig("f_s"), i + 1)
                dve.tensor_reduce(negmax[:, tiles], s[:, i, :, :], X, ALU.max, negate=True).then_inc(sig("f_negmax"), 1)
                dve.wait_ge(sig("f_negmax"), i + 1)
                dve.tensor_tensor(s1[:, i, :, :], s[:, i, :, :],
                                  negmax[:, tiles].unsqueeze(2).broadcast_to([P, 4, P]), ALU.add)\
                   .then_inc(sig("f_s1"), 1)
            for i in range(2):
                tiles = slice(4 * i, 4 * i + 4)
                dve.wait_ge(sig("f_exp"), i + 1)
                dve.tensor_reduce(total[:, tiles], s[:, i, :, :], X, ALU.add).then_inc(sig("f_total"), 1)
                dve.wait_ge(sig("f_total"), i + 1)
                dve.reciprocal(inv[:, tiles], total[:, tiles]).then_inc(sig("f_inv"), 1)
                dve.wait_ge(sig("f_inv"), i + 1)
                dve.tensor_tensor(prob[:, i, :, :], s[:, i, :, :],
                                  inv[:, tiles].unsqueeze(2).broadcast_to([P, 4, P]), ALU.mult)\
                   .then_inc(sig("f_prob"), 1)
            for i in range(NT // 2):
                dve.wait_ge(sig("f_out_ps"), i + 1)
                dve.tensor_tensor(x[:, 2 * i:2 * i + 2, :], x[:, 2 * i:2 * i + 2, :], two(ps[:, i, :]), ALU.add)\
                   .then_inc(sig("f_x"), 1)


def perceiver(nc, drams, out):
    with ExitStack() as ctx:
        core = Core(nc, ctx)
        x = core.tensor(ctx, "x", [P, NT, D])
        mean = core.tensor(ctx, "row_mean", [P, B * NC])
        rstd = core.tensor(ctx, "row_rstd", [P, B * NC])
        core.load_pack(ctx, "pk")
        with ExitStack() as early:
            cstats = core.tensor(early, "cstats", [P, B * NC, 6])
            core.load_pack(early, "pb0")
            core.phase(phase_topk_read, x, drams, cstats)
            core.phase(phase_retention, x, drams, cstats, mean, rstd)
        core.phase(phase_moe, x, drams)
        core.phase(phase_heads_read, x, drams, mean, rstd)
        core.phase(phase_features, x, drams)
        core.phase(phase_trees, x, drams)
        core.phase(store, x, out)


def store(core, x, out):
    sig = core.sig
    with ExitStack() as ctx:
        block = ctx.enter_context(core.nc.Block())

        @block.sync
        def _(sp):
            sp.dma_start(out, x[:, :, :]).then_inc(sig("x_out"), 16)
            sp.wait_ge(sig("x_out"), 16)


def halves(w):
    return w.reshape(KD, P, -1).transpose(1, 0, 2).reshape(P, -1)


def column(v):
    return v.reshape(-1, P).T


def rows(v):
    return np.broadcast_to(v.reshape(1, -1), (P, v.size))


def lay_out(a):
    p = np.arange(P)
    zeros = np.zeros((P, 1), np.float32)
    v = {"ident": np.eye(P, dtype=np.float32)}
    v["l0_wqT"] = halves(a["L0_xattn_Wq"].T)
    v["l0_wk"] = halves(a["L0_xattn_Wk"])
    v["l0_wvT"] = halves(a["L0_xattn_Wv"].T)
    v["l0_woT"] = halves(a["L0_xattn_Wo"].T)
    for n in ("bq", "bk", "bv"):
        v[f"l0_{n}"] = column(a[f"L0_xattn_{n}"])
    v["l0_bo"] = rows(a["L0_xattn_bo"])
    for n in "qkv":
        v[f"ret_w{n}"] = halves(a[f"L0_attn_weight_{n}"])
    v["ret_theta"] = column(a["L0_attn_theta"])
    j, i = p[:, None], p[None, :]
    same = (i // L) == (j // L)
    decay = np.float32(0.96875) ** (i - j).astype(np.float32)
    v["ret_decay"] = np.where(same & (i >= j), decay, 0).astype(np.float32)
    for k, n in enumerate("qkv"):
        v[f"mha_w{n}T"] = halves(a["L0_ffn_in_proj_w"][k * D:(k + 1) * D].T)
    v["mha_bq"] = column(a["L0_ffn_in_proj_b"][0:D])
    v["mha_bk"] = column(a["L0_ffn_in_proj_b"][D:2 * D])
    v["mha_bv"] = rows(a["L0_ffn_in_proj_b"][2 * D:])
    v["mha_mask"] = np.tile(np.where(i % 8 == j % 8, 0, MASKED).astype(np.float32), (1, 2))
    v["mha_woT"] = halves(a["L0_ffn_out_proj_w"].T)
    v["mha_bo"] = rows(a["L0_ffn_out_proj_b"])
    for n in ("ln1_g", "ln1_b", "ln2_g", "ln2_b"):
        v[n] = rows(a[f"L0_ffn_{n}"])
    v["moe_wg"] = halves(a["L0_ffn_wg"])
    v["moe_prefer"] = rows(np.arange(E, 0, -1).astype(np.float32))
    v["moe_base"] = rows((np.arange(E) * CAP).astype(np.float32))
    v["moe_tri"] = (j <= i).astype(np.float32)
    v["moe_ones"] = np.ones((P, P), np.float32)
    v["moe_iota"] = rows(np.arange(E * CAP).astype(np.float32))
    v["moe_b1"] = a["L0_ffn_b1"].reshape(E, FC, P).transpose(2, 0, 1).reshape(P, -1)
    v["moe_b2"] = rows(a["L0_ffn_b2"])
    v["n_wcol"], v["n_bcol"] = column(a["L1_xattn_norm_w"]), column(a["L1_xattn_norm_b"])
    v["n1_wcol"], v["n1_bcol"] = column(a["L1_xattn_norm1_w"]), column(a["L1_xattn_norm1_b"])
    for n in "qkvo":
        v[f"l1_w{n}"] = halves(a[f"L1_xattn_W{n}"])
    for n in ("bq", "bk", "bv"):
        v[f"l1_{n}"] = column(a[f"L1_xattn_{n}"])
    v["l1_bo"] = rows(a["L1_xattn_bo"])
    own = (p[:, None] // HD1 == np.arange(8)[None, :]) | ((p[:, None] + 64) % P // HD1 == np.arange(8)[None, :])
    v["head_mask"] = np.where(own, HD1 ** -0.5, 0).astype(np.float32)
    v["parity"] = (p[:, None] // HD1 % 2 == np.arange(2)[None, :]).astype(np.float32)
    v["rf_gsT"] = halves(a["L1_attn_proj_matrix"].T)
    v["rf_iwT"] = halves(a["L1_attn_input_weights"].T)
    v["rf_ab"], v["rf_abcol"] = rows(a["L1_attn_xis"]), column(a["L1_attn_xis"])
    trees = "qkv"
    v["ff_nodes"] = halves(np.concatenate([a[f"L1_ffn_{n}_node_w"] for n in trees]).T)
    v["ff_nodeb"] = rows(np.concatenate([a[f"L1_ffn_{n}_node_b"] for n in trees]))
    v["ff_b1"] = np.concatenate([a[f"L1_ffn_{n}_b1"].reshape(8, P).T for n in trees], 1)
    b2 = np.zeros((P, TREES * D), np.float32)
    b2[0:NLEAF] = np.concatenate([a[f"L1_ffn_{n}_b2"] for n in trees], 1)
    v["ff_b2"] = b2
    leaf = np.zeros((P, 8 * P), np.float32)
    leaf[0:NLEAF] = np.where(np.arange(8 * P)[None, :] // 64 == np.arange(NLEAF)[:, None], 0, MASKED)
    v["ff_leaf"] = leaf
    v["pair_mask"] = np.where(same, 0, MASKED).astype(np.float32)
    packed = {}
    for pack, parts in PACKS.items():
        for name, n in parts:
            assert v[name].shape == (P, n), (name, v[name].shape)
        packed[pack] = np.ascontiguousarray(np.concatenate([v[name] for name, _ in parts], 1))
    ctx = a["ctx_1024"]
    packed["ctx_rows"] = ctx[:, np.minimum(np.arange(NC * P), S - 1)]
    packed["ctxT"] = np.ascontiguousarray(ctx.transpose(0, 2, 1))
    packed["x"] = a["x"]
    packed["trees"] = np.stack([np.concatenate(
        [halves(a[f"L1_ffn_{n}_w1"].transpose(1, 0, 2).reshape(D, -1)),
         a[f"L1_ffn_{n}_w2"].reshape(8, P, D).transpose(1, 0, 2).reshape(P, -1)], 1) for n in trees])
    packed["moe_w1"] = a["L0_ffn_w1"]
    packed["moe_w2"] = a["L0_ffn_w2"]
    return packed


def kernel(**inputs):
    import concourse.bacc as _bacc
    from concourse.bass_utils import run_bass_kernel_spmd as _run

    nc = _bacc.Bacc("TRN2", target_bir_lowering=False, num_devices=1)
    arrays = lay_out({k: np.asarray(v) for k, v in inputs.items()})
    drams = {}
    for name, a in arrays.items():
        arrays[name] = np.ascontiguousarray(a)
        drams[name] = nc.dram_tensor(name + "_dram", a.shape, mybir.dt.from_np(a.dtype), kind="ExternalInput").ap()
    out = nc.dram_tensor("out_dram", (B, L, D), F32, kind="ExternalOutput").ap()
    drams["mixed"] = nc.dram_tensor("mixed_dram", (B, L, D), F32, kind="Internal").ap()
    perceiver(nc, drams, natural(out))
    r = _run(nc, [{k + "_dram": v for k, v in arrays.items()}], core_ids=[0])
    return r.results[0]["out_dram"]
```
